# Optimizing a Trainium2 kernel written in Bass

```python
import numpy as np
import jax
import jax.numpy as jnp

def _softmax(x, axis=-1):
    return jax.nn.softmax(x, axis=axis)

def _gelu(x):
    return jax.nn.gelu(x, approximate=True)

def _silu(x):
    return jax.nn.silu(x)

def _sigmoid(x):
    return jax.nn.sigmoid(x)

def _layernorm(x, axis=-1, eps=1e-05):
    m = jnp.mean(x, axis=axis, keepdims=True)
    v = jnp.var(x, axis=axis, keepdims=True)
    return (x - m) / jnp.sqrt(v + eps)

def _scatter_add(tgt, idx, src, axis=0):
    return tgt.at[idx].add(src)

def _segment_sum(src, seg, n):
    return jax.ops.segment_sum(src, seg, n)
kernel_name = 'mk_gnn_resnorm_d2_gnn_r32_5546b2'

def setup_inputs(seed: int=0):
    np.random.seed(seed)
    _w = jnp.asarray

    def _rec_inputs():
        import jax
        import jax.numpy as jnp
        _gk = jax.random.key(seed)
        x = -0.000202 + 1 * jax.random.normal(jax.random.fold_in(_gk, 1), (3125, 128), jnp.float32)
        _s = jax.random.randint(jax.random.fold_in(_gk, 2), (25000,), 0, 3125, jnp.int32)
        _d = jax.random.randint(jax.random.fold_in(_gk, 3), (25000,), 0, 3125, jnp.int32)
        _loop = jnp.arange(3125, dtype=jnp.int32)
        src = jnp.concatenate([_s, _d, _loop])
        dst = jnp.concatenate([_d, _s, _loop])
        _o = jnp.argsort(dst, stable=True)
        src = src[_o]
        dst = dst[_o]
        edge_type_8 = jax.random.randint(jax.random.fold_in(_gk, 12), (53125,), 0, 8, jnp.int32)
        return (x, src, dst, edge_type_8)
    x, src, dst, edge_type_8 = _rec_inputs()

    def _L0_gnn_setup():
        import jax, jax.numpy as jnp
        import numpy as np
        NUM_HEADS = 8
        NEG_SLOPE = 0.2

        def typed_linear(x, W, etype):
            out = jnp.zeros((x.shape[0], W.shape[2]), x.dtype)
            for t in range(W.shape[0]):
                out = out + jnp.where((etype == t)[:, None], x @ W[t], jnp.zeros((), x.dtype))
            return out
        key = jax.random.key(seed)
        ks = jax.random.split(key, 9)
        N, E, IN = (50000, 25000, 128)
        H, D = (NUM_HEADS, 16)
        HD = H * D
        T = 8
        s = 0.05
        return {'x': jax.random.normal(ks[0], (N, IN), jnp.float32), 'src': jax.random.randint(ks[1], (E,), 0, N), 'dst': jax.random.randint(ks[2], (E,), 0, N), 'etype': jax.random.randint(ks[3], (E,), 0, T), 'W_w': jax.random.normal(ks[4], (T, IN, HD), jnp.float32) * s, 'W_al': jax.random.normal(ks[5], (T, HD, HD), jnp.float32) * s, 'W_ar': jax.random.normal(ks[6], (T, HD, HD), jnp.float32) * s, 'W_res': jax.random.normal(ks[7], (IN, HD), jnp.float32) * s, 'b_res': jnp.zeros((HD,), jnp.float32)}
    _L0_gnn_all = _L0_gnn_setup()
    _L0_gnn_in = {k: v for k, v in _L0_gnn_all.items() if k in ('W_w', 'W_al', 'W_ar', 'W_res', 'b_res')}
    del _L0_gnn_all

    def _L1_gnn_setup():
        import jax, jax.numpy as jnp
        import numpy as np
        N_NODES = 3125
        N_EDGES = 18750
        D = 128
        EPS = 1e-05

        def _gcn_conv(x, src, dst, W, b, n_nodes):
            h = x @ W
            loops = jnp.arange(n_nodes, dtype=src.dtype)
            s = jnp.concatenate([src, loops])
            d = jnp.concatenate([dst, loops])
            deg = jax.ops.segment_sum(jnp.ones_like(d, dtype=h.dtype), d, num_segments=n_nodes)
            dis = jnp.where(deg > 0, jax.lax.rsqrt(deg), 0.0)
            norm = dis[s] * dis[d]
            msg = h[s] * norm[:, None]
            out = jax.ops.segment_sum(msg, d, num_segments=n_nodes)
            return out + b

        def _batch_norm(x, gamma, beta):
            mean = jnp.mean(x, axis=0)
            var = jnp.mean(jnp.square(x - mean), axis=0)
            return (x - mean) * jax.lax.rsqrt(var + EPS) * gamma + beta
        key = jax.random.key(seed)
        ks = jax.random.split(key, 16)
        glorot = lambda k, i, o: jax.random.normal(k, (i, o), jnp.float32) * np.sqrt(2.0 / (i + o))
        return {'x': jax.random.normal(ks[0], (N_NODES, D), jnp.float32), 'edge_src': jax.random.randint(ks[1], (N_EDGES,), 0, N_NODES, jnp.int32), 'edge_dst': jax.random.randint(ks[2], (N_EDGES,), 0, N_NODES, jnp.int32), 'W1': glorot(ks[3], D, D), 'b1': jnp.zeros((D,), jnp.float32), 'g1': jnp.ones((D,), jnp.float32), 'be1': jnp.zeros((D,), jnp.float32), 'W2': glorot(ks[4], D, D), 'b2': jnp.zeros((D,), jnp.float32), 'g2': jnp.ones((D,), jnp.float32), 'be2': jnp.zeros((D,), jnp.float32), 'W3': glorot(ks[5], D, D), 'b3': jnp.zeros((D,), jnp.float32)}
    _L1_gnn_all = _L1_gnn_setup()
    _L1_gnn_in = {k: v for k, v in _L1_gnn_all.items() if k in ('W1', 'b1', 'g1', 'be1', 'W2', 'b2', 'g2', 'be2', 'W3', 'b3')}
    del _L1_gnn_all
    return {'x': x, 'src': src, 'dst': dst, 'edge_type_8': edge_type_8, 'L0_gnn_W_w': _L0_gnn_in['W_w'], 'L0_gnn_W_al': _L0_gnn_in['W_al'], 'L0_gnn_W_ar': _L0_gnn_in['W_ar'], 'L0_gnn_W_res': _L0_gnn_in['W_res'], 'L0_gnn_b_res': _L0_gnn_in['b_res'], 'L1_gnn_W1': _L1_gnn_in['W1'], 'L1_gnn_b1': _L1_gnn_in['b1'], 'L1_gnn_g1': _L1_gnn_in['g1'], 'L1_gnn_be1': _L1_gnn_in['be1'], 'L1_gnn_W2': _L1_gnn_in['W2'], 'L1_gnn_b2': _L1_gnn_in['b2'], 'L1_gnn_g2': _L1_gnn_in['g2'], 'L1_gnn_be2': _L1_gnn_in['be2'], 'L1_gnn_W3': _L1_gnn_in['W3'], 'L1_gnn_b3': _L1_gnn_in['b3']}

def reference(x, src, dst, edge_type_8, L0_gnn_W_w, L0_gnn_W_al, L0_gnn_W_ar, L0_gnn_W_res, L0_gnn_b_res, L1_gnn_W1, L1_gnn_b1, L1_gnn_g1, L1_gnn_be1, L1_gnn_W2, L1_gnn_b2, L1_gnn_g2, L1_gnn_be2, L1_gnn_W3, L1_gnn_b3):
    import jax
    import jax.numpy as jnp

    def _L0_gnn_ref(x, src, dst, etype, W_w, W_al, W_ar, W_res, b_res):
        import jax, jax.numpy as jnp
        import numpy as np
        NUM_HEADS = 8
        NEG_SLOPE = 0.2

        def typed_linear(x, W, etype):
            out = jnp.zeros((x.shape[0], W.shape[2]), x.dtype)
            for t in range(W.shape[0]):
                out = out + jnp.where((etype == t)[:, None], x @ W[t], jnp.zeros((), x.dtype))
            return out
        N = x.shape[0]
        HD = W_w.shape[2]
        H = NUM_HEADS
        D = HD // H
        m = x[src]
        feat = typed_linear(m, W_w, etype)
        h = feat
        h_l = typed_linear(h, W_al, etype).reshape(-1, H, D).sum(-1)
        h_r = typed_linear(h, W_ar, etype).reshape(-1, H, D).sum(-1)
        att = jax.nn.leaky_relu(h_l + h_r, NEG_SLOPE)
        att_max = jax.ops.segment_max(att, dst, num_segments=N)
        att_exp = jnp.exp(att - att_max[dst])
        denom = jax.ops.segment_sum(att_exp, dst, num_segments=N)
        att = att_exp / denom[dst]
        alpha = jnp.einsum('ehd,eh->ed', h.reshape(-1, H, D), att)
        del alpha
        emb = jax.ops.segment_sum(h, dst, num_segments=N)
        out = emb + x @ W_res + b_res
        return jax.nn.elu(out)

    def _L1_gnn_ref(x, edge_src, edge_dst, W1, b1, g1, be1, W2, b2, g2, be2, W3, b3):
        import jax, jax.numpy as jnp
        import numpy as np
        N_NODES = 3125
        N_EDGES = 18750
        D = 128
        EPS = 1e-05

        def _gcn_conv(x, src, dst, W, b, n_nodes):
            h = x @ W
            loops = jnp.arange(n_nodes, dtype=src.dtype)
            s = jnp.concatenate([src, loops])
            d = jnp.concatenate([dst, loops])
            deg = jax.ops.segment_sum(jnp.ones_like(d, dtype=h.dtype), d, num_segments=n_nodes)
            dis = jnp.where(deg > 0, jax.lax.rsqrt(deg), 0.0)
            norm = dis[s] * dis[d]
            msg = h[s] * norm[:, None]
            out = jax.ops.segment_sum(msg, d, num_segments=n_nodes)
            return out + b

        def _batch_norm(x, gamma, beta):
            mean = jnp.mean(x, axis=0)
            var = jnp.mean(jnp.square(x - mean), axis=0)
            return (x - mean) * jax.lax.rsqrt(var + EPS) * gamma + beta
        n = x.shape[0]
        h = _gcn_conv(x, edge_src, edge_dst, W1, b1, n)
        h = jax.nn.relu(_batch_norm(h, g1, be1))
        h = _gcn_conv(h, edge_src, edge_dst, W2, b2, n)
        h = jax.nn.relu(_batch_norm(h, g2, be2))
        h = jax.nn.relu(_gcn_conv(h, edge_src, edge_dst, W3, b3, n))
        h = _gcn_conv(h, edge_src, edge_dst, W3, b3, n)
        return h
    x = _layernorm(x + _L0_gnn_ref(x, src, dst, edge_type_8, L0_gnn_W_w, L0_gnn_W_al, L0_gnn_W_ar, L0_gnn_W_res, L0_gnn_b_res), axis=-1)
    x = _layernorm(x + _L1_gnn_ref(x, src, dst, L1_gnn_W1, L1_gnn_b1, L1_gnn_g1, L1_gnn_be1, L1_gnn_W2, L1_gnn_b2, L1_gnn_g2, L1_gnn_be2, L1_gnn_W3, L1_gnn_b3), axis=-1)
    return x

_drawn_inputs = setup_inputs


def setup_inputs(seed=0):
    import zlib

    import numpy as np

    out = dict(_drawn_inputs(seed))
    spreads = {'L0_gnn_b_res': (0.0, 0.1),
     'L1_gnn_b1': (0.0, 2.0),
     'L1_gnn_g1': (1.0, 0.6),
     'L1_gnn_be1': (0.0, 2.0),
     'L1_gnn_b2': (0.0, 2.0),
     'L1_gnn_g2': (1.0, 0.2),
     'L1_gnn_be2': (0.0, 0.348),
     'L1_gnn_b3': (0.0, 0.1)}
    factors = {}
    for name, (base, spread) in spreads.items():
        noise = np.random.default_rng([zlib.crc32(name.encode()), seed]).standard_normal(out[name].shape)
        drawn = base * np.exp(spread * noise) if base else spread * noise
        out[name] = jnp.asarray(drawn.astype(out[name].dtype))
    for name, factor in factors.items():
        out[name] = (out[name] * factor).astype(out[name].dtype)
    return out
```

```python
import concourse.bass as bass
from concourse import mybir
from contextlib import ExitStack

F32 = mybir.dt.float32
F16 = mybir.dt.float16
I32 = mybir.dt.int32
ALU = mybir.AluOpType
ACT = mybir.ActivationFunctionType
AX = mybir.AxisListType

P = 128
N = 3125
F = 128
E = 53125
T = 8
EPS = 1e-5
NB = (N + P - 1) // P
LAST = N - (NB - 1) * P
NPAD = NB * P
SLOTS = T + 1
KT = (E + P - 1) // P
KG = KT + NB + 1
EB = 4
ER = KT // EB
ETAIL = E - (ER - 1) * EB * P
CH = 448
NCH = 7
DW = NCH * CH
NOWHERE = 4095
RING = 4
ROUNDS = (NB - 1) // RING


class Chain:

    def __init__(self, eng, sem):
        self.eng, self.sem, self.n, self.at = eng, sem, 0, 0

    def step(self, ins):
        self.n += 1
        ins.then_inc(self.sem, 1)
        self.eng.wait_ge(self.sem, self.at + self.n)

    def loop(self, count):
        return self.n


def build(nc, x, src, dst, etype, W_w, W_res, b_res, W1, b1, g1, be1, W2, b2, g2, be2, W3, b3, out):
    ctx = ExitStack()
    with ctx:
        def sb(name, shape, dt):
            return ctx.enter_context(nc.sbuf_tensor(name, shape, dt))

        def sem(name):
            return ctx.enter_context(nc.semaphore(name))

        table = nc.dram_tensor("node_table", (NPAD, SLOTS * F), F32, kind="Internal").ap()
        table_rows = table.rearrange("n (t f) -> (n t) f", f=F)
        y_dram = nc.dram_tensor("y_rows", (NPAD, F), F32, kind="Internal").ap()
        x1_dram = nc.dram_tensor("x1_rows", (NPAD, F), F32, kind="Internal").ap()

        ident = sb("ident", [P, P], F32)
        ones = sb("ones", [P, P], F32)
        eps = sb("eps", [P, 1], F32)
        Ww = sb("Ww", [P, T, F], F32)
        Wres = sb("Wres", [P, F], F32)
        bres = sb("bres", [1, F], F32)
        Wc = sb("Wc", [P, 3, F], F32)
        cols = sb("cols", [P, 7], F32)
        src_col = sb("src_col", [P, KG], I32)
        row_col = sb("row_col", [P, KT], I32)
        dst_col = sb("dst_col", [P, KG], F32)
        S = sb("S", [P, NPAD], F32)
        disB = sb("disB", [P, NPAD], F32)
        disC = sb("disC", [P, NB], F32)
        xs = sb("xs", [P, RING, F], F32)
        hb = sb("hb", [P, RING, F], F32)
        rs = sb("rs", [P, RING, F], F32)
        ob = sb("ob", [P, RING, F], F32)
        trow = sb("trow", [P, RING, SLOTS * F], F32)
        w1t = sb("w1t", [P, F], F32)
        w2t = sb("w2t", [P, F], F32)
        w3t = sb("w3t", [P, F], F32)
        w4t = sb("w4t", [P, F], F32)
        bst = sb("bst", [P, NCH, 6], F32)
        mv = sb("mv", [P, 2], F32)
        sd = sb("sd", [P, 2], F32)
        gs = sb("gs", [P, 2], F32)
        iota = sb("iota", [P, DW], F32)
        onehot = sb("onehot", [P, 2, DW], F32)
        gath = sb("gath", [P, 2, F], F32)
        islot = sb("islot", [P, 2], I32)
        e_int = sb("e_int", [ER, 3, EB * P], I32)
        e_f = sb("e_f", [ER, 3, EB * P], F32)

        acc = ctx.enter_context(nc.psum_tensor("acc", [P, NCH, 512], F32))
        pst = ctx.enter_context(nc.psum_tensor("pst", [P, 2, 256], F32))

        s_const = sem("s_const")
        s_w = sem("s_w")
        s_e = sem("s_e")
        s_ef = sem("s_ef")
        s_et = sem("s_et")
        s_idx = sem("s_idx")
        s_xfree = sem("s_xfree")
        s_xin = [sem(f"s_xin{b}") for b in range(RING)]
        s_xt = sem("s_xt")
        s_xTs = sem("s_xTs")
        s_mm1 = sem("s_mm1")
        s_ev_d = sem("s_ev_d")
        s_ev_a = sem("s_ev_a")
        s_tw = [sem(f"s_tw{b}") for b in range(RING)]
        s_isl = sem("s_isl")
        s_oh = sem("s_oh")
        s_ga = [sem(f"s_ga{b}") for b in range(2)]
        s_mm = sem("s_mm")
        s_drain = sem("s_drain")
        s_dis = sem("s_dis")
        s_hb = sem("s_hb")
        s_tr = sem("s_tr")
        s_blk = sem("s_blk")
        s_res = [sem(f"s_res{b}") for b in range(RING)]
        s_st = [sem(f"s_st{b}") for b in range(RING)]
        s_exp = sem("s_exp")
        s_var = sem("s_var")
        s_tr2 = sem("s_tr2")
        s_back = sem("s_back")
        s_vq = sem("s_vq")
        s_gsq = sem("s_gsq")
        s_bias = sem("s_bias")
        s_pass = sem("s_pass")
        s_blk2 = sem("s_blk2")
        block = ctx.enter_context(nc.Block())

        def blk(c):
            return bass.ds(c * P, P)

        def over_blocks(eng, body):
            with eng.Fori(0, ROUNDS) as i:
                for b in range(RING):
                    body(i * RING + b, i, b)
            body(NB - 1, ROUNDS, 0)

        stages = [("deg", KG)] + [("l0", KT)] + [(f"c{j}", KG) for j in range(4)]
        base_mm, base_t, a, t = [], [], 0, 0
        for name, k in stages:
            base_mm.append(a)
            base_t.append(t)
            a += 2 + k
            t += k
        base_g = [0] * len(stages)
        g = 0
        for q, (name, k) in enumerate(stages):
            base_g[q] = g
            g += 0 if name == "deg" else k

        def agg_pool(pool, q):
            name, k = stages[q]
            rows = table_rows if name == "l0" else y_dram
            with pool.Fori(0, k // 2) as i:
                for b in range(2):
                    pool.wait_ge(s_isl, base_g[q] + i * 2 + b + 1)
                    pool.wait_ge(s_mm, base_mm[q] + i * 2 + b + 1)
                    pool.sem_inc(s_pass, 1)
                    pool.indirect_dma_start(out=gath[:, b, :], out_offset=None, in_=rows[:, :],
                                            in_offset=bass.IndirectOffsetOnAxis(ap=islot[:, b:b + 1], axis=0)
                                            ).then_inc(s_ga[b], 16)

        def agg_dve(dve, q):
            name, k = stages[q]

            def tiles(i):
                for b in range(2):
                    if name != "deg":
                        if base_g[q] or not isinstance(i, int):
                            dve.wait_ge(s_ga[b], 16 * (base_g[q] // 2) + i * 16)
                        col = row_col if name == "l0" else src_col
                        nc.vector.tensor_copy(islot[:, b:b + 1], col[:, bass.ds(i * 2 + b, 1)]).then_inc(s_isl, 1)
                    dve.wait_ge(s_mm, base_mm[q] + i * 2 + b + 1)
                    nc.vector.tensor_scalar(onehot[:, b, :], iota[:], dst_col[:, bass.ds(i * 2 + b, 1)], None,
                                            ALU.is_equal).then_inc(s_oh, 1)

            tiles(0)
            with dve.Fori(1, k // 2) as i:
                tiles(i)

        def agg_pe(pe, q):
            name, k = stages[q]
            if q:
                pe.wait_ge(s_drain, NCH * q)
            for c in range(NCH):
                m = nc.tensor.matmul(acc[:, c, 0:CH], zero[:], iota[:, 0:CH], start=True, stop=False,
                                     skip_group_check=True)
                if c >= NCH - 2:
                    m.then_inc(s_mm, 1)
            with pe.Fori(0, k // 2) as i:
                for b in range(2):
                    if name != "deg":
                        pe.wait_ge(s_ga[b], 16 * (base_g[q] // 2) + i * 16 + 16)
                    pe.wait_ge(s_oh, base_t[q] + i * 2 + b + 1)
                    lhs = ones[:] if name == "deg" else gath[:, b, :]
                    for c in range(NCH):
                        m = nc.tensor.matmul(acc[:, c, 0:CH], lhs, onehot[:, b, c * CH:(c + 1) * CH],
                                             start=False, stop=False, skip_group_check=True)
                    m.then_inc(s_mm, 1)

        def agg_done(eng, q):
            eng.wait_ge(s_mm, base_mm[q] + 2 + stages[q][1])

        zero = sb("zero", [P, P], F32)

        @block.sync
        def _(sp):
            for b in range(RING):
                sp.sem_inc(s_tw[b], 16)
                sp.sem_inc(s_st[b], 16)
            sp.dma_start(Ww[:], W_w.rearrange("t k f -> k t f")).then_inc(s_w, 16)
            sp.dma_start(Wres[:], W_res).then_inc(s_w, 16)
            sp.dma_start(bres[:], b_res.rearrange("(a f) -> a f", a=1)).then_inc(s_w, 16)
            for j, w in enumerate((W1, W2, W3)):
                sp.dma_start(Wc[:, j, :], w).then_inc(s_w, 16)
            for j, v in enumerate((b1, g1, be1, b2, g2, be2, b3)):
                sp.dma_start(cols[:, j:j + 1], v.rearrange("(f a) -> f a", a=1)).then_inc(s_w, 16)
            sp.wait_ge(s_const, 1)
            for j, v in enumerate((src, dst, etype)):
                full = (ER - 1) * EB * P
                sp.dma_start(e_int[0:ER - 1, j, :], v[0:full].rearrange("(p e) -> p e", e=EB * P)).then_inc(s_e, 16)
                sp.dma_start(e_int[ER - 1:ER, j, 0:ETAIL], v[full:E].rearrange("(a e) -> a e", a=1)).then_inc(s_e, 16)

            def store(c, i, b):
                sp.wait_ge(s_ev_d, c + 2)
                sp.wait_ge(s_ev_a, c + 2)
                sp.dma_start(table[blk(c), :], trow[:, b, :]).then_inc(s_tw[b], 16)
            over_blocks(sp, store)

            def l0_out(c, i, b):
                sp.wait_ge(s_blk, c + 1)
                sp.dma_start(x1_dram[blk(c), :], ob[:, b, :]).then_inc(s_st[b], 16)
            over_blocks(sp, l0_out)

            for j in range(4):
                def y_out(c, i, b):
                    sp.wait_ge(s_blk, NB * (j + 1) + c + 1)
                    sp.dma_start(y_dram[blk(c), :], ob[:, b, :]).then_inc(s_st[b], 16)
                over_blocks(sp, y_out)

            def fin_out(c, i, b):
                sp.wait_ge(s_blk, NB * 5 + c + 1)
                rows = LAST if isinstance(c, int) else P
                sp.dma_start(out[bass.ds(c * P, rows), :], ob[0:rows, b, :]).then_inc(s_st[b], 16)
            over_blocks(sp, fin_out)
            for b in range(RING):
                sp.wait_ge(s_st[b], 16 * 6 * (ROUNDS + (b == 0)) + 16)

        def load_rows(pool, first, which):
            pool.wait_ge(s_xfree, RING + first)

            def body(c, i, b):
                pool.wait_ge(s_xfree, first + c + 1)
                rows = LAST if isinstance(c, int) else P
                if which == "x":
                    pool.dma_start(xs[0:rows, b, :], x[bass.ds(c * P, rows), :]).then_inc(s_xin[b], 16)
                elif which == "l0":
                    pool.dma_start(xs[0:rows, b, :], x[bass.ds(c * P, rows), :]).then_inc(s_res[b], 16)
                    pool.dma_start(rs[:, b, :], table[blk(c), T * F:SLOTS * F]).then_inc(s_res[b], 16)
                else:
                    pool.dma_start(xs[:, b, :], x1_dram[blk(c), :]).then_inc(s_res[b], 16)
            over_blocks(pool, body)

        @block.gpsimd
        def _(pool):
            nc.gpsimd.memset(e_int[:, 0, :], 0)
            nc.gpsimd.memset(e_int[:, 1, :], NOWHERE)
            nc.gpsimd.memset(e_int[:, 2, :], 0).then_inc(s_const, 1)
            nc.gpsimd.memset(ident[:], 0.0).then_inc(s_const, 1)
            nc.gpsimd.memset(ones[:], 1.0)
            nc.gpsimd.memset(eps[:], EPS)
            nc.gpsimd.memset(zero[:], 0.0)
            nc.gpsimd.memset(disB[:], 1.0)
            nc.gpsimd.memset(S[:], 0.0)
            nc.gpsimd.iota(src_col[:, KT:KT + NB], pattern=[[P, NB]], base=0, channel_multiplier=1)
            nc.gpsimd.iota(dst_col[:, KT:KT + NB], pattern=[[P, NB]], base=0, channel_multiplier=1,
                           allow_small_or_imprecise_dtypes=True)
            nc.gpsimd.memset(src_col[:, KG - 1:KG], 0)
            nc.gpsimd.memset(dst_col[:, KG - 1:KG], float(NOWHERE))
            nc.gpsimd.iota(iota[:], pattern=[[1, DW]], base=0, channel_multiplier=0,
                           allow_small_or_imprecise_dtypes=True).then_inc(s_const, 1)
            pool.wait_ge(s_const, 3)
            nc.gpsimd.affine_select(out=ident[:], in_=ident[:], compare_op=ALU.not_equal, fill=1.0, base=0,
                                    pattern=[[-1, P]], channel_multiplier=1).then_inc(s_const, 1)
            load_rows(pool, 0, "x")
            for b in range(RING):
                pool.wait_ge(s_tw[b], 16 * (ROUNDS + (b == 0)) + 16)
            agg_pool(pool, 1)
            load_rows(pool, NB, "l0")
            for j in range(4):
                for b in range(RING):
                    pool.wait_ge(s_st[b], 16 * (j + 2) * (ROUNDS + (b == 0)) + 16)
                agg_pool(pool, 2 + j)
            load_rows(pool, 2 * NB, "x1")

        def evac(i):
            return acc[:, i, 0:CH]

        @block.scalar
        def _(act):
            act.sem_inc(s_ev_a, 1)
            act.wait_ge(s_w, 16 * 13)
            def table_block(c, i, b):
                act.wait_ge(s_xt, c + 1)
                act.sem_inc(s_xfree, 1)
                nc.scalar.copy(hb[:, b, :], pst[:, b % 2, 0:P]).then_inc(s_xTs, 1)
                act.wait_ge(s_mm1, c + 1)
                act.wait_ge(s_tw[b], 16 * i + 16)
                nc.scalar.copy(trow[:, b, 512:1024], acc[:, 1, 0:512]).then_inc(s_ev_a, 1)
            over_blocks(act, table_block)

            agg_done(act, 0)
            for c in range(NCH):
                nc.scalar.activation(disB[:, c * CH:(c + 1) * CH], evac(c), ACT.Sqrt).then_inc(s_drain, 1)

            def hb_count(stage):
                return NB * stage

            def copy_block(stage, func, bias=None, scale=None):
                def body(c, i, b):
                    act.wait_ge(s_tr, hb_count(stage) + c + 1)
                    act.sem_inc(s_pass, 1)
                    kw = {}
                    if bias is not None:
                        kw = dict(bias=bias, scale=scale)
                    nc.scalar.activation(hb[:, b, :], S[:, blk(c)], func, **kw).then_inc(s_hb, 1)
                return body

            def dis_block(c, i, b):
                act.wait_ge(s_tr, c + 1)
                act.sem_inc(s_pass, 1)
                nc.scalar.copy(hb[:, b, :], disB[:, blk(c)]).then_inc(s_hb, 1)
            act.wait_ge(s_dis, 1)
            act.wait_ge(s_tr, RING)
            over_blocks(act, dis_block)

            agg_done(act, 1)
            for c in range(NCH):
                nc.scalar.copy(S[:, c * CH:(c + 1) * CH], evac(c)).then_inc(s_drain, 1)
            act.wait_ge(s_drain, 2 * NCH)
            first = copy_block(1, ACT.Copy)

            def l0_block(c, i, b):
                first(c, i, b)
                act.wait_ge(s_exp, c * 2 + 1)
                nc.scalar.activation(w2t[:], w1t[:], ACT.Exp).then_inc(s_exp, 1)
                act.wait_ge(s_var, c * 2 + 1)
                nc.scalar.activation(sd[:, 0:1], mv[:, 1:2], ACT.Sqrt, bias=eps[:], scale=1.0).then_inc(s_var, 1)
                act.wait_ge(s_tr2, c + 1)
                act.sem_inc(s_pass, 1)
                nc.scalar.copy(S[:, blk(c)], pst[:, b % 2, P:2 * P]).then_inc(s_back, 1)
            act.wait_ge(s_tr, RING + NB)
            over_blocks(act, l0_block)
            act.wait_ge(s_back, NB)

            nvar = 2 * NB
            for j in range(4):
                if j == 0:
                    body = copy_block(2 + j, ACT.Copy)
                elif j < 3:
                    act.wait_ge(s_gsq, j)
                    body = copy_block(2 + j, ACT.Relu, gs[:, 1:2], gs[:, 0:1])
                else:
                    body = copy_block(2 + j, ACT.Relu, cols[:, 6:7], 1.0)
                act.wait_ge(s_tr, RING + NB * (2 + j))
                over_blocks(act, body)
                if j < 2:
                    for c in range(NCH):
                        act.wait_ge(s_drain, NCH * (3 + j) - NCH + c + 1)
                        nc.scalar.activation(S[:, c * CH:(c + 1) * CH], S[:, c * CH:(c + 1) * CH], ACT.Identity,
                                             bias=cols[:, 3 * j:3 * j + 1], scale=1.0).then_inc(s_bias, 1)
                    act.wait_ge(s_var, nvar + 1)
                    nc.scalar.activation(sd[:, 0:1], mv[:, 1:2], ACT.Sqrt, bias=eps[:], scale=1.0).then_inc(s_var, 1)
                    nvar += 2
                else:
                    act.wait_ge(s_drain, NCH * (3 + j))
            first = copy_block(6, ACT.Identity, cols[:, 6:7], 1.0)

            def fin_block(c, i, b):
                first(c, i, b)
                act.wait_ge(s_var, nvar + c * 2 + 1)
                nc.scalar.activation(sd[:, 0:1], mv[:, 1:2], ACT.Sqrt, bias=eps[:], scale=1.0).then_inc(s_var, 1)
            act.wait_ge(s_tr, RING + NB * 6)
            over_blocks(act, fin_block)

        @block.vector
        def _(dve):
            vq = Chain(dve, s_vq)
            dve.sem_inc(s_xfree, RING)
            dve.sem_inc(s_ev_d, 1)
            dve.sem_inc(s_blk2, 1)
            dve.wait_ge(s_e, 16 * 6)
            nc.vector.tensor_copy(e_f[:, 0, :], e_int[:, 0, :])
            nc.vector.tensor_copy(e_f[:, 1, :], e_int[:, 1, :])
            nc.vector.scalar_tensor_tensor(e_f[:, 2, :], e_int[:, 0, :], float(SLOTS), e_int[:, 2, :],
                                           ALU.mult, ALU.add).then_inc(s_ef, 1)
            dve.wait_ge(s_et, 1)
            for j, col in enumerate((src_col, dst_col, row_col)):
                v = nc.vector.tensor_copy(col[:, 0:KT].rearrange("q (p b) -> q b p", b=EB),
                                          acc[:, j, 0:KT].rearrange("q (b p) -> q b p", b=EB))
            v.then_inc(s_idx, 1)

            def table_block(c, i, b):
                dve.wait_ge(s_mm1, c + 1)
                dve.wait_ge(s_tw[b], 16 * i + 16)
                nc.vector.tensor_copy(trow[:, b, 0:512], acc[:, 0, 0:512])
                nc.vector.tensor_copy(trow[:, b, 1024:1152], acc[:, 2, 0:128]).then_inc(s_ev_d, 1)
            over_blocks(dve, table_block)

            dve.wait_ge(s_const, 4)
            agg_dve(dve, 0)
            dve.wait_ge(s_drain, NCH)
            nc.vector.reciprocal(disB[:], disB[:]).then_inc(s_dis, 1)

            def dis_block(c, i, b):
                dve.wait_ge(s_tr, RING + c + 1)
                nc.vector.tensor_copy(disC[:, bass.ds(c, 1)], pst[:, b % 2, 0:1]).then_inc(s_blk2, 1)
            over_blocks(dve, dis_block)

            agg_dve(dve, 1)

            def norm(c, b, nv):
                vq.step(nc.vector.bn_stats(bst[:, 0, :], w3t[:]))
                dve.sem_inc(s_pass, 1)
                nc.vector.bn_aggr(mv[:], bst[:, 0, :]).then_inc(s_var, 1)
                dve.wait_ge(s_var, nv + c * 2 + 2)
                vq.step(nc.vector.reciprocal(sd[:, 1:2], sd[:, 0:1]))

            def l0_block(c, i, b):
                vq.at = i * RING * 5 if not isinstance(i, int) else 0
                dve.wait_ge(s_tr, RING + NB + c + 1)
                dve.wait_ge(s_res[b], 32 * i + 32)
                vq.step(nc.vector.tensor_tensor(w4t[:], pst[:, b % 2, 0:P], rs[:, b, :], ALU.add))
                nc.vector.tensor_scalar(w1t[:], w4t[:], 0.0, None, ALU.min).then_inc(s_exp, 1)
                vq.step(nc.vector.scalar_tensor_tensor(w3t[:], w4t[:], 0.0, xs[:, b, :], ALU.max, ALU.add))
                dve.sem_inc(s_xfree, 1)
                dve.wait_ge(s_exp, c * 2 + 2)
                vq.step(nc.vector.scalar_tensor_tensor(w3t[:], w2t[:], -1.0, w3t[:], ALU.add, ALU.add))
                norm(c, b, 0)
                dve.wait_ge(s_st[b], 16 * i + 16)
                nc.vector.tensor_scalar(ob[:, b, :], w3t[:], mv[:, 0:1], sd[:, 1:2], ALU.subtract,
                                        ALU.mult).then_inc(s_blk, 1)
                dve.wait_ge(s_blk, c + 1)

            def chained_blocks(body):
                n0 = vq.n
                with dve.Fori(0, ROUNDS) as i:
                    per = None
                    for b in range(RING):
                        if b == 0:
                            s0 = vq.n
                        body(i * RING + b, i, b)
                    per = vq.n - s0
                assert per == RING * 5, per
                vq.n = n0 + ROUNDS * per
                vq.at = 0
                body(NB - 1, ROUNDS, 0)
            chained_blocks(l0_block)

            nvar = 2 * NB
            for j in range(4):
                def y_block(c, i, b):
                    dve.wait_ge(s_tr, RING + NB * (2 + j) + c + 1)
                    dve.wait_ge(s_st[b], 16 * ((j + 1) * (ROUNDS + (b == 0)) + i) + 16)
                    nc.vector.tensor_scalar(ob[:, b, :], pst[:, b % 2, 0:P], disC[:, bass.ds(c, 1)], None,
                                            ALU.mult).then_inc(s_blk, 1)
                over_blocks(dve, y_block)
                agg_dve(dve, 2 + j)
                agg_done(dve, 2 + j)
                for c in range(NCH):
                    nc.vector.tensor_tensor(S[:, c * CH:(c + 1) * CH], evac(c), disB[:, c * CH:(c + 1) * CH],
                                            ALU.mult).then_inc(s_drain, 1)
                if j < 2:
                    for c in range(NCH):
                        dve.wait_ge(s_bias, NCH * j + c + 1)
                        w = min(N, (c + 1) * CH) - c * CH
                        v = nc.vector.bn_stats(bst[:, c, :], S[:, c * CH:c * CH + w])
                    vq.step(v)
                    nc.vector.bn_aggr(mv[:], bst[:, :, :].rearrange("p c s -> p (c s)")).then_inc(s_var, 1)
                    dve.wait_ge(s_var, nvar + 2)
                    nvar += 2
                    vq.step(nc.vector.reciprocal(sd[:, 1:2], sd[:, 0:1]))
                    vq.step(nc.vector.tensor_tensor(gs[:, 0:1], sd[:, 1:2], cols[:, 3 * j + 1:3 * j + 2], ALU.mult))
                    vq.step(nc.vector.tensor_tensor(sd[:, 1:2], mv[:, 0:1], gs[:, 0:1], ALU.mult))
                    nc.vector.tensor_tensor(gs[:, 1:2], cols[:, 3 * j + 2:3 * j + 3], sd[:, 1:2],
                                            ALU.subtract).then_inc(s_gsq, 1)

            def fin_block(c, i, b):
                vq.at = i * RING * 3 if not isinstance(i, int) else 0
                dve.wait_ge(s_tr, RING + NB * 6 + c + 1)
                dve.wait_ge(s_res[b], 32 * (ROUNDS + (b == 0)) + 16 * i + 16)
                vq.step(nc.vector.tensor_tensor(w3t[:], pst[:, b % 2, 0:P], xs[:, b, :], ALU.add))
                dve.sem_inc(s_xfree, 1)
                norm(c, b, nvar)
                dve.wait_ge(s_st[b], 16 * (5 * (ROUNDS + (b == 0)) + i) + 16)
                nc.vector.tensor_scalar(ob[:, b, :], w3t[:], mv[:, 0:1], sd[:, 1:2], ALU.subtract,
                                        ALU.mult).then_inc(s_blk, 1)
                dve.wait_ge(s_blk, NB * 5 + c + 1)

            n0 = vq.n
            with dve.Fori(0, ROUNDS) as i:
                for b in range(RING):
                    fin_block(i * RING + b, i, b)
            vq.n = n0 + ROUNDS * (vq.n - n0)
            vq.at = 0
            fin_block(NB - 1, ROUNDS, 0)

        @block.tensor
        def _(pe):
            pe.wait_ge(s_const, 4)
            pe.wait_ge(s_ef, 1)
            for j in range(3):
                for b in range(EB):
                    m = nc.tensor.transpose(acc[:, j, b * ER:(b + 1) * ER], e_f[:, j, b * P:(b + 1) * P],
                                            ident[0:ER, 0:ER])
            m.then_inc(s_et, 1)
            pe.wait_ge(s_idx, 1)
            pe.wait_ge(s_w, 16 * 13)

            def table_block(c, i, b):
                pe.wait_ge(s_xin[b], 16 * i + 16)
                pe.wait_ge(s_ev_a, c + 1)
                nc.tensor.transpose(pst[:, b % 2, 0:P], xs[:, b, :], ident[:]).then_inc(s_xt, 1)
                pe.wait_ge(s_xTs, c + 1)
                pe.wait_ge(s_ev_d, c + 1)
                for h in range(2):
                    nc.tensor.matmul(acc[:, h, 0:512], hb[:, b, :], Ww[:, 4 * h:4 * h + 4, :], start=True, stop=True)
                nc.tensor.matmul(acc[:, 2, 0:F], hb[:, b, :], Wres[:], start=True, stop=False)
                nc.tensor.matmul(acc[:, 2, 0:F], ones[0:1, :], bres[:], start=False, stop=True).then_inc(s_mm1, 1)
            over_blocks(pe, table_block)

            pe.wait_ge(s_ev_a, NB + 1)
            pe.wait_ge(s_ev_d, NB + 1)
            agg_pe(pe, 0)
            pe.sem_inc(s_tr, RING)

            def dis_block(c, i, b):
                pe.wait_ge(s_hb, c + 1)
                pe.wait_ge(s_blk2, c + 1)
                nc.tensor.transpose(pst[:, b % 2, 0:P], hb[:, b, :], ident[:]).then_inc(s_tr, 1)
            over_blocks(pe, dis_block)

            pe.wait_ge(s_blk2, NB + 1)
            agg_pe(pe, 1)

            def l0_block(c, i, b):
                pe.wait_ge(s_hb, NB + c + 1)
                nc.tensor.transpose(pst[:, b % 2, 0:P], hb[:, b, :], ident[:]).then_inc(s_tr, 1)
                pe.wait_ge(s_blk, c + 1)
                nc.tensor.transpose(pst[:, b % 2, P:2 * P], ob[:, b, :], ident[:]).then_inc(s_tr2, 1)
            over_blocks(pe, l0_block)
            pe.wait_ge(s_back, NB)

            for j in range(4):
                def y_block(c, i, b):
                    pe.wait_ge(s_hb, NB * (2 + j) + c + 1)
                    pe.wait_ge(s_blk, NB * (j + 1) + c)
                    nc.tensor.matmul(pst[:, b % 2, 0:P], hb[:, b, :], Wc[:, min(j, 2), :], start=True,
                                     stop=True).then_inc(s_tr, 1)
                over_blocks(pe, y_block)
                agg_pe(pe, 2 + j)

            def fin_block(c, i, b):
                pe.wait_ge(s_hb, NB * 6 + c + 1)
                pe.wait_ge(s_blk, NB * 5 + c)
                nc.tensor.transpose(pst[:, b % 2, 0:P], hb[:, b, :], ident[:]).then_inc(s_tr, 1)
            over_blocks(pe, fin_block)


_INS = ["x", "src", "dst", "edge_type_8", "L0_gnn_W_w", "L0_gnn_W_res", "L0_gnn_b_res",
        "L1_gnn_W1", "L1_gnn_b1", "L1_gnn_g1", "L1_gnn_be1", "L1_gnn_W2", "L1_gnn_b2", "L1_gnn_g2", "L1_gnn_be2",
        "L1_gnn_W3", "L1_gnn_b3"]


def kernel(**inputs):
    import numpy as _np
    import concourse.bacc as _bacc
    from concourse import mybir as _mybir
    from concourse.bass_utils import run_bass_kernel_spmd as _run

    nc = _bacc.Bacc("TRN2", target_bir_lowering=False, num_devices=1)
    arrays, args = {}, []
    for name in _INS:
        a = _np.ascontiguousarray(inputs[name])
        arrays[f"in_{name}_dram"] = a
        args.append(nc.dram_tensor(f"in_{name}_dram", a.shape, _mybir.dt.from_np(a.dtype), kind="ExternalInput").ap())
    args.append(nc.dram_tensor("out_0_dram", (N, F), _mybir.dt.float32, kind="ExternalOutput").ap())
    build(nc, *args)
    r = _run(nc, [arrays], core_ids=[0])
    return r.results[0]["out_0_dram"]
```

```python
import concourse.bass as bass
from concourse import mybir
from contextlib import ExitStack, contextmanager
import numpy as np

F32 = mybir.dt.float32
F16 = mybir.dt.float16
I32 = mybir.dt.int32
ALU = mybir.AluOpType
ACT = mybir.ActivationFunctionType
AX = mybir.AxisListType

P = 128
N = 3125
F = 128
E = 53125
T = 8
EPS = 1e-5
NB = (N + P - 1) // P
LAST = N - (NB - 1) * P
NPAD = NB * P
SLOTS = T + 1
KT = (E + P - 1) // P
KG = KT + NB + 1
EB = 4
ER = KT // EB
EW = EB * P
ETAIL = E - (ER - 1) * EW
CH = 448
NCH = 7
DW = NCH * CH
NOWHERE = 4095
RING = 4
ROUNDS = (NB - 1) // RING

TB = E // N
MARGIN = 5
GW = 16
GB = P // GW
NG = DW // GW
GH = NG // 2
GR = 32
GROWS = 12
GE = GR * GROWS
GT = GE // P
KW = NB * GW
CROWS = (KT * P + GE) // GR
NTHR = 9
BATCH = [(0, 5), (5, 9), (9, 13), (13, 17)]
OHS = 6
AHS = 4
JR = 6
JP = 3
S1 = 17


def constants():
    c = np.zeros((P, 8 + NTHR + 3 * EB + (NTHR + 1) * (NG + 1)), np.float32)
    p = np.arange(ER)
    gb = (p * EW * N) // (E * GW) - 3
    c[:ER, 0] = EW
    c[ER - 1, 0] = ETAIL
    c[:LAST, 3] = 1
    for h in range(2):
        c[:GH, 1 + h] = GW * (GH * h + np.arange(GH))
    for m in range(NTHR):
        c[:ER, 8 + m] = GW * (gb + m)
    for b in range(EB):
        k = EB * p + b
        j, i = k // TB, k % TB
        low = i < MARGIN
        base = P * (j - low)
        width = np.where(low | (i >= TB - MARGIN), 2 * P, P)
        c[:ER, 8 + NTHR + b] = base
        c[:ER, 8 + NTHR + EB + b] = np.where(j == NB - 1, NOWHERE, base + width - 1)
    at = 8 + NTHR + 3 * EB
    g = np.arange(NG + 1)
    for m in range(NTHR):
        c[:ER, at + m * (NG + 1):at + (m + 1) * (NG + 1)] = g[None] == (gb + m)[:, None]
    c[:ER, at + NTHR * (NG + 1):] = g[None] >= (gb + NTHR)[:, None]
    return c


class Chain:

    def __init__(self, eng, sem):
        self.eng, self.sem, self.n, self.at = eng, sem, 0, 0

    def step(self, ins):
        self.n += 1
        ins.then_inc(self.sem, 1)
        self.eng.wait_ge(self.sem, self.at + self.n)

    @contextmanager
    def rounds(self, first, last, per):
        n0 = self.n
        with self.eng.Fori(first, last) as i:
            self.at = (i - first) * per if first else i * per
            yield i
        assert self.n - n0 == per, (self.n - n0, per)
        self.n = n0 + (last - first) * per
        self.at = 0


def build(nc, x, src, dst, etype, W_w, W_res, b_res, W1, b1, g1, be1, W2, b2, g2, be2, W3, b3, const, out):
    ctx = ExitStack()
    with ctx:
        def sb(name, shape, dt):
            return ctx.enter_context(nc.sbuf_tensor(name, shape, dt))

        def sem(name):
            return ctx.enter_context(nc.semaphore(name))

        table = nc.dram_tensor("node_table", (NPAD, SLOTS * F), F32, kind="Internal").ap()
        table_rows = table.rearrange("n (t f) -> (n t) f", f=F)
        y_dram = nc.dram_tensor("y_rows", (NPAD, F), F32, kind="Internal").ap()
        x1_dram = nc.dram_tensor("x1_rows", (NPAD, F), F32, kind="Internal").ap()
        packed = nc.dram_tensor("packed_edges", (CROWS, GR), I32, kind="Internal").ap()

        ident = sb("ident", [P, P], F32)
        ident16 = sb("ident16", [P, P], F16)
        ones = sb("ones", [P, P], F32)
        eps = sb("eps", [P, 1], F32)
        iota16 = sb("iota16", [P, KW], F16)
        Wc = sb("Wc", [P, 3, F], F32)
        cols = sb("cols", [P, 7], F32)
        scl = sb("scl", [P, 16], F32)
        row_col = sb("row_col", [P, TB * NB], I32)
        rel_col = sb("rel_col", [P, KT], F32)
        lo_col = sb("lo_col", [P, GT, NG], F16)
        key_col = sb("key_col", [P, GT, NG], F16)
        disC = sb("disC", [P, NB], F32)
        dcc = sb("dcc", [P, NB], F32)
        small = sb("small", [P, 24], F32)
        vall = sb("vall", [P, 8], F32)
        flag = sb("flag", [P, 1], I32)
        valid = sb("valid", [P, 1], F32)
        bst = sb("bst", [P, 8, 6], F32)
        mv = sb("mv", [P, 4, 2], F32)
        sd = sb("sd", [P, 8], F32)
        gs = sb("gs", [P, 2], F32)
        mx = sb("mx", [P, 8], F32)
        Yhl = sb("Yhl", [P, NB, 2 * P], F16)
        U = sb("U", [P, 8 * F], F32)

        def u(a, n=1):
            return U[:, a * F:(a + n) * F]
        w1t, w2t, w3t, w4t, xs1, rs1, ob1, hb1 = (u(a) for a in range(8))
        ring6 = U[:, 0:JR * F].rearrange("p (a f) -> p a f", f=F)

        R = sb("R", [P, 6400], F32)
        S = R[:, 0:NPAD]
        disB = R[:, NPAD:2 * NPAD]
        land = R[:, 0:TB * F].rearrange("p (t f) -> p t f", f=F)
        at = TB * F
        ghl = R[:, at:at + TB * 130].bitcast(F16).rearrange("p (t w) -> p t w", w=260)
        at += TB * 130
        oh = R[:, at:at + OHS * P].bitcast(F16).rearrange("p (t w) -> p t w", w=2 * P)
        at += OHS * P
        aoh = R[:, at:at + AHS * (P + KW) // 2].bitcast(F16).rearrange("p (t w) -> p t w", w=P + KW)
        assert at + AHS * (P + KW) // 2 <= 6400

        A = sb("A", [P, NB, DW], F16)
        Aflat = A[:, :, :].rearrange("p s d -> p (s d)")
        taken = [0]

        def early(n, dt=F32, parts=P):
            a = taken[0]
            taken[0] += n
            assert taken[0] * 2 <= NB * DW
            return Aflat[0:parts, 2 * a:2 * (a + n)].bitcast(dt)

        Ww = early(T * F)
        Wres = early(F)
        bres = early(F)
        Wmax = early(F)
        wtmp = early(F)
        cst = early(8 + NTHR + 3 * EB + (NTHR + 1) * (NG + 1))
        x_all = early(NB * F).rearrange("p (c f) -> p c f", f=F)
        e_int = early(3 * EW, I32).rearrange("p (a e) -> p a e", a=3)
        e_f = early(4 * EW).rearrange("p (a e) -> p a e", a=4)
        e_tmp = early(EW)
        e_pack = early(EW, I32)
        d_next = early(1)
        n_next = early(2, I32)
        cnt = early(NTHR)
        g_idx = early(2 * GROWS, I32).rearrange("p (h m) -> p h m", h=2)
        g_e = early(2 * GE, I32)
        g_t = early(2 * GE, I32)
        g_a = early(2 * GE)
        g_b = early(2 * GE)
        g_c = early(2 * GE)
        off_i = early(6, I32)
        src_col = early(KG, I32)
        dst_col = early(KG)
        xs = early(RING * F).rearrange("p (a f) -> p a f", f=F)
        hb = early(RING * F).rearrange("p (a f) -> p a f", f=F)
        trow = early(RING * SLOTS * F).rearrange("p (a f) -> p a f", a=RING)
        rs = early(RING * F).rearrange("p (a f) -> p a f", f=F)
        ob = early(RING * F).rearrange("p (a f) -> p a f", f=F)
        iota = early(DW)
        onehot = early(2 * DW).rearrange("p (a d) -> p a d", a=2)
        gath = early(2 * F).rearrange("p (a f) -> p a f", a=2)
        islot = early(2, I32)

        acc = ctx.enter_context(nc.psum_tensor("acc", [P, NCH, 512], F32))
        pst = ctx.enter_context(nc.psum_tensor("pst", [P, 4, P], F32))

        s_const = sem("s_const")
        s_w = sem("s_w")
        s_e = sem("s_e")
        s_xall = sem("s_xall")
        s_ef = sem("s_ef")
        s_et = sem("s_et")
        s_idx = sem("s_idx")
        s_pack = sem("s_pack")
        s_packed = sem("s_packed")
        s_cnt = sem("s_cnt")
        s_off = sem("s_off")
        s_gidx = sem("s_gidx")
        s_gf = sem("s_gf")
        s_gk = sem("s_gk")
        s_gt = sem("s_gt")
        s_gc = sem("s_gc")
        s_viol = sem("s_viol")
        s_vsum = sem("s_vsum")
        s_flag = sem("s_flag")
        s_bnd = sem("s_bnd")
        s_bnp = sem("s_bnp")
        s_xfree = sem("s_xfree")
        s_xin = [sem(f"s_xin{b}") for b in range(RING)]
        s_xt = sem("s_xt")
        s_xTs = sem("s_xTs")
        s_mm1 = sem("s_mm1")
        s_ev_a = sem("s_ev_a")
        s_tw = [sem(f"s_tw{b}") for b in range(RING)]
        s_vq = sem("s_vq")
        s_pass = sem("s_pass")

        block = ctx.enter_context(nc.Block())

        def blk(c):
            return bass.ds(c * P, P)

        def over_blocks(eng, body):
            with eng.Fori(0, ROUNDS) as i:
                for b in range(RING):
                    body(i * RING + b, i, b)
            body(NB - 1, ROUNDS, 0)

        def rounds_of(b):
            return ROUNDS + (b == 0)

        def chunk(c):
            return bass.ds(c * CH, CH)

        def unsorted(eng):
            eng.wait_ge(s_flag, 1)
            return eng.value_load(flag[0:1, 0:1], min_val=0, max_val=1)

        g_const = sem("g_const")
        g_isl = sem("g_isl")
        g_oh = sem("g_oh")
        g_ga = [sem(f"g_ga{b}") for b in range(2)]
        g_mm = sem("g_mm")
        g_drain = sem("g_drain")
        g_dis = sem("g_dis")
        g_hb = sem("g_hb")
        g_tr = sem("g_tr")
        g_blk = sem("g_blk")
        g_blk2 = sem("g_blk2")
        g_used = sem("g_used")
        g_res = [sem(f"g_res{b}") for b in range(RING)]
        g_st = [sem(f"g_st{b}") for b in range(RING)]
        g_exp = sem("g_exp")
        g_var = sem("g_var")
        g_tr2 = sem("g_tr2")
        g_back = sem("g_back")
        g_vq = sem("g_vq")
        g_bn = sem("g_bn")
        g_bias = sem("g_bias")
        gS = early(NPAD)
        gB = early(NPAD)
        zero = early(P)
        stages = [("deg", KG), ("l0", KT)] + [(f"c{j}", KG) for j in range(4)]
        base_mm, base_t, base_g = [], [], []
        for q in range(len(stages)):
            base_mm.append(sum(2 + k for _, k in stages[:q]))
            base_t.append(sum(k for _, k in stages[:q]))
            base_g.append(sum(k for _, k in stages[1:q]))

        def agg_pool(pool, q):
            name, k = stages[q]
            rows = table_rows if name == "l0" else y_dram
            with pool.Fori(0, k // 2) as i:
                for b in range(2):
                    pool.wait_ge(g_isl, base_g[q] + i * 2 + b + 1)
                    pool.wait_ge(g_mm, base_mm[q] + i * 2 + b + 1)
                    pool.sem_inc(s_pass, 1)
                    pool.indirect_dma_start(out=gath[:, b, :], out_offset=None, in_=rows[:, :],
                                            in_offset=bass.IndirectOffsetOnAxis(ap=islot[:, b:b + 1], axis=0)
                                            ).then_inc(g_ga[b], 16)

        def agg_dve(dve, q):
            name, k = stages[q]

            def tiles(i):
                for b in range(2):
                    if name != "deg":
                        if base_g[q] or not isinstance(i, int):
                            dve.wait_ge(g_ga[b], 16 * (base_g[q] // 2) + i * 16)
                        col = row_col if name == "l0" else src_col
                        nc.vector.tensor_copy(islot[:, b:b + 1], col[:, bass.ds(i * 2 + b, 1)]).then_inc(g_isl, 1)
                    dve.wait_ge(g_mm, base_mm[q] + i * 2 + b + 1)
                    nc.vector.tensor_scalar(onehot[:, b, :], iota, dst_col[:, bass.ds(i * 2 + b, 1)], None,
                                            ALU.is_equal).then_inc(g_oh, 1)
            tiles(0)
            with dve.Fori(1, k // 2) as i:
                tiles(i)

        def agg_pe(pe, q):
            name, k = stages[q]
            if q:
                pe.wait_ge(g_drain, NCH * q)
            for c in range(NCH):
                m = nc.tensor.matmul(acc[:, c, 0:CH], zero, iota[:, 0:CH], start=True, stop=False,
                                     skip_group_check=True)
                if c >= NCH - 2:
                    m.then_inc(g_mm, 1)
            with pe.Fori(0, k // 2) as i:
                for b in range(2):
                    if name != "deg":
                        pe.wait_ge(g_ga[b], 16 * (base_g[q] // 2) + i * 16 + 16)
                    pe.wait_ge(g_oh, base_t[q] + i * 2 + b + 1)
                    lhs = ones[:] if name == "deg" else gath[:, b, :]
                    for c in range(NCH):
                        m = nc.tensor.matmul(acc[:, c, 0:CH], lhs, onehot[:, b, c * CH:(c + 1) * CH],
                                             start=False, stop=False, skip_group_check=True)
                    m.then_inc(g_mm, 1)

        def agg_done(eng, q):
            eng.wait_ge(g_mm, base_mm[q] + 2 + stages[q][1])

        def general_sp(sp):
            for b in range(RING):
                sp.sem_inc(g_st[b], 16)

            def residual(first, l0):
                def body(c, i, b):
                    sp.wait_ge(g_used, first + c + 1)
                    rows = LAST if isinstance(c, int) else P
                    if l0:
                        sp.dma_start(xs[0:rows, b, :], x[bass.ds(c * P, rows), :]).then_inc(g_res[b], 16)
                        sp.dma_start(rs[:, b, :], table[blk(c), T * F:SLOTS * F]).then_inc(g_res[b], 16)
                    else:
                        sp.dma_start(xs[:, b, :], x1_dram[blk(c), :]).then_inc(g_res[b], 16)
                return body

            def result(stage, dram):
                def body(c, i, b):
                    sp.wait_ge(g_blk, NB * stage + c + 1)
                    rows = LAST if dram is out and isinstance(c, int) else P
                    sp.dma_start(dram[bass.ds(c * P, rows), :], ob[0:rows, b, :]).then_inc(g_st[b], 16)
                return body
            agg_done(sp, 0)
            for first, stage, l0, dram in ((0, 0, True, x1_dram), (NB, 5, False, out)):
                load, put = residual(first, l0), result(stage, dram)
                if stage:
                    for j in range(4):
                        over_blocks(sp, result(j + 1, y_dram))
                    for b in range(RING):
                        sp.wait_ge(g_st[b], 16 * 5 * rounds_of(b) + 16)
                sp.wait_ge(g_used, RING + first)

                def both(c, i, b):
                    load(c, i, b)
                    put(c, i, b)
                over_blocks(sp, both)
            for b in range(RING):
                sp.wait_ge(g_st[b], 16 * 6 * rounds_of(b) + 16)

        def general_pool(pool):
            pool.wait_ge(s_idx, 1)
            nc.gpsimd.memset(zero, 0.0)
            nc.gpsimd.memset(gB, 1.0)
            nc.gpsimd.memset(gS, 0.0)
            nc.gpsimd.iota(iota, pattern=[[1, DW]], base=0, channel_multiplier=0,
                           allow_small_or_imprecise_dtypes=True).then_inc(g_const, 1)
            agg_pool(pool, 1)
            for j in range(4):
                for b in range(RING):
                    pool.wait_ge(g_st[b], 16 * (j + 2) * rounds_of(b) + 16)
                agg_pool(pool, 2 + j)

        def general_act(act):
            act.wait_ge(g_const, 1)
            agg_done(act, 0)
            for c in range(NCH):
                nc.scalar.activation(gB[:, chunk(c)], acc[:, c, 0:CH], ACT.Sqrt).then_inc(g_drain, 1)

            def copy_block(stage, func, bias=None, scale=None):
                def body(c, i, b):
                    act.wait_ge(g_tr, NB * stage + c + 1)
                    act.sem_inc(s_pass, 1)
                    kw = {} if bias is None else dict(bias=bias, scale=scale)
                    nc.scalar.activation(hb[:, b, :], gS[:, blk(c)], func, **kw).then_inc(g_hb, 1)
                return body

            def dis_block(c, i, b):
                act.wait_ge(g_tr, c + 1)
                act.sem_inc(s_pass, 1)
                nc.scalar.copy(hb[:, b, :], gB[:, blk(c)]).then_inc(g_hb, 1)
            act.wait_ge(g_dis, 1)
            act.wait_ge(g_tr, RING)
            over_blocks(act, dis_block)

            agg_done(act, 1)
            for c in range(NCH):
                nc.scalar.copy(gS[:, chunk(c)], acc[:, c, 0:CH]).then_inc(g_drain, 1)
            act.wait_ge(g_drain, 2 * NCH)
            first = copy_block(1, ACT.Copy)

            def l0_block(c, i, b):
                first(c, i, b)
                act.wait_ge(g_exp, c * 2 + 1)
                nc.scalar.activation(w2t, w1t, ACT.Exp).then_inc(g_exp, 1)
                act.wait_ge(g_var, c * 2 + 1)
                nc.scalar.activation(sd[:, 0:1], mv[:, 0, 1:2], ACT.Sqrt, bias=eps[:], scale=1.0).then_inc(g_var, 1)
                act.wait_ge(g_tr2, c + 1)
                act.sem_inc(s_pass, 1)
                nc.scalar.copy(gS[:, blk(c)], pst[:, 2 + b % 2, :]).then_inc(g_back, 1)
            act.wait_ge(g_tr, RING + NB)
            over_blocks(act, l0_block)
            act.wait_ge(g_back, NB)

            nvar = 2 * NB
            for j in range(4):
                if j == 0:
                    body = copy_block(2 + j, ACT.Copy)
                elif j < 3:
                    act.wait_ge(g_bn, j)
                    body = copy_block(2 + j, ACT.Relu, gs[:, 1:2], gs[:, 0:1])
                else:
                    body = copy_block(2 + j, ACT.Relu, cols[:, 6:7], 1.0)
                act.wait_ge(g_tr, RING + NB * (2 + j))
                over_blocks(act, body)
                if j < 2:
                    for c in range(NCH):
                        act.wait_ge(g_drain, NCH * (2 + j) + c + 1)
                        nc.scalar.activation(gS[:, chunk(c)], gS[:, chunk(c)], ACT.Identity,
                                             bias=cols[:, 3 * j:3 * j + 1], scale=1.0).then_inc(g_bias, 1)
                    act.wait_ge(g_var, nvar + 1)
                    nc.scalar.activation(sd[:, 0:1], mv[:, 0, 1:2], ACT.Sqrt, bias=eps[:], scale=1.0).then_inc(g_var, 1)
                    nvar += 2
                else:
                    act.wait_ge(g_drain, NCH * (3 + j))
            first = copy_block(6, ACT.Identity, cols[:, 6:7], 1.0)

            def fin_block(c, i, b):
                first(c, i, b)
                act.wait_ge(g_var, nvar + c * 2 + 1)
                nc.scalar.activation(sd[:, 0:1], mv[:, 0, 1:2], ACT.Sqrt, bias=eps[:], scale=1.0).then_inc(g_var, 1)
            act.wait_ge(g_tr, RING + NB * 6)
            over_blocks(act, fin_block)

        def general_dve(dve):
            vq = Chain(dve, g_vq)
            dve.sem_inc(g_used, RING)
            dve.sem_inc(g_blk2, 1)
            dve.wait_ge(g_const, 1)
            agg_dve(dve, 0)
            dve.wait_ge(g_drain, NCH)
            nc.vector.reciprocal(gB, gB).then_inc(g_dis, 1)

            def dis_block(c, i, b):
                dve.wait_ge(g_tr, RING + c + 1)
                nc.vector.tensor_copy(disC[:, bass.ds(c, 1)], pst[:, b % 2, 0:1]).then_inc(g_blk2, 1)
            over_blocks(dve, dis_block)
            agg_dve(dve, 1)

            def norm(c, nv):
                vq.step(nc.vector.bn_stats(bst[:, 0, :], w3t))
                dve.sem_inc(s_pass, 1)
                nc.vector.bn_aggr(mv[:, 0, :], bst[:, 0, :]).then_inc(g_var, 1)
                dve.wait_ge(g_var, nv + c * 2 + 2)
                vq.step(nc.vector.reciprocal(sd[:, 1:2], sd[:, 0:1]))

            def write_out(c, b, stored, nblk):
                dve.wait_ge(g_st[b], stored)
                nc.vector.tensor_scalar(ob[:, b, :], w3t, mv[:, 0, 0:1], sd[:, 1:2], ALU.subtract,
                                        ALU.mult).then_inc(g_blk, 1)
                dve.wait_ge(g_blk, nblk + c + 1)

            def l0_block(c, i, b):
                dve.wait_ge(g_tr, RING + NB + c + 1)
                dve.wait_ge(g_res[b], 32 * i + 32)
                vq.step(nc.vector.tensor_tensor(w4t, pst[:, b % 2, :], rs[:, b, :], ALU.add))
                nc.vector.tensor_scalar(w1t, w4t, 0.0, None, ALU.min).then_inc(g_exp, 1)
                vq.step(nc.vector.scalar_tensor_tensor(w3t, w4t, 0.0, xs[:, b, :], ALU.max, ALU.add))
                dve.sem_inc(g_used, 1)
                dve.wait_ge(g_exp, c * 2 + 2)
                vq.step(nc.vector.scalar_tensor_tensor(w3t, w2t, -1.0, w3t, ALU.add, ALU.add))
                norm(c, 0)
                write_out(c, b, 16 * i + 16, 0)

            with vq.rounds(0, ROUNDS, RING * 5) as i:
                for b in range(RING):
                    l0_block(i * RING + b, i, b)
            l0_block(NB - 1, ROUNDS, 0)

            nvar = 2 * NB
            for j in range(4):
                def y_block(c, i, b):
                    dve.wait_ge(g_tr, RING + NB * (2 + j) + c + 1)
                    dve.wait_ge(g_st[b], 16 * ((j + 1) * rounds_of(b) + i) + 16)
                    nc.vector.tensor_scalar(ob[:, b, :], pst[:, b % 2, :], disC[:, bass.ds(c, 1)], None,
                                            ALU.mult).then_inc(g_blk, 1)
                over_blocks(dve, y_block)
                agg_dve(dve, 2 + j)
                agg_done(dve, 2 + j)
                for c in range(NCH):
                    nc.vector.tensor_tensor(gS[:, chunk(c)], acc[:, c, 0:CH], gB[:, chunk(c)],
                                            ALU.mult).then_inc(g_drain, 1)
                if j < 2:
                    for c in range(NCH):
                        dve.wait_ge(g_bias, NCH * j + c + 1)
                        w = min(N, (c + 1) * CH) - c * CH
                        v = nc.vector.bn_stats(bst[:, c, :], gS[:, c * CH:c * CH + w])
                    vq.step(v)
                    nc.vector.bn_aggr(mv[:, 0, :], bst[:, 0:NCH, :].rearrange("p c s -> p (c s)")).then_inc(g_var, 1)
                    dve.wait_ge(g_var, nvar + 2)
                    nvar += 2
                    batch_norm(vq, j).then_inc(g_bn, 1)

            def fin_block(c, i, b):
                dve.wait_ge(g_tr, RING + NB * 6 + c + 1)
                dve.wait_ge(g_res[b], 32 * rounds_of(b) + 16 * i + 16)
                vq.step(nc.vector.tensor_tensor(w3t, pst[:, b % 2, :], xs[:, b, :], ALU.add))
                dve.sem_inc(g_used, 1)
                norm(c, nvar)
                write_out(c, b, 16 * (5 * rounds_of(b) + i) + 16, NB * 5)

            with vq.rounds(0, ROUNDS, RING * 3) as i:
                for b in range(RING):
                    fin_block(i * RING + b, i, b)
            fin_block(NB - 1, ROUNDS, 0)

        def general_pe(pe):
            pe.wait_ge(g_const, 1)
            agg_pe(pe, 0)
            pe.sem_inc(g_tr, RING)

            def dis_block(c, i, b):
                pe.wait_ge(g_hb, c + 1)
                pe.wait_ge(g_blk2, c + 1)
                nc.tensor.transpose(pst[:, b % 2, :], hb[:, b, :], ident[:]).then_inc(g_tr, 1)
            over_blocks(pe, dis_block)
            pe.wait_ge(g_blk2, NB + 1)
            agg_pe(pe, 1)

            def l0_block(c, i, b):
                pe.wait_ge(g_hb, NB + c + 1)
                nc.tensor.transpose(pst[:, b % 2, :], hb[:, b, :], ident[:]).then_inc(g_tr, 1)
                pe.wait_ge(g_blk, c + 1)
                nc.tensor.transpose(pst[:, 2 + b % 2, :], ob[:, b, :], ident[:]).then_inc(g_tr2, 1)
            over_blocks(pe, l0_block)
            pe.wait_ge(g_back, NB)

            for j in range(4):
                def y_block(c, i, b):
                    pe.wait_ge(g_hb, NB * (2 + j) + c + 1)
                    pe.wait_ge(g_blk, NB * (j + 1) + c)
                    nc.tensor.matmul(pst[:, b % 2, :], hb[:, b, :], Wc[:, min(j, 2), :], start=True,
                                     stop=True).then_inc(g_tr, 1)
                over_blocks(pe, y_block)
                agg_pe(pe, 2 + j)

            def fin_block(c, i, b):
                pe.wait_ge(g_hb, NB * 6 + c + 1)
                pe.wait_ge(g_blk, NB * 5 + c)
                nc.tensor.transpose(pst[:, b % 2, :], hb[:, b, :], ident[:]).then_inc(g_tr, 1)
            over_blocks(pe, fin_block)

        def batch_norm(vq, j):
            vq.step(nc.vector.reciprocal(sd[:, 1:2], sd[:, 0:1]))
            vq.step(nc.vector.tensor_tensor(gs[:, 0:1], sd[:, 1:2], cols[:, 3 * j + 1:3 * j + 2], ALU.mult))
            vq.step(nc.vector.tensor_tensor(sd[:, 1:2], mv[:, 0, 0:1], gs[:, 0:1], ALU.mult))
            return nc.vector.tensor_tensor(gs[:, 1:2], cols[:, 3 * j + 2:3 * j + 3], sd[:, 1:2], ALU.subtract)

        def nc_scale(vq, rows, at, n):
            b = small[:, 12:12 + n]
            vq.step(nc.vector.reduce_max(b, rows, axis=AX.X))
            vq.step(nc.vector.tensor_scalar(b, b, 1e-30, None, ALU.max))
            vq.step(nc.vector.tensor_scalar(b.bitcast(I32), b.bitcast(I32), 0x7F800000, None, ALU.bitwise_and))
            vq.step(nc.vector.tensor_scalar(scl[:, 8 + at:8 + at + n], b, 2.0 ** -14, None, ALU.mult))
            vq.step(nc.vector.reciprocal(scl[:, at:at + n], scl[:, 8 + at:8 + at + n]))
        k_start = sem("k_start")
        k_ix = sem("k_ix")
        k_ld = [sem(f"k_ld{q}") for q in range(4)]
        k_hi = sem("k_hi")
        k_lo = sem("k_lo")
        k_oh = sem("k_oh")
        k_pt = sem("k_pt")
        k_ao = sem("k_ao")
        k_pa = sem("k_pa")
        k_pg = sem("k_pg")
        k_av = sem("k_av")
        k_acc = sem("k_acc")
        k_ldm = sem("k_ldm")
        k_used = sem("k_used")
        k_z = sem("k_z")
        k_ex = sem("k_ex")
        k_var = sem("k_var")
        k_sq = sem("k_sq")
        k_ob = sem("k_ob")
        k_x1s = sem("k_x1s")
        k_tx = sem("k_tx")
        k_hbx = sem("k_hbx")
        k_y = sem("k_y")
        k_yh = sem("k_yh")
        k_yl = sem("k_yl")
        k_js = sem("k_js")
        k_jd = sem("k_jd")
        k_jh = sem("k_jh")
        k_jf = sem("k_jf")
        k_dcc = sem("k_dcc")
        k_ch = sem("k_ch")
        k_se = sem("k_se")
        k_sb = sem("k_sb")
        k_bv = sem("k_bv")
        k_bs = sem("k_bs")
        k_bn = sem("k_bn")
        k_mx = sem("k_mx")
        k_x1l = sem("k_x1l")
        k_fa = sem("k_fa")
        k_ft = sem("k_ft")
        k_fv = sem("k_fv")
        k_fs = sem("k_fs")
        k_fo = sem("k_fo")
        k_out = [sem(f"k_out{b}") for b in range(2)]

        islot_q = sb("islot_q", [P, TB], I32)
        HALF = MARGIN
        L0B = 7 - 1
        NGR = (NB + 3) // 4
        x1a = Yhl[:, 0:S1, :].rearrange("p c f -> p (c f)").bitcast(F32).rearrange("p (c f) -> p c f", f=F)
        x1b = Aflat[:, 0:(NB - S1) * 2 * F].bitcast(F32).rearrange("p (c f) -> p c f", f=F)
        wabs = sb("wabs", [P, F], F32)
        wf = Aflat[:, DW:DW + 4 * 512].bitcast(F32).rearrange("p (a w) -> p a w", a=2)
        of = Aflat[:, 2 * DW:2 * DW + 4 * 512].bitcast(F32).rearrange("p (a w) -> p a w", a=2)
        mvf = sb("mvf", [P, 2, 4, 2], F32)
        sdf = sb("sdf", [P, 2, 4], F32)

        def batches(last):
            return BATCH[:2] if last else BATCH

        def tiles_of(last, q):
            a, e = batches(last)[q]
            return a, min(e, KT - TB * (NB - 1)) if last else e

        def over_rounds(eng, body, vq=None, per=0):
            body(0, True, False)
            if vq is None:
                with eng.Fori(1, NB - 1) as j:
                    body(j, False, False)
            else:
                with vq.rounds(1, NB - 1, per) as j:
                    body(j, False, False)
            body(NB - 1, False, True)

        def bank_of(j):
            return j % 2

        def bank(b):
            return b if isinstance(b, int) else bass.ds(b, 1)

        def quick_pool(pool):
            pool.wait_ge(s_idx, 1)

            def gathers(j, first, last):
                for q in range(len(batches(last))):
                    pool.wait_ge(k_ix, 4 * j + q + 1)
                    pool.sem_inc(s_pass, 1)
                    a, e = tiles_of(last, q)
                    for i in range(a, e):
                        pool.indirect_dma_start(out=land[:, i, :], out_offset=None, in_=table_rows[:, :],
                                                in_offset=bass.IndirectOffsetOnAxis(ap=islot_q[:, i:i + 1], axis=0)
                                                ).then_inc(k_ld[q], 16)
            over_rounds(pool, gathers)

        def quick_sp(sp):
            sp.sem_inc(k_x1s, 16)
            for b in range(RING):
                sp.wait_ge(s_tw[b], 16 * rounds_of(b) + 16)

            def load(m):
                sp.wait_ge(k_used, m + 1)
                rows = LAST if isinstance(m, int) and m == NB - 1 else P
                sp.dma_start(xs1[0:rows], x[bass.ds(m * P, rows), :]).then_inc(k_ldm, 16)
                sp.dma_start(rs1, table[blk(m), T * F:SLOTS * F]).then_inc(k_ldm, 16)

            def store(m):
                sp.wait_ge(k_ob, m + 1)
                sp.dma_start(x1_dram[blk(m), :], ob1).then_inc(k_x1s, 16)
            load(0)
            with sp.Fori(0, NB - 2) as m:
                load(m + 1)
                store(m)
            load(NB - 1)
            store(NB - 2)
            store(NB - 1)
            sp.wait_ge(k_ch, NCH * 3 + 1)
            sp.wait_ge(k_x1s, 16 * NB + 16)
            sp.dma_start(x1a, x1_dram[0:S1 * P, :].rearrange("(c p) f -> p c f", p=P)).then_inc(k_x1l, 16)
            sp.dma_start(x1b, x1_dram[S1 * P:NPAD, :].rearrange("(c p) f -> p c f", p=P)).then_inc(k_x1l, 16)
            for g in range(NGR):
                sp.wait_ge(k_fo, g + 1)
                if g < NGR - 1:
                    sp.dma_start(out[g * 512:(g + 1) * 512, :].rearrange("(c p) f -> p c f", p=P),
                                 of[:, g % 2, :].rearrange("p (c f) -> p c f", f=F)).then_inc(k_out[g % 2], 16)
                else:
                    sp.dma_start(out[g * 512:N, :], of[0:LAST, g % 2, 0:F]).then_inc(k_out[g % 2], 16)
            for b in range(2):
                sp.wait_ge(k_out[b], 16 * ((NGR + 1 - b) // 2))

        def quick_act(act):
            for b in range(RING):
                act.wait_ge(s_tw[b], 16 * rounds_of(b) + 16)
            act.wait_ge(k_start, 1)

            def finish_exp(m):
                act.wait_ge(k_z, m + 1)
                nc.scalar.activation(w2t, w1t, ACT.Exp).then_inc(k_ex, 1)

            def finish_roots(m):
                act.wait_ge(k_var, m + 1)
                nc.scalar.activation(sd[:, 0:1], mv[:, 0, 1:2], ACT.Sqrt, bias=eps[:], scale=1.0)
                nc.scalar.activation(sd[:, 1:2], small[:, 20:21], ACT.Sqrt).then_inc(k_sq, 1)

            def finish_y(m):
                act.wait_ge(k_tx, m + 1)
                nc.scalar.copy(hb1, acc[:, 4, 0:F]).then_inc(k_hbx, 1)
                act.wait_ge(k_y, m + 1)
                act.sem_inc(s_pass, 1)
                nc.scalar.activation(Yhl[:, bass.ds(m, 1), 0:F], acc[:, 5:6, 0:F], ACT.Copy,
                                     scale=dcc[:, bass.ds(m, 1)]).then_inc(k_yh, 1)

            def work(j, first, last):
                n = len(batches(last))
                for q in range(n):
                    for gi in (2 * q, 2 * q + 1):
                        act.wait_ge(k_pg, GB * j + gi + 1)
                        act.sem_inc(s_pass, 1)
                        nc.scalar.activation(A[:, :, bass.ds(j * P + GW * gi, GW)],
                                             acc[:, 2 + gi % 2, 0:KW].rearrange("p (s r) -> p s r", r=GW),
                                             ACT.Copy).then_inc(k_av, 1)
                    a, e = tiles_of(last, q)
                    full = BATCH[q][1] - BATCH[q][0]
                    act.wait_ge(k_ld[q], 16 * (full * j + e - a))
                    if not first:
                        act.wait_ge(k_pt, TB * (j - 1) + BATCH[q][1])
                    nc.scalar.activation(ghl[:, a:e, 0:F], land[:, a:e, :], ACT.Copy,
                                         scale=scl[:, 0:1]).then_inc(k_hi, 1)
                    if not first and q == 1:
                        finish_exp(j - 1)
                    if not first and q == min(2, n - 1):
                        finish_roots(j - 1)
                if not first:
                    finish_y(j - 1)
            over_rounds(act, work)
            finish_exp(NB - 1)
            finish_roots(NB - 1)
            finish_y(NB - 1)

            act.sem_inc(k_jf, 1)
            for q in range(4):
                def apply(n, slot):
                    act.wait_ge(k_jd, NB * q + n + 1)
                    act.sem_inc(s_pass, 1)
                    bias, scale = (gs[:, 1:2], gs[:, 0:1]) if q < 3 else (cols[:, 6:7], 1.0)
                    nc.scalar.activation(ring6[:, slot, :], S[:, blk(n)], ACT.Relu, bias=bias,
                                         scale=scale).then_inc(k_js, 1)

                def high(n):
                    act.wait_ge(k_jd, JR + NB * q + n + 1)
                    act.sem_inc(s_pass, 1)
                    if q == 0:
                        nc.scalar.activation(disB[:, blk(n)], pst[:, 0, :], ACT.Copy).then_inc(k_jf, 1)
                    else:
                        nc.scalar.activation(Yhl[:, bass.ds(n, 1), 0:F], pst[:, 0:1, :], ACT.Copy,
                                             scale=dcc[:, bass.ds(n, 1)]).then_inc(k_jh, 1)
                if q == 0:
                    high(0)
                    with act.Fori(1, NB) as n:
                        high(n)
                else:
                    if q < 3:
                        act.wait_ge(k_bn, q)
                    else:
                        act.wait_ge(k_se, NCH * q)
                    apply(0, 0)
                    with act.Fori(0, (NB - 1) // JR) as i:
                        for m in range(JR):
                            apply(i * JR + m + 1, (m + 1) % JR)
                            if m == 0:
                                act.wait_ge(k_dcc, q)
                            high(i * JR + m)
                    high(NB - 1)
                if q < 2:
                    for c in range(NCH):
                        act.wait_ge(k_se, NCH * q + c + 1)
                        nc.scalar.activation(S[:, chunk(c)], S[:, chunk(c)], ACT.Identity,
                                             bias=cols[:, 3 * q:3 * q + 1], scale=1.0).then_inc(k_sb, 1)
                    act.wait_ge(k_bv, q + 1)
                    nc.scalar.activation(sd[:, 0:1], mv[:, 0, 1:2], ACT.Sqrt, bias=eps[:], scale=1.0).then_inc(k_bs, 1)

            def roots(g):
                w = min(4, NB - 4 * g)
                act.wait_ge(k_fv, g + 1)
                nc.scalar.activation(sdf[:, g % 2, 0:w], mvf[:, g % 2, 0:w, 1], ACT.Sqrt, bias=eps[:],
                                     scale=1.0).then_inc(k_fs, 1)
            act.wait_ge(k_jd, JR + NB * 4)
            act.wait_ge(k_x1s, 16 * NB + 16)
            for g in range(NGR):
                w = min(512, NPAD - 512 * g)
                act.wait_ge(k_se, NCH * 3 + min(NCH, (512 * g + w + CH - 1) // CH))
                if g >= 2:
                    act.wait_ge(k_ft, g - 1)
                nc.scalar.activation(U[:, (g % 2) * 512:(g % 2) * 512 + w], S[:, 512 * g:512 * g + w], ACT.Identity,
                                     bias=cols[:, 6:7], scale=1.0).then_inc(k_fa, 1)
                if g:
                    roots(g - 1)
            roots(NGR - 1)

        def quick_dve(dve, vq):
            dve.sem_inc(k_used, 1)
            for a, e in BATCH:
                nc.vector.tensor_copy(islot_q[:, a:e], row_col[:, a:e]).then_inc(k_ix, 1)
            nc.vector.tensor_copy(ident16[:], ident[:])
            nc.vector.memset(ghl[:, :, F:F + 1], 1.0).then_inc(k_start, 1)
            dve.wait_ge(s_gc, 1)

            def finish_z(m, bk):
                dve.wait_ge(k_acc, m + 1)
                dve.wait_ge(k_ldm, 32 * m + 32)
                vq.step(stt(w4t, acc[:, bank(bk), 0:F], scl[:, 8:9], rs1, ALU.mult, ALU.add))
                nc.vector.tensor_scalar(small[:, 20:21], acc[:, bank(bk), F:F + 1], 1.0, None, ALU.add)
                nc.vector.tensor_scalar(w1t, w4t, 0.0, None, ALU.min).then_inc(k_z, 1)
                vq.step(stt(w3t, w4t, 0.0, xs1, ALU.max, ALU.add))
                dve.sem_inc(k_used, 1)

            def finish_stats(m):
                dve.wait_ge(k_ex, m + 1)
                vq.step(stt(w3t, w2t, -1.0, w3t, ALU.add, ALU.add))
                vq.step(nc.vector.bn_stats(bst[:, 0, :], w3t))
                dve.sem_inc(s_pass, 1)
                nc.vector.bn_aggr(mv[:, 0, :], bst[:, 0, :]).then_inc(k_var, 1)

            def finish_x1(m):
                dve.wait_ge(k_sq, m + 1)
                vq.step(nc.vector.reciprocal(sd[:, 2:4], sd[:, 0:2]))
                if isinstance(m, int) and m == NB - 1:
                    vq.step(nc.vector.tensor_tensor(sd[:, 3:4], sd[:, 3:4], valid[:], ALU.mult))
                nc.vector.tensor_scalar(disC[:, bass.ds(m, 1)], sd[:, 3:4], 1.0, None, ALU.mult)
                nc.vector.tensor_scalar(dcc[:, bass.ds(m, 1)], sd[:, 3:4], scl[:, 1:2], None, ALU.mult)
                dve.wait_ge(k_x1s, 16 * m + 16)
                nc.vector.tensor_scalar(ob1, w3t, mv[:, 0, 0:1], sd[:, 2:3], ALU.subtract, ALU.mult).then_inc(k_ob, 1)

            def finish_low(m):
                dve.wait_ge(k_yh, m + 1)
                stt(Yhl[:, bass.ds(m, 1), F:2 * F].rearrange("p a f -> p (a f)"), acc[:, 5, 0:F],
                    dcc[:, bass.ds(m, 1)], Yhl[:, bass.ds(m, 1), 0:F].rearrange("p a f -> p (a f)"), ALU.mult,
                    ALU.subtract).then_inc(k_yl, 1)

            def work(j, first, last):
                n = len(batches(last))
                for q in range(n):
                    for t in range(6 * q, 6 * q + 6):
                        if not (first and t < AHS):
                            dve.wait_ge(k_pa, GB * GT * j + t - AHS + 1)
                        g = GB * j + t // GT
                        nc.vector.tensor_scalar(aoh[:, t % AHS, 0:P], iota16[:, 0:P],
                                                lo_col[:, t % GT, bass.ds(g, 1)], None, ALU.is_equal)
                        nc.vector.tensor_scalar(aoh[:, t % AHS, P:P + KW], iota16[:],
                                                key_col[:, t % GT, bass.ds(g, 1)], None,
                                                ALU.is_equal).then_inc(k_ao, 1)
                    a, e = tiles_of(last, q)
                    dve.wait_ge(k_hi, 4 * j + q + 1)
                    stt(ghl[:, a:e, 130:130 + F], land[:, a:e, :], scl[:, 0:1], ghl[:, a:e, 0:F], ALU.mult,
                        ALU.subtract).then_inc(k_lo, 1)
                    if not last:
                        nc.vector.tensor_copy(islot_q[:, a:e],
                                              row_col[:, bass.ds(TB * j + TB + a, e - a)]).then_inc(k_ix, 1)
                    for i in range(a, e):
                        if i >= OHS:
                            dve.wait_ge(k_pt, TB * j + i - OHS + 1)
                        elif not first:
                            before = max(t for t in range(TB) if t % OHS == i)
                            dve.wait_ge(k_pt, TB * (j - 1) + before + 1)
                        w = P if HALF <= i < TB - HALF else 2 * P
                        nc.vector.tensor_scalar(oh[:, i % OHS, 0:w], iota16[:, 0:w],
                                                rel_col[:, bass.ds(TB * j + i, 1)], None,
                                                ALU.is_equal).then_inc(k_oh, 1)
                    if not first and q == 1:
                        finish_z(j - 1, bank_of(j + 1))
                    if not first and q == min(2, n - 1):
                        finish_stats(j - 1)
                if not first:
                    finish_x1(j - 1)
                    finish_low(j - 1)
            over_rounds(dve, work, vq, 5)
            finish_z(NB - 1, bank_of(NB - 1))
            finish_stats(NB - 1)
            finish_x1(NB - 1)
            finish_low(NB - 1)

            vq.step(nc.vector.memset(S[:, DW:], 0.0))
            for q in range(4):
                if q == 0:
                    def diagonal(n, slot):
                        dve.wait_ge(k_jd, n + 1)
                        nc.vector.tensor_scalar(ring6[:, slot, :], ident[:], disC[:, bass.ds(n, 1)], None,
                                                ALU.mult).then_inc(k_js, 1)
                    diagonal(0, 0)
                    with dve.Fori(0, (NB - 1) // JR) as i:
                        for m in range(JR):
                            diagonal(i * JR + m + 1, (m + 1) % JR)
                else:
                    if q == 3:
                        vq.step(nc.vector.reduce_max(small[:, 16:17], mx[:, 0:NCH], axis=AX.X))
                        vq.step(nc.vector.tensor_scalar(small[:, 16:17], small[:, 16:17], cols[:, 6:7], 0.0, ALU.add,
                                                        ALU.max))
                        vq.step(magnitude(wabs[:], Wc[:, 2, :]))
                        nc.vector.tensor_scalar(wabs[:], wabs[:], small[:, 16:17], 1.01, ALU.mult,
                                                ALU.mult).then_inc(k_mx, 1)
                        dve.wait_ge(k_mx, 2)
                        nc_scale(vq, pst[:, 3:4, :], 4, 1)
                    nc.vector.tensor_scalar(dcc[:], disC[:], scl[:, q + 1:q + 2], None, ALU.mult).then_inc(k_dcc, 1)

                    def low(n):
                        dve.wait_ge(k_jh, NB * (q - 1) + n + 1)
                        stt(Yhl[:, bass.ds(n, 1), F:2 * F].rearrange("p a f -> p (a f)"), pst[:, 0, :],
                            dcc[:, bass.ds(n, 1)], Yhl[:, bass.ds(n, 1), 0:F].rearrange("p a f -> p (a f)"),
                            ALU.mult, ALU.subtract).then_inc(k_jf, 1)
                    with dve.Fori(0, NB) as n:
                        low(n)

                def stats(c):
                    w = min(N, (c + 1) * CH) - c * CH
                    if q < 2:
                        dve.wait_ge(k_sb, NCH * q + c + 1)
                        return nc.vector.bn_stats(bst[:, c, :], S[:, c * CH:c * CH + w])
                    dve.wait_ge(k_se, NCH * q + c + 1)
                    return nc.vector.reduce_max(mx[:, c:c + 1], S[:, c * CH:c * CH + w], axis=AX.X)
                if q == 0:
                    dve.wait_ge(k_jf, NB + 1)
                for c in range(NCH):
                    dve.wait_ge(k_ch, NCH * q + c + 1)
                    stt(S[:, chunk(c)], acc[:, c, 0:CH], scl[:, 9 + q:10 + q], disB[:, chunk(c)], ALU.mult,
                        ALU.mult).then_inc(k_se, 1)
                    if c and q < 3:
                        stats(c - 1)
                if q < 3:
                    vq.step(stats(NCH - 1))
                if q < 2:
                    nc.vector.bn_aggr(mv[:, 0, :], bst[:, 0:NCH, :].rearrange("p c s -> p (c s)")).then_inc(k_bv, 1)
                    dve.wait_ge(k_bs, q + 1)
                    batch_norm(vq, q).then_inc(k_bn, 1)

            def outputs(g):
                w = min(4, NB - 4 * g)
                dve.wait_ge(k_fs, g + 1)
                vq.step(nc.vector.reciprocal(sdf[:, g % 2, 0:w], sdf[:, g % 2, 0:w]))
                if g >= 2:
                    dve.wait_ge(k_out[g % 2], 16 * (g // 2))
                for k in range(w):
                    v = nc.vector.tensor_scalar(of[:, g % 2, k * F:(k + 1) * F], wf[:, g % 2, k * F:(k + 1) * F],
                                                mvf[:, g % 2, k, 0:1], sdf[:, g % 2, k:k + 1], ALU.subtract, ALU.mult)
                v.then_inc(k_fo, 1)
            dve.wait_ge(k_x1l, 32)
            for g in range(NGR):
                w = min(4, NB - 4 * g)
                dve.wait_ge(k_ft, g + 1)
                if g >= 2:
                    dve.wait_ge(k_fo, g - 1)
                ps = pst if g % 2 else acc[:, 0, :].rearrange("p (c f) -> p c f", f=F)
                for c0, c1, x1v, off in ((4 * g, min(4 * g + w, S1), x1a, 0), (max(4 * g, S1), 4 * g + w, x1b, S1)):
                    if c0 < c1:
                        lo, hi = c0 - 4 * g, c1 - 4 * g
                        v = nc.vector.tensor_tensor(wf[:, g % 2, lo * F:hi * F].rearrange("p (c f) -> p c f", f=F),
                                                    ps[:, lo:hi, :], x1v[:, c0 - off:c1 - off, :], ALU.add)
                vq.step(v)
                for k in range(w):
                    v = nc.vector.bn_stats(bst[:, 4 * (g % 2) + k, :], wf[:, g % 2, k * F:(k + 1) * F])
                vq.step(v)
                for k in range(w):
                    v = nc.vector.bn_aggr(mvf[:, g % 2, k, :], bst[:, 4 * (g % 2) + k, :])
                v.then_inc(k_fv, 1)
                if g:
                    outputs(g - 1)
            outputs(NGR - 1)

        def quick_pe(pe):
            pe.wait_ge(k_start, 1)

            def finish(m):
                pe.wait_ge(k_ob, m + 1)
                nc.tensor.transpose(acc[:, 4, 0:F], ob1, ident[:]).then_inc(k_tx, 1)
                pe.wait_ge(k_hbx, m + 1)
                nc.tensor.matmul(acc[:, 5, 0:F], hb1, Wc[:, 0, :], start=True, stop=True).then_inc(k_y, 1)

            def work(j, first, last):
                for q in range(len(batches(last))):
                    for gi in (2 * q, 2 * q + 1):
                        if not (first and gi < 2):
                            pe.wait_ge(k_av, GB * j + gi - 1)
                        for e in range(GT):
                            t = GT * gi + e
                            pe.wait_ge(k_ao, GB * GT * j + t + 1)
                            nc.tensor.matmul(acc[:, 2 + gi % 2, 0:KW], aoh[:, t % AHS, 0:P],
                                             aoh[:, t % AHS, P:P + KW], start=(e == 0), stop=False).then_inc(k_pa, 1)
                        nc.tensor.matmul(acc[:, 2 + gi % 2, bass.ds(j * GW, GW)], ident16[:],
                                         ident16[:, GW * gi:GW * gi + GW], start=False, stop=True).then_inc(k_pg, 1)
                    pe.wait_ge(k_lo, 4 * j + q + 1)
                    a, e = tiles_of(last, q)
                    for i in range(a, e):
                        pe.wait_ge(k_oh, TB * j + i + 1)
                        if i < HALF:
                            halves = [(j - 1, bank_of(j + 1))] * (not first) + [(j, bank_of(j))]
                        elif i < TB - HALF:
                            halves = [(j, bank_of(j))]
                        else:
                            halves = [(j, bank_of(j)), (j + 1, bank_of(j + 1))]
                        for n, (b, bk) in enumerate(halves):
                            own = n if i >= TB - HALF else n + (len(halves) < 2 and i < HALF)
                            begins = (i == TB - HALF and n == 1) or (first and i == 0)
                            ends = (i == HALF - 1 and n == 0 and not first) or (last and i == e - 1 and e < BATCH[q][1])
                            if i == TB - HALF and n == 1 and not first:
                                pe.wait_ge(k_z, j)
                            lhs = oh[:, i % OHS, own * P:(own + 1) * P]
                            nc.tensor.matmul(acc[:, bank(bk), 0:F + 1], lhs, ghl[:, i, 0:F + 1], start=begins,
                                             stop=False)
                            v = nc.tensor.matmul(acc[:, bank(bk), 0:F], lhs, ghl[:, i, 130:130 + F], start=False,
                                                 stop=ends)
                            if ends:
                                v.then_inc(k_acc, 1)
                                if last and i == e - 1:
                                    pe.sem_inc(k_pt, 1)
                            if n == len(halves) - 1 and not ends:
                                v.then_inc(k_pt, 1)
                if not first:
                    finish(j - 1)
            over_rounds(pe, work)
            finish(NB - 1)

            pe.wait_ge(k_yl, NB)
            pe.sem_inc(k_jd, JR)
            for q in range(4):
                if q == 3:
                    pe.wait_ge(k_mx, 1)
                    nc.tensor.matmul(pst[:, 3, :], ones[:], wabs[:], start=True, stop=True).then_inc(k_mx, 1)
                if q:
                    pe.wait_ge(k_se, NCH * q)
                    pe.wait_ge(k_dcc, q)

                def job(n, slot):
                    pe.wait_ge(k_js, NB * q + n + 1)
                    pe.wait_ge(k_jf, NB * q + n + 1)
                    lhs, rhs = (ones[:], ring6[:, slot, :]) if q == 0 else (ring6[:, slot, :], Wc[:, min(q, 2), :])
                    nc.tensor.matmul(pst[:, 0, :], lhs, rhs, start=True, stop=True).then_inc(k_jd, 1)

                def add(s, half, first=False):
                    if q and half == 0:
                        pe.wait_ge(k_jf, NB * q + s + 2)
                    for c in range(NCH):
                        lhs = Yhl[:, s, half * F:(half + 1) * F] if first else \
                            Yhl[:, bass.ds(s, 1), half * F:(half + 1) * F].rearrange("p a f -> p (a f)")
                        rhs = A[:, s, c * CH:(c + 1) * CH] if first else \
                            A[:, bass.ds(s, 1), c * CH:(c + 1) * CH].rearrange("p a f -> p (a f)")
                        nc.tensor.matmul(acc[:, c, 0:CH], lhs, rhs, start=(first and half == 0), stop=False)
                job(0, 0)
                add(0, 0, True)
                add(0, 1, True)
                with pe.Fori(0, 4) as i:
                    for h in range(8):
                        if h % 4 < 3:
                            m = h - h // 4
                            job(i * JR + m + 1, (m + 1) % JR)
                        add(i * 4 + 1 + h // 2, h % 2)
                if q:
                    pe.wait_ge(k_jf, NB * q + NB + 1)
                with pe.Fori(0, NCH) as c:
                    for s in range(S1, NB):
                        for half in range(2):
                            v = nc.tensor.matmul(acc[:, bass.ds(c, 1), 0:CH], Yhl[:, s, half * F:(half + 1) * F],
                                                 A[:, s, bass.ds(c * CH, CH)], start=False,
                                                 stop=(s == NB - 1 and half == 1))
                    v.then_inc(k_ch, 1)

            for g in range(NGR):
                w = min(4, NB - 4 * g)
                pe.wait_ge(k_fa, g + 1)
                if g >= 2:
                    pe.wait_ge(k_fv, g - 1)
                ps = pst if g % 2 else acc[:, 0, :].rearrange("p (c f) -> p c f", f=F)
                for k in range(w):
                    v = nc.tensor.transpose(ps[:, k, :], U[:, (g % 2) * 512 + k * F:(g % 2) * 512 + (k + 1) * F],
                                            ident[:])
                v.then_inc(k_ft, 1)
        @block.sync
        def _(sp):
            for b in range(RING):
                sp.sem_inc(s_tw[b], 16)

            def load_x(c, count, b):
                rows = LAST if isinstance(c, int) and c == NB - 1 else P
                sp.dma_start(xs[0:rows, b, :], x[bass.ds(c * P, rows), :]).then_inc(s_xin[b], 16)

            for b in range(RING):
                load_x(b, 0, b)
            sp.wait_ge(s_const, 1)
            full = (ER - 1) * EW
            for j, v in enumerate((src, dst, etype)):
                sp.dma_start(e_int[0:ER - 1, j, :], v[0:full].rearrange("(p e) -> p e", e=EW)).then_inc(s_e, 16)
                sp.dma_start(e_int[ER - 1:ER, j, 0:ETAIL], v[full:E].rearrange("(a e) -> a e", a=1)).then_inc(s_e, 16)
            sp.dma_start(n_next[0:ER - 2, :], dst[EW:full].rearrange("(p e) -> p e", e=EW)[:, 0:2]).then_inc(s_e, 16)
            sp.dma_start(n_next[ER - 2:ER - 1, :], dst[full:full + 2].rearrange("(p e) -> p e", e=2)).then_inc(s_e, 16)
            sp.wait_ge(s_pack, 1)
            rows = KT * P // GR
            sp.dma_start(packed[0:rows, :].rearrange("(p r) e -> p (r e)", r=EW // GR), e_pack[0:ER, :]).then_inc(s_packed, 16)
            sp.dma_start(packed[rows:CROWS, :], g_t[0:CROWS - rows, 0:GR]).then_inc(s_packed, 16)

            def store(c, i, b):
                sp.wait_ge(s_ev_a, c + 3)
                sp.dma_start(table[blk(c), :], trow[:, b, :]).then_inc(s_tw[b], 16)

            with sp.Fori(0, ROUNDS - 1) as i:
                for b in range(RING):
                    store(i * RING + b, i, b)
                    sp.wait_ge(s_xfree, i * RING + b + 1)
                    load_x((i + 1) * RING + b, i + 1, b)
            for b in range(RING):
                store((ROUNDS - 1) * RING + b, ROUNDS - 1, b)
                if b == 0:
                    sp.wait_ge(s_xfree, NB - RING)
                    load_x(NB - 1, ROUNDS, 0)
            store(NB - 1, ROUNDS, 0)

            bad = unsorted(sp)
            with sp.If(bad == 0):
                quick_sp(sp)
            with sp.Else():
                general_sp(sp)

        @block.gpsimd
        def _(pool):
            nc.gpsimd.memset(e_int[:, 0, :], 0)
            nc.gpsimd.memset(e_int[:, 1, :], NOWHERE)
            nc.gpsimd.memset(n_next[:], NOWHERE)
            nc.gpsimd.memset(e_int[:, 2, :], 0).then_inc(s_const, 1)
            nc.gpsimd.memset(ident[:], 0.0).then_inc(s_const, 1)
            pool.wait_ge(s_const, 2)
            nc.gpsimd.affine_select(out=ident[:], in_=ident[:], compare_op=ALU.not_equal, fill=1.0, base=0,
                                    pattern=[[-1, P]], channel_multiplier=1).then_inc(s_const, 1)
            nc.gpsimd.memset(ones[:], 1.0)
            nc.gpsimd.memset(eps[:], EPS)
            nc.gpsimd.memset(vall[:], 0.0)
            nc.gpsimd.memset(x_all[:, NB - 1, :], 0.0)
            nc.gpsimd.memset(g_t[:], NOWHERE * 4096)
            nc.gpsimd.iota(src_col[:, KT:KT + NB], pattern=[[P, NB]], base=0, channel_multiplier=1)
            nc.gpsimd.iota(dst_col[:, KT:KT + NB], pattern=[[P, NB]], base=0, channel_multiplier=1,
                           allow_small_or_imprecise_dtypes=True)
            nc.gpsimd.memset(src_col[:, KG - 1:KG], 0)
            nc.gpsimd.memset(dst_col[:, KG - 1:KG], float(NOWHERE))
            nc.gpsimd.memset(row_col[:, KT:], 0)
            nc.gpsimd.iota(iota16[:], pattern=[[1, KW]], base=0, channel_multiplier=0,
                           allow_small_or_imprecise_dtypes=True).then_inc(s_const, 1)
            pool.wait_ge(s_gidx, 1)
            pool.wait_ge(s_packed, 32)
            for h in range(2):
                for m in range(GROWS):
                    at = h * GE + m * GR
                    pool.indirect_dma_start(out=g_e[0:GH, at:at + GR], out_offset=None, in_=packed[:, :],
                                            in_offset=bass.IndirectOffsetOnAxis(ap=g_idx[0:GH, h, m:m + 1], axis=0)
                                            ).then_inc(s_gf, 16)
            for b in range(RING):
                pool.wait_ge(s_tw[b], 16 * rounds_of(b) + 16)
            bad = unsorted(pool)
            with pool.If(bad == 0):
                quick_pool(pool)
            with pool.Else():
                general_pool(pool)

        @block.scalar
        def _(act):
            act.sem_inc(s_ev_a, 2)
            act.dma_start(Ww.rearrange("k (t f) -> k t f", t=T), W_w.rearrange("t k f -> k t f")).then_inc(s_w, 16)
            act.dma_start(Wres, W_res).then_inc(s_w, 16)
            act.dma_start(bres[0:1, :], b_res.rearrange("(a f) -> a f", a=1)).then_inc(s_w, 16)
            act.dma_start(cst, const).then_inc(s_w, 16)
            for j, w in enumerate((W1, W2, W3)):
                act.dma_start(Wc[:, j, :], w).then_inc(s_w, 16)
            for j, v in enumerate((b1, g1, be1, b2, g2, be2, b3)):
                act.dma_start(cols[:, j:j + 1], v.rearrange("(f a) -> f a", a=1)).then_inc(s_w, 16)
            act.wait_ge(s_const, 4)
            act.dma_start(x_all[:, 0:NB - 1, :], x[0:(NB - 1) * P, :].rearrange("(c p) f -> p c f", p=P)).then_inc(s_xall, 16)
            act.dma_start(x_all[0:LAST, NB - 1, :], x[(NB - 1) * P:N, :]).then_inc(s_xall, 16)

            def turned(c, b):
                act.wait_ge(s_xt, c + 1)
                nc.scalar.copy(hb[:, b, :], pst[:, b, :]).then_inc(s_xTs, 1)
                act.sem_inc(s_xfree, 1)

            def rows_out(c, i, b):
                act.wait_ge(s_mm1, c + 1)
                act.wait_ge(s_tw[b], 16 * i + 16)
                k = 3 * (b % 2)
                nc.scalar.copy(trow[:, b, 0:T * F].rearrange("p (a w) -> p a w", a=2), acc[:, k:k + 2, :])
                nc.scalar.copy(trow[:, b, T * F:SLOTS * F], acc[:, k + 2, 0:F]).then_inc(s_ev_a, 1)

            turned(0, 0)
            with act.Fori(0, ROUNDS) as i:
                for b in range(RING):
                    c = i * RING + b
                    turned(c + 1, (b + 1) % RING)
                    rows_out(c, i, b)
            rows_out(NB - 1, ROUNDS, 0)

            act.wait_ge(s_gt, 1)
            for h in range(2):
                for col, bank in ((key_col, h), (lo_col, 2 + h)):
                    v = nc.scalar.copy(col[:, :, h * GH:(h + 1) * GH],
                                       acc[:, bank, 0:GT * GH].rearrange("p (e g) -> p e g", e=GT))
            v.then_inc(s_gc, 1)
            bad = unsorted(act)
            with act.If(bad == 0):
                quick_act(act)
            with act.Else():
                general_act(act)

        def stt(*a, **k):
            return nc.vector.scalar_tensor_tensor(*a, **k)

        def magnitude(o, i):
            return nc.vector.tensor_scalar(o.bitcast(I32), i.bitcast(I32), 0x7FFFFFFF, None, ALU.bitwise_and)

        @block.vector
        def _(dve):
            vq = Chain(dve, s_vq)
            dve.wait_ge(s_e, 16 * 8)
            dve.wait_ge(s_w, 16 * 14)
            dve.wait_ge(s_const, 4)
            d, n = e_int[0:ER, 1, :], e_int[0:ER, 0, :]
            ef = e_f[0:ER]
            tmp = e_tmp[0:ER]
            base = cst[0:ER, 8 + NTHR:8 + NTHR + EB]
            top = cst[0:ER, 8 + NTHR + EB:8 + NTHR + 2 * EB]

            def per_tile(v):
                return v.unsqueeze(2).to_broadcast([ER, EB, P])

            def as_tiles(v):
                return v.rearrange("p (b e) -> p b e", b=EB)
            stt(e_pack[0:ER], d, 4096.0, n, ALU.mult, ALU.add).then_inc(s_pack, 1)
            nc.vector.tensor_copy(valid[:], cst[:, 3:4])
            nc.vector.tensor_copy(ef[:, 0, :], n)
            vq.step(nc.vector.tensor_copy(ef[:, 1, :], d))
            stt(ef[:, 2, :], n, float(SLOTS), e_int[0:ER, 2, :], ALU.mult, ALU.add)
            nc.vector.tensor_tensor(as_tiles(ef[:, 3, :]), as_tiles(ef[:, 1, :]), per_tile(base),
                                    ALU.subtract).then_inc(s_ef, 1)
            for m in range(NTHR):
                v = nc.vector.tensor_scalar(tmp, ef[:, 1, :], cst[0:ER, 8 + m:9 + m], None, ALU.is_lt, ALU.add,
                                            accum_out=cnt[0:ER, m:m + 1])
                if m < NTHR - 1:
                    vq.step(v)
            v.then_inc(s_cnt, 1)
            dve.wait_ge(s_et, 1)
            dve.wait_ge(s_cnt, 1)
            for j, col in enumerate((src_col, dst_col, row_col, rel_col)):
                v = nc.vector.tensor_copy(col[:, 0:KT].rearrange("q (p b) -> q b p", b=EB),
                                          acc[:, j, 0:KT].rearrange("q (b p) -> q b p", b=EB))
            v.then_inc(s_idx, 1)
            dve.wait_ge(s_off, 1)
            vq.step(nc.vector.tensor_copy(off_i[0:GH, 0:4], acc[0:GH, 6, 0:4]))
            vq.step(nc.vector.tensor_scalar(off_i[0:GH, 0:2], off_i[0:GH, 0:2], 5, None, ALU.logical_shift_right))
            for h in range(2):
                for m in range(GROWS):
                    v = nc.vector.tensor_scalar(g_idx[0:GH, h, m:m + 1], off_i[0:GH, h:h + 1], float(m), None, ALU.add)
            v.then_inc(s_gidx, 1)
            stt(small[0:GH, 0:2], off_i[0:GH, 0:2], -float(GR), off_i[0:GH, 2:4], ALU.mult, ALU.add)
            vq.step(nc.vector.tensor_copy(d_next[0:ER], n_next[0:ER, 0:1]))
            vq.step(nc.vector.tensor_scalar(vall[0:GH, 6:8], small[0:GH, 0:2], float(GE), None, ALU.is_gt))
            vq.step(stt(tmp[:, 0:EW - 1], ef[:, 1, 0:EW - 1], 0.0, ef[:, 1, 1:EW], ALU.add, ALU.is_gt,
                        accum_out=vall[0:ER, 0:1]))
            nc.vector.tensor_tensor(vall[0:ER, 1:2], ef[:, 1, EW - 1:EW], d_next[0:ER], ALU.is_gt)
            nc.vector.tensor_copy(vall[0:ER, 2:3], cnt[0:ER, 0:1])
            nc.vector.tensor_tensor(vall[0:ER, 3:4], cst[0:ER, 0:1], cnt[0:ER, NTHR - 1:NTHR], ALU.subtract)
            vq.step(stt(as_tiles(tmp), as_tiles(ef[:, 1, :]), 0.0, per_tile(base), ALU.add, ALU.is_lt,
                        accum_out=vall[0:ER, 4:5]))
            vq.step(stt(as_tiles(tmp), as_tiles(ef[:, 1, :]), 0.0, per_tile(top), ALU.add, ALU.is_gt,
                        accum_out=vall[0:ER, 5:6]))
            nc.vector.reduce_sum(small[:, 2:3], vall[:], axis=AX.X).then_inc(s_viol, 1)

            dve.wait_ge(s_xall, 32)
            nc.vector.tensor_reduce(small[:, 3:4], x_all[:, :, :].rearrange("p c f -> p (c f)"), AX.X, ALU.max,
                                    apply_absolute_value=True).then_inc(s_bnd, 1)
            nc.vector.tensor_reduce(Wmax, Ww.rearrange("k (t f) -> k f t", t=T), AX.X, ALU.max,
                                    apply_absolute_value=True)
            dve.wait_ge(s_bnp, 1)
            vq.step(nc.vector.reduce_max(small[0:1, 4:5], acc[0:1, 6, 8:8 + P], axis=AX.X))
            dve.sem_inc(s_bnd, 1)
            dve.wait_ge(s_bnp, 2)
            vq.step(nc.vector.tensor_copy(small[:, 5:6], acc[:, 6, 4:5]))
            nc.vector.tensor_scalar(e_f[:, 0, 0:F], Wmax, small[:, 5:6], None, ALU.mult)
            magnitude(e_f[:, 0, F:4 * F], Wc[:, :, :].rearrange("p j f -> p (j f)"))
            for j in range(2):
                magnitude(small[:, 6 + j:7 + j], cols[:, 3 * j + 1:3 * j + 2])
                v = magnitude(small[:, 8 + j:9 + j], cols[:, 3 * j + 2:3 * j + 3])
            vq.step(v)
            vq.step(stt(small[:, 10:12], small[:, 6:8], 1.01 * N ** 0.5, small[:, 8:10], ALU.mult, ALU.add))
            nc.vector.tensor_scalar(e_f[:, 0, F:2 * F], e_f[:, 0, F:2 * F], 1.01 * F ** 0.5, None, ALU.mult)
            for j in range(2):
                w = e_f[:, 0, (2 + j) * F:(3 + j) * F]
                v = nc.vector.tensor_scalar(w, w, small[:, 10 + j:11 + j], None, ALU.mult)
            v.then_inc(s_bnd, 1)
            dve.wait_ge(s_bnp, 3)
            nc_scale(vq, acc[:, 6, :].rearrange("p (q f) -> p q f", f=F), 0, 4)

            dve.wait_ge(s_gf, 16 * 2 * GROWS)
            e, t, a, b, cc = g_e[0:GH], g_t[0:GH], g_a[0:GH], g_b[0:GH], g_c[0:GH]
            vq.step(nc.vector.tensor_scalar(t, e, 12, None, ALU.logical_shift_right))
            for h in range(2):
                v = nc.vector.tensor_scalar(a[:, h * GE:(h + 1) * GE], t[:, h * GE:(h + 1) * GE],
                                            cst[0:GH, 1 + h:2 + h], None, ALU.subtract)
            vq.step(v)
            vq.step(nc.vector.tensor_scalar(b, a, float(GW), None, ALU.is_ge))
            nc.vector.tensor_scalar(cc, a, 0.0, float(GW - 1), ALU.max, ALU.min)
            vq.step(nc.vector.tensor_scalar(t, e, 4095, 7, ALU.bitwise_and, ALU.logical_shift_right))
            vq.step(stt(b, a, 0.0, b, ALU.is_lt, ALU.add))
            vq.step(stt(cc, b, 1024.0, cc, ALU.mult, ALU.add))
            vq.step(stt(a, t, float(GW), cc, ALU.mult, ALU.add))
            vq.step(nc.vector.tensor_scalar(t, e, P - 1, None, ALU.bitwise_and))
            nc.vector.tensor_copy(b, t).then_inc(s_gk, 1)
            dve.wait_ge(s_vsum, 1)
            nc.vector.tensor_scalar(flag[:], acc[:, 6, 4:5], 1.0, None, ALU.min).then_inc(s_flag, 1)
            bad = unsorted(dve)
            with dve.If(bad == 0):
                quick_dve(dve, vq)
            with dve.Else():
                general_dve(dve)

        @block.tensor
        def _(pe):
            pe.wait_ge(s_const, 4)
            pe.wait_ge(s_ef, 1)
            for j in range(4):
                for b in range(EB):
                    m = nc.tensor.transpose(acc[:, j, b * ER:(b + 1) * ER], e_f[0:ER, j, b * P:(b + 1) * P],
                                            ident[0:ER, 0:ER])
            m.then_inc(s_et, 1)
            pe.wait_ge(s_w, 16 * 14)

            def turn(c, count, b):
                pe.wait_ge(s_xin[b], 16 * count + 16)
                if not isinstance(c, int) or c:
                    pe.wait_ge(s_xTs, c)
                nc.tensor.transpose(pst[:, b, :], xs[:, b, :], ident[:]).then_inc(s_xt, 1)

            def products(c, i, b):
                pe.wait_ge(s_xTs, c + 1)
                pe.wait_ge(s_ev_a, c + 1)
                k = 3 * (b % 2)
                for h in range(2):
                    nc.tensor.matmul(acc[:, k + h, 0:512], hb[:, b, :], Ww[:, h * 512:(h + 1) * 512], start=True,
                                     stop=True)
                nc.tensor.matmul(acc[:, k + 2, 0:F], hb[:, b, :], Wres, start=True, stop=False)
                nc.tensor.matmul(acc[:, k + 2, 0:F], ones[0:1, :], bres[0:1, :], start=False,
                                 stop=True).then_inc(s_mm1, 1)

            def table_round(i):
                for b in range(RING):
                    turn(i * RING + b + 1, i + (b + 1) // RING, (b + 1) % RING)
                    products(i * RING + b, i, b)

            turn(0, 0, 0)
            pe.wait_ge(s_idx, 1)
            table_round(0)
            pe.wait_ge(s_cnt, 1)
            at = 8 + NTHR + 3 * EB
            for j in range(4):
                h, nxt = j % 2, j // 2
                for m in range(NTHR + 1):
                    a = at + m * (NG + 1) + h * GH + nxt
                    rhs = cnt[0:ER, m:m + 1] if m < NTHR else cst[0:ER, 0:1]
                    v = nc.tensor.matmul(acc[0:GH, 6, j:j + 1], cst[0:ER, a:a + GH], rhs, start=(m == 0),
                                         stop=(m == NTHR))
            v.then_inc(s_off, 1)
            with pe.Fori(1, ROUNDS) as i:
                table_round(i)
            products(NB - 1, ROUNDS, 0)
            pe.wait_ge(s_bnd, 1)
            nc.tensor.transpose(acc[0:1, 6, 8:8 + P], small[:, 3:4], ident[:]).then_inc(s_bnp, 1)
            pe.wait_ge(s_bnd, 2)
            nc.tensor.matmul(acc[:, 6, 4:5], ones[0:1, :], small[0:1, 4:5], start=True, stop=True).then_inc(s_bnp, 1)
            pe.wait_ge(s_bnd, 3)
            nc.tensor.matmul(acc[:, 6, 0:512], ones[:], e_f[:, 0, :], start=True, stop=True).then_inc(s_bnp, 1)
            pe.wait_ge(s_gk, 1)
            pe.wait_ge(s_ev_a, NB + 2)
            for src_, bank in ((g_a, 0), (g_b, 2)):
                for h in range(2):
                    for e in range(GT):
                        v = nc.tensor.transpose(acc[:, bank + h, e * GH:(e + 1) * GH],
                                                src_[0:GH, h * GE + e * P:h * GE + (e + 1) * P], ident[0:GH, 0:GH])
            v.then_inc(s_gt, 1)
            pe.wait_ge(s_viol, 1)
            nc.tensor.matmul(acc[:, 6, 4:5], ones[:], small[:, 2:3], start=True, stop=True).then_inc(s_vsum, 1)
            pe.wait_ge(s_gc, 1)
            bad = unsorted(pe)
            with pe.If(bad == 0):
                quick_pe(pe)
            with pe.Else():
                general_pe(pe)


_INS = ["x", "src", "dst", "edge_type_8", "L0_gnn_W_w", "L0_gnn_W_res", "L0_gnn_b_res",
        "L1_gnn_W1", "L1_gnn_b1", "L1_gnn_g1", "L1_gnn_be1", "L1_gnn_W2", "L1_gnn_b2", "L1_gnn_g2", "L1_gnn_be2",
        "L1_gnn_W3", "L1_gnn_b3"]


def kernel(**inputs):
    import numpy as _np
    import concourse.bacc as _bacc
    from concourse import mybir as _mybir
    from concourse.bass_utils import run_bass_kernel_spmd as _run

    nc = _bacc.Bacc("TRN2", target_bir_lowering=False, num_devices=1)
    arrays, args = {}, []
    for name in _INS:
        a = _np.ascontiguousarray(inputs[name])
        arrays[f"in_{name}_dram"] = a
        args.append(nc.dram_tensor(f"in_{name}_dram", a.shape, _mybir.dt.from_np(a.dtype), kind="ExternalInput").ap())
    c = constants()
    arrays["const_dram"] = c
    args.append(nc.dram_tensor("const_dram", c.shape, _mybir.dt.float32, kind="ExternalInput").ap())
    args.append(nc.dram_tensor("out_0_dram", (N, F), _mybir.dt.float32, kind="ExternalOutput").ap())
    build(nc, *args)
    r = _run(nc, [arrays], core_ids=[0])
    return r.results[0]["out_0_dram"]
```

```python
import concourse.bass as bass
from concourse import mybir
from contextlib import ExitStack, contextmanager
import numpy as np

F32 = mybir.dt.float32
F16 = mybir.dt.float16
I32 = mybir.dt.int32
ALU = mybir.AluOpType
ACT = mybir.ActivationFunctionType
AX = mybir.AxisListType

P = 128
N = 3125
F = 128
E = 53125
T = 8
EPS = 1e-5
NB = (N + P - 1) // P
LAST = N - (NB - 1) * P
NPAD = NB * P
KT = (E + P - 1) // P
KG = KT + NB + 1
EB = 4
ER = KT // EB
EW = EB * P
ETAIL = E - (ER - 1) * EW
CH = 448
NCH = 7
DW = NCH * CH
NOWHERE = 4095
RING = 4
ROUNDS = (NB - 1) // RING

TB = E // N
MARGIN = 5
GW = 16
GB = P // GW
NG = DW // GW
GH = NG // 2
GR = 32
GROWS = 12
GE = GR * GROWS
GT = GE // P
KW = NB * GW
CROWS = (KT * P + GE) // GR
NTHR = 9
GCODE = 1 << 16
KCODE = 1 << 7
PAD_EDGE = (NOWHERE // GW) * GCODE
TR = 3
TROUNDS = (NB - 1) // TR
BATCH = [(0, 5), (5, 9), (9, 13), (13, 17)]
OHS = 6
AHS = 4
S1 = 17
S2 = 21


def constants():
    c = np.zeros((P, 8 + NTHR + 2 * EB), np.float32)
    p = np.arange(ER)
    gb = (p * EW * N) // (E * GW) - 3
    c[:ER, 0] = EW
    c[ER - 1, 0] = ETAIL
    c[:LAST, 3] = 1
    for h in range(2):
        c[:GH, 1 + h] = GCODE * (GH * h + np.arange(GH))
    for m in range(NTHR):
        c[:ER, 8 + m] = GW * (gb + m)
    for b in range(EB):
        k = EB * p + b
        j, i = k // TB, k % TB
        low = i < MARGIN
        base = P * (j - low)
        width = np.where(low | (i >= TB - MARGIN), 2 * P, P)
        c[:ER, 8 + NTHR + b] = base
        c[:ER, 8 + NTHR + EB + b] = np.where(j == NB - 1, NOWHERE, base + width - 1)
    return c


def window_masks():
    gb = (np.arange(ER) * EW * N) // (E * GW) - 3
    g = np.arange(NG + 1)
    m = np.zeros((ER, NTHR + 1, NG + 1), np.float16)
    for k in range(NTHR):
        m[:, k] = g[None] == (gb + k)[:, None]
    m[:, NTHR] = g[None] >= (gb + NTHR)[:, None]
    return m.reshape(ER, -1)


class Chain:

    def __init__(self, eng, sem):
        self.eng, self.sem, self.n, self.at = eng, sem, 0, 0

    def step(self, ins):
        self.n += 1
        ins.then_inc(self.sem, 1)
        self.eng.wait_ge(self.sem, self.at + self.n)

    @contextmanager
    def rounds(self, first, last, per):
        n0 = self.n
        with self.eng.Fori(first, last) as i:
            self.at = (i - first) * per if first else i * per
            yield i
        assert self.n - n0 == per, (self.n - n0, per)
        self.n = n0 + (last - first) * per
        self.at = 0


def build(nc, x, src, dst, etype, W_w, W_res, b_res, W1, b1, g1, be1, W2, b2, g2, be2, W3, b3, const, masks, out):
    ctx = ExitStack()
    with ctx:
        def sb(name, shape, dt):
            return ctx.enter_context(nc.sbuf_tensor(name, shape, dt))

        def sem(name):
            return ctx.enter_context(nc.semaphore(name))

        table = nc.dram_tensor("node_table", (NPAD, T * 2 * F), F16, kind="Internal").ap()
        table_rows = table.rearrange("n (t f) -> (n t) f", f=2 * F)
        res_dram = nc.dram_tensor("residual_rows", (NPAD, F), F32, kind="Internal").ap()
        y_dram = nc.dram_tensor("y_rows", (NPAD, F), F32, kind="Internal").ap()
        dis_dram = nc.dram_tensor("degree_roots", (NB, P), F32, kind="Internal").ap()
        x1_dram = nc.dram_tensor("x1_rows", (NPAD, F), F32, kind="Internal").ap()
        packed = nc.dram_tensor("packed_edges", (CROWS, GR), I32, kind="Internal").ap()

        ident = sb("ident", [P, P], F32)
        ident16 = sb("ident16", [P, P], F16)
        ones = sb("ones", [P, P], F32)
        eps = sb("eps", [P, 1], F32)
        iota16 = sb("iota16", [P, KW], F16)
        Wc = sb("Wc", [P, 3, F], F32)
        Wres = sb("Wres", [P, F], F32)
        bres = sb("bres", [1, F], F32)
        cols = sb("cols", [P, 7], F32)
        scl = sb("scl", [P, 16], F32)
        row_col = sb("row_col", [P, TB * NB], I32)
        rel_col = sb("rel_col", [P, KT], F32)
        lo_col = sb("lo_col", [P, GT, NG], F16)
        key_col = sb("key_col", [P, GT, NG], F16)
        disC = sb("disC", [P, NB], F32)
        dcc = sb("dcc", [P, NB], F32)
        small = sb("small", [P, 24], F32)
        vall = sb("vall", [P, 8], F32)
        flag = sb("flag", [P, 1], I32)
        valid = sb("valid", [P, 1], F32)
        bst = sb("bst", [P, 8, 6], F32)
        mv = sb("mv", [P, 4, 2], F32)
        sd = sb("sd", [P, 8], F32)
        gs = sb("gs", [P, 2], F32)
        mx = sb("mx", [P, 8], F32)
        Yhl = sb("Yhl", [P, NB, 2 * P], F16)
        U = sb("U", [P, 8 * F], F32)

        def u(a, n=1):
            return U[:, a * F:(a + n) * F]
        w1t, w2t, w3t, w4t, xs1, hbr, ob1, hb1 = (u(a) for a in range(8))

        R = sb("R", [P, 6400], F32)
        S = R[:, 0:NPAD]
        disB = R[:, NPAD:2 * NPAD]
        ghl = R[:, 0:TB * 130].bitcast(F16).rearrange("p (t w) -> p t w", w=260)
        at = TB * 130
        oh = R[:, at:at + OHS * P].bitcast(F16).rearrange("p (t w) -> p t w", w=2 * P)
        at += OHS * P
        aoh = R[:, at:at + AHS * (P + KW) // 2].bitcast(F16).rearrange("p (t w) -> p t w", w=P + KW)
        assert at + AHS * (P + KW) // 2 <= 6400

        A = sb("A", [P, NB, DW], F16)
        Aflat = A[:, :, :].rearrange("p s d -> p (s d)")
        taken = [0]

        def early(n, dt=F32, parts=P):
            a = taken[0]
            taken[0] += n
            assert taken[0] * 2 <= NB * DW
            return Aflat[0:parts, 2 * a:2 * (a + n)].bitcast(dt)

        Ww = early(T * F)
        bounds = early(1 + F)
        wtmp = early(3 * F)
        cst = early(8 + NTHR + 2 * EB)
        mask16 = early((NTHR + 1) * (NG + 1) // 2)[0:ER].bitcast(F16)
        cnt16 = early((NTHR + 1) // 2)[0:ER].bitcast(F16)
        x_all = early(NB * F).rearrange("p (c f) -> p c f", f=F)
        g_m = early(GROWS, I32)
        e_int = early(3 * EW, I32).rearrange("p (a e) -> p a e", a=3)
        e_f = early(4 * EW).rearrange("p (a e) -> p a e", a=4)
        e_tmp = early(EW)
        e_pack = early(EW, I32)
        d_next = early(1)
        n_next = early(2, I32)
        cnt = early(NTHR)
        g_idx = early(2 * GROWS, I32).rearrange("p (h m) -> p h m", h=2)
        g_e = early(2 * GE, I32)
        g_t = early(2 * GE, I32)
        g_a = early(2 * GE)
        g_b = early(2 * GE)
        g_w = early(2 * GE, I32)
        t_src = early(EW, I32)
        t_dst = early(EW, I32)
        off_i = early(6, I32)
        src_col = early(KG, I32)
        dst_col = early(KG)
        xs = early(RING * F).rearrange("p (a f) -> p a f", f=F)
        hb = early(RING * F).rearrange("p (a f) -> p a f", f=F)
        trow = early(TR * T * F).bitcast(F16).rearrange("p (a t f) -> p a t f", a=TR, t=T)
        rs = early(RING * F).rearrange("p (a f) -> p a f", f=F)
        ob = early(RING * F).rearrange("p (a f) -> p a f", f=F)
        iota = early(DW)
        onehot_ = early(2 * DW)
        onehot = onehot_.rearrange("p (a d) -> p a d", a=2)
        onehot16 = onehot_.bitcast(F16).rearrange("p (a d) -> p a d", a=4)
        gath_ = early(2 * F)
        gath = gath_.rearrange("p (a f) -> p a f", a=2)
        gath16 = gath_.bitcast(F16).rearrange("p (a f) -> p a f", a=2)
        islot = early(2, I32)

        acc = ctx.enter_context(nc.psum_tensor("acc", [P, NCH, 512], F32))
        pst = ctx.enter_context(nc.psum_tensor("pst", [P, 4, P], F32))

        s_const = sem("s_const")
        s_w = sem("s_w")
        s_cst = sem("s_cst")
        s_w1 = sem("s_w1")
        s_e = sem("s_e")
        s_xa = [sem(f"s_xa{h}") for h in range(2)]
        s_ef = sem("s_ef")
        s_et = sem("s_et")
        s_idx = sem("s_idx")
        s_pack = sem("s_pack")
        s_packed = sem("s_packed")
        s_cnt = sem("s_cnt")
        s_off = sem("s_off")
        s_gidx = sem("s_gidx")
        s_gf = sem("s_gf")
        s_gk = sem("s_gk")
        s_gt = sem("s_gt")
        s_gc = sem("s_gc")
        s_viol = sem("s_viol")
        s_vsum = sem("s_vsum")
        s_flag = sem("s_flag")
        s_bnd = sem("s_bnd")
        s_bnp = sem("s_bnp")
        s_xin = [sem(f"s_xin{b}") for b in range(TR)]
        s_scl = sem("s_scl")
        s_xt = sem("s_xt")
        s_xTs = sem("s_xTs")
        s_mm1 = sem("s_mm1")
        s_thi = sem("s_thi")
        s_tlo = sem("s_tlo")
        s_tw = [sem(f"s_tw{b}") for b in range(TR)]
        s_vq = sem("s_vq")
        s_pass = sem("s_pass")

        block = ctx.enter_context(nc.Block())

        def blk(c):
            return bass.ds(c * P, P)

        def over_blocks(eng, body):
            with eng.Fori(0, ROUNDS) as i:
                for b in range(RING):
                    body(i * RING + b, i, b)
            body(NB - 1, ROUNDS, 0)

        def rounds_of(b):
            return ROUNDS + (b == 0)

        def table_stored(b):
            return 16 * (TROUNDS + (b == 0)) + 16

        def chunk(c):
            return bass.ds(c * CH, CH)

        def unsorted(eng):
            eng.wait_ge(s_flag, 1)
            return eng.value_load(flag[0:1, 0:1], min_val=0, max_val=1)

        g_et = sem("g_et")
        g_col = sem("g_col")
        g_rl = sem("g_rl")
        g_rt = sem("g_rt")
        g_rh = sem("g_rh")
        g_rm = sem("g_rm")
        g_ro = sem("g_ro")
        g_rs = sem("g_rs")
        g_const = sem("g_const")
        g_isl = sem("g_isl")
        g_oh = sem("g_oh")
        g_ga = [sem(f"g_ga{b}") for b in range(2)]
        g_mm = sem("g_mm")
        g_drain = sem("g_drain")
        g_dis = sem("g_dis")
        g_hb = sem("g_hb")
        g_tr = sem("g_tr")
        g_blk = sem("g_blk")
        g_blk2 = sem("g_blk2")
        g_used = sem("g_used")
        g_res = [sem(f"g_res{b}") for b in range(RING)]
        g_st = [sem(f"g_st{b}") for b in range(RING)]
        g_exp = sem("g_exp")
        g_var = sem("g_var")
        g_tr2 = sem("g_tr2")
        g_back = sem("g_back")
        g_vq = sem("g_vq")
        g_bn = sem("g_bn")
        g_bias = sem("g_bias")
        gS = early(NPAD)
        gB = early(NPAD)
        zero = early(P)
        stages = [("deg", KG), ("l0", KT)] + [(f"c{j}", KG) for j in range(4)]
        base_mm, base_t, base_g = [], [], []
        for q in range(len(stages)):
            base_mm.append(sum(2 + k for _, k in stages[:q]))
            base_t.append(sum(k for _, k in stages[:q]))
            base_g.append(sum(k for _, k in stages[1:q]))

        def agg_pool(pool, q):
            name, k = stages[q]
            rows = table_rows if name == "l0" else y_dram
            with pool.Fori(0, k // 2) as i:
                for b in range(2):
                    pool.wait_ge(g_isl, base_g[q] + i * 2 + b + 1)
                    pool.wait_ge(g_mm, base_mm[q] + i * 2 + b + 1)
                    pool.sem_inc(s_pass, 1)
                    pool.indirect_dma_start(out=(gath16 if name == "l0" else gath)[:, b, :], out_offset=None, in_=rows[:, :],
                                            in_offset=bass.IndirectOffsetOnAxis(ap=islot[:, b:b + 1], axis=0)
                                            ).then_inc(g_ga[b], 16)

        def agg_dve(dve, q):
            name, k = stages[q]

            def tiles(i):
                for b in range(2):
                    if name != "deg":
                        if base_g[q] or not isinstance(i, int):
                            dve.wait_ge(g_ga[b], 16 * (base_g[q] // 2) + i * 16)
                        col = row_col if name == "l0" else src_col
                        nc.vector.tensor_copy(islot[:, b:b + 1], col[:, bass.ds(i * 2 + b, 1)]).then_inc(g_isl, 1)
                    dve.wait_ge(g_mm, base_mm[q] + i * 2 + b + 1)
                    nc.vector.tensor_scalar((onehot16 if name == "l0" else onehot)[:, b, :], iota, dst_col[:, bass.ds(i * 2 + b, 1)], None,
                                            ALU.is_equal).then_inc(g_oh, 1)
            tiles(0)
            with dve.Fori(1, k // 2) as i:
                tiles(i)

        def agg_pe(pe, q):
            name, k = stages[q]
            if q:
                pe.wait_ge(g_drain, NCH * q)
            for c in range(NCH):
                m = nc.tensor.matmul(acc[:, c, 0:CH], zero, iota[:, 0:CH], start=True, stop=False,
                                     skip_group_check=True)
                if c >= NCH - 2:
                    m.then_inc(g_mm, 1)
            with pe.Fori(0, k // 2) as i:
                for b in range(2):
                    if name != "deg":
                        pe.wait_ge(g_ga[b], 16 * (base_g[q] // 2) + i * 16 + 16)
                    pe.wait_ge(g_oh, base_t[q] + i * 2 + b + 1)
                    if name == "l0":
                        parts, hot = [gath16[:, b, 0:F], gath16[:, b, F:2 * F]], onehot16
                    else:
                        parts, hot = [ones[:] if name == "deg" else gath[:, b, :]], onehot
                    for lhs in parts:
                        for c in range(NCH):
                            m = nc.tensor.matmul(acc[:, c, 0:CH], lhs, hot[:, b, c * CH:(c + 1) * CH],
                                                 start=False, stop=False, skip_group_check=True)
                    m.then_inc(g_mm, 1)

        def agg_done(eng, q):
            eng.wait_ge(g_mm, base_mm[q] + 2 + stages[q][1])

        def general_sp(sp):
            for b in range(RING):
                sp.sem_inc(g_st[b], 16)

            def residual(first, l0):
                def body(c, i, b):
                    sp.wait_ge(g_used, first + c + 1)
                    rows = LAST if isinstance(c, int) else P
                    if l0:
                        sp.dma_start(xs[0:rows, b, :], x[bass.ds(c * P, rows), :]).then_inc(g_res[b], 16)
                        sp.dma_start(rs[:, b, :], res_dram[blk(c), :]).then_inc(g_res[b], 16)
                    else:
                        sp.dma_start(xs[:, b, :], x1_dram[blk(c), :]).then_inc(g_res[b], 16)
                return body

            def result(stage, dram):
                def body(c, i, b):
                    sp.wait_ge(g_blk, NB * stage + c + 1)
                    rows = LAST if dram is out and isinstance(c, int) else P
                    sp.dma_start(dram[bass.ds(c * P, rows), :], ob[0:rows, b, :]).then_inc(g_st[b], 16)
                return body
            sp.sem_inc(g_rs, 16)

            def residual_rows(c):
                rows = LAST if isinstance(c, int) else P
                sp.wait_ge(g_rt, c + 1)
                sp.dma_start(xs[0:rows, 0, :], x[bass.ds(c * P, rows), :]).then_inc(g_rl, 16)
                sp.wait_ge(g_ro, c + 2)
                sp.dma_start(res_dram[blk(c), :], rs[:, 0, :]).then_inc(g_rs, 16)
            with sp.Fori(0, NB - 1) as c:
                residual_rows(c)
            residual_rows(NB - 1)
            sp.wait_ge(g_rs, 16 * NB + 16)
            agg_done(sp, 0)
            for first, stage, l0, dram in ((0, 0, True, x1_dram), (NB, 5, False, out)):
                load, put = residual(first, l0), result(stage, dram)
                if stage:
                    for j in range(4):
                        over_blocks(sp, result(j + 1, y_dram))
                    for b in range(RING):
                        sp.wait_ge(g_st[b], 16 * 5 * rounds_of(b) + 16)
                sp.wait_ge(g_used, RING + first)

                def both(c, i, b):
                    load(c, i, b)
                    put(c, i, b)
                over_blocks(sp, both)
            for b in range(RING):
                sp.wait_ge(g_st[b], 16 * 6 * rounds_of(b) + 16)

        def general_pool(pool):
            pool.wait_ge(s_idx, 1)
            pool.wait_ge(g_col, 1)
            nc.gpsimd.memset(zero, 0.0)
            nc.gpsimd.memset(gB, 1.0)
            nc.gpsimd.memset(gS, 0.0)
            nc.gpsimd.iota(iota, pattern=[[1, DW]], base=0, channel_multiplier=0,
                           allow_small_or_imprecise_dtypes=True).then_inc(g_const, 1)
            agg_pool(pool, 1)
            for j in range(4):
                for b in range(RING):
                    pool.wait_ge(g_st[b], 16 * (j + 2) * rounds_of(b) + 16)
                agg_pool(pool, 2 + j)

        def general_act(act):
            act.sem_inc(g_ro, 1)
            with act.Fori(0, NB) as c:
                act.wait_ge(g_rt, c + 2)
                nc.scalar.copy(hb[:, 0, :], pst[:, 0, :]).then_inc(g_rh, 1)
                act.wait_ge(g_rm, c + 1)
                act.wait_ge(g_rs, 16 * c + 16)
                nc.scalar.copy(rs[:, 0, :], pst[:, 1, :]).then_inc(g_ro, 1)
            act.wait_ge(g_const, 1)
            agg_done(act, 0)
            for c in range(NCH):
                nc.scalar.activation(gB[:, chunk(c)], acc[:, c, 0:CH], ACT.Sqrt).then_inc(g_drain, 1)

            def copy_block(stage, func, bias=None, scale=None):
                def body(c, i, b):
                    act.wait_ge(g_tr, NB * stage + c + 1)
                    act.sem_inc(s_pass, 1)
                    kw = {} if bias is None else dict(bias=bias, scale=scale)
                    nc.scalar.activation(hb[:, b, :], gS[:, blk(c)], func, **kw).then_inc(g_hb, 1)
                return body

            def dis_block(c, i, b):
                act.wait_ge(g_tr, c + 1)
                act.sem_inc(s_pass, 1)
                nc.scalar.copy(hb[:, b, :], gB[:, blk(c)]).then_inc(g_hb, 1)
            act.wait_ge(g_dis, 1)
            act.wait_ge(g_tr, RING)
            over_blocks(act, dis_block)

            agg_done(act, 1)
            for c in range(NCH):
                nc.scalar.activation(gS[:, chunk(c)], acc[:, c, 0:CH], ACT.Copy, scale=scl[:, 8:9]).then_inc(g_drain, 1)
            act.wait_ge(g_drain, 2 * NCH)
            first = copy_block(1, ACT.Copy)

            def l0_block(c, i, b):
                first(c, i, b)
                act.wait_ge(g_exp, c * 2 + 1)
                nc.scalar.activation(w2t, w1t, ACT.Exp).then_inc(g_exp, 1)
                act.wait_ge(g_var, c * 2 + 1)
                nc.scalar.activation(sd[:, 0:1], mv[:, 0, 1:2], ACT.Sqrt, bias=eps[:], scale=1.0).then_inc(g_var, 1)
                act.wait_ge(g_tr2, c + 1)
                act.sem_inc(s_pass, 1)
                nc.scalar.copy(gS[:, blk(c)], pst[:, 2 + b % 2, :]).then_inc(g_back, 1)
            act.wait_ge(g_tr, RING + NB)
            over_blocks(act, l0_block)
            act.wait_ge(g_back, NB)

            nvar = 2 * NB
            for j in range(4):
                if j == 0:
                    body = copy_block(2 + j, ACT.Copy)
                elif j < 3:
                    act.wait_ge(g_bn, j)
                    body = copy_block(2 + j, ACT.Relu, gs[:, 1:2], gs[:, 0:1])
                else:
                    body = copy_block(2 + j, ACT.Relu, cols[:, 6:7], 1.0)
                act.wait_ge(g_tr, RING + NB * (2 + j))
                over_blocks(act, body)
                if j < 2:
                    for c in range(NCH):
                        act.wait_ge(g_drain, NCH * (2 + j) + c + 1)
                        nc.scalar.activation(gS[:, chunk(c)], gS[:, chunk(c)], ACT.Identity,
                                             bias=cols[:, 3 * j:3 * j + 1], scale=1.0).then_inc(g_bias, 1)
                    act.wait_ge(g_var, nvar + 1)
                    nc.scalar.activation(sd[:, 0:1], mv[:, 0, 1:2], ACT.Sqrt, bias=eps[:], scale=1.0).then_inc(g_var, 1)
                    nvar += 2
                else:
                    act.wait_ge(g_drain, NCH * (3 + j))
            first = copy_block(6, ACT.Identity, cols[:, 6:7], 1.0)

            def fin_block(c, i, b):
                first(c, i, b)
                act.wait_ge(g_var, nvar + c * 2 + 1)
                nc.scalar.activation(sd[:, 0:1], mv[:, 0, 1:2], ACT.Sqrt, bias=eps[:], scale=1.0).then_inc(g_var, 1)
            act.wait_ge(g_tr, RING + NB * 6)
            over_blocks(act, fin_block)

        def general_dve(dve):
            vq = Chain(dve, g_vq)
            dve.sem_inc(g_used, RING)
            dve.sem_inc(g_blk2, 1)
            dve.wait_ge(g_et, 1)
            for j, col in enumerate((src_col, dst_col)):
                v = nc.vector.tensor_copy(col[:, 0:KT].rearrange("q (p b) -> q b p", b=EB),
                                          acc[:, j, 0:KT].rearrange("q (b p) -> q b p", b=EB))
            v.then_inc(g_col, 1)
            dve.wait_ge(g_const, 1)
            agg_dve(dve, 0)
            dve.wait_ge(g_drain, NCH)
            nc.vector.reciprocal(gB, gB).then_inc(g_dis, 1)

            def dis_block(c, i, b):
                dve.wait_ge(g_tr, RING + c + 1)
                nc.vector.tensor_copy(disC[:, bass.ds(c, 1)], pst[:, b % 2, 0:1]).then_inc(g_blk2, 1)
            over_blocks(dve, dis_block)
            agg_dve(dve, 1)

            def norm(c, nv):
                vq.step(nc.vector.bn_stats(bst[:, 0, :], w3t))
                dve.sem_inc(s_pass, 1)
                nc.vector.bn_aggr(mv[:, 0, :], bst[:, 0, :]).then_inc(g_var, 1)
                dve.wait_ge(g_var, nv + c * 2 + 2)
                vq.step(nc.vector.reciprocal(sd[:, 1:2], sd[:, 0:1]))

            def write_out(c, b, stored, nblk):
                dve.wait_ge(g_st[b], stored)
                nc.vector.tensor_scalar(ob[:, b, :], w3t, mv[:, 0, 0:1], sd[:, 1:2], ALU.subtract,
                                        ALU.mult).then_inc(g_blk, 1)
                dve.wait_ge(g_blk, nblk + c + 1)

            def l0_block(c, i, b):
                dve.wait_ge(g_tr, RING + NB + c + 1)
                dve.wait_ge(g_res[b], 32 * i + 32)
                vq.step(nc.vector.tensor_tensor(w4t, pst[:, b % 2, :], rs[:, b, :], ALU.add))
                nc.vector.tensor_scalar(w1t, w4t, 0.0, None, ALU.min).then_inc(g_exp, 1)
                vq.step(nc.vector.scalar_tensor_tensor(w3t, w4t, 0.0, xs[:, b, :], ALU.max, ALU.add))
                dve.sem_inc(g_used, 1)
                dve.wait_ge(g_exp, c * 2 + 2)
                vq.step(nc.vector.scalar_tensor_tensor(w3t, w2t, -1.0, w3t, ALU.add, ALU.add))
                norm(c, 0)
                write_out(c, b, 16 * i + 16, 0)

            with vq.rounds(0, ROUNDS, RING * 5) as i:
                for b in range(RING):
                    l0_block(i * RING + b, i, b)
            l0_block(NB - 1, ROUNDS, 0)

            nvar = 2 * NB
            for j in range(4):
                def y_block(c, i, b):
                    dve.wait_ge(g_tr, RING + NB * (2 + j) + c + 1)
                    dve.wait_ge(g_st[b], 16 * ((j + 1) * rounds_of(b) + i) + 16)
                    nc.vector.tensor_scalar(ob[:, b, :], pst[:, b % 2, :], disC[:, bass.ds(c, 1)], None,
                                            ALU.mult).then_inc(g_blk, 1)
                over_blocks(dve, y_block)
                agg_dve(dve, 2 + j)
                agg_done(dve, 2 + j)
                for c in range(NCH):
                    nc.vector.tensor_tensor(gS[:, chunk(c)], acc[:, c, 0:CH], gB[:, chunk(c)],
                                            ALU.mult).then_inc(g_drain, 1)
                if j < 2:
                    for c in range(NCH):
                        dve.wait_ge(g_bias, NCH * j + c + 1)
                        w = min(N, (c + 1) * CH) - c * CH
                        v = nc.vector.bn_stats(bst[:, c, :], gS[:, c * CH:c * CH + w])
                    vq.step(v)
                    nc.vector.bn_aggr(mv[:, 0, :], bst[:, 0:NCH, :].rearrange("p c s -> p (c s)")).then_inc(g_var, 1)
                    dve.wait_ge(g_var, nvar + 2)
                    nvar += 2
                    batch_norm(vq, j).then_inc(g_bn, 1)

            def fin_block(c, i, b):
                dve.wait_ge(g_tr, RING + NB * 6 + c + 1)
                dve.wait_ge(g_res[b], 32 * rounds_of(b) + 16 * i + 16)
                vq.step(nc.vector.tensor_tensor(w3t, pst[:, b % 2, :], xs[:, b, :], ALU.add))
                dve.sem_inc(g_used, 1)
                norm(c, nvar)
                write_out(c, b, 16 * (5 * rounds_of(b) + i) + 16, NB * 5)

            with vq.rounds(0, ROUNDS, RING * 3) as i:
                for b in range(RING):
                    fin_block(i * RING + b, i, b)
            fin_block(NB - 1, ROUNDS, 0)

        def general_pe(pe):
            pe.wait_ge(s_w1, 16 * 12)
            pe.wait_ge(g_blk2, 1)
            pe.sem_inc(g_rt, 1)
            with pe.Fori(0, NB) as c:
                pe.wait_ge(g_rl, 16 * c + 16)
                pe.wait_ge(g_ro, c + 1)
                nc.tensor.transpose(pst[:, 0, :], xs[:, 0, :], ident[:]).then_inc(g_rt, 1)
                pe.wait_ge(g_rh, c + 1)
                nc.tensor.matmul(pst[:, 1, :], hb[:, 0, :], Wres[:], start=True, stop=False)
                nc.tensor.matmul(pst[:, 1, :], ones[0:1, :], bres[:], start=False, stop=True).then_inc(g_rm, 1)
            pe.wait_ge(g_ro, NB + 1)
            for j in range(2):
                for b in range(EB):
                    m = nc.tensor.transpose(acc[:, j, b * ER:(b + 1) * ER], e_f[0:ER, j, b * P:(b + 1) * P],
                                            ident[0:ER, 0:ER])
            m.then_inc(g_et, 1)
            pe.wait_ge(g_col, 1)
            pe.wait_ge(g_const, 1)
            agg_pe(pe, 0)
            pe.sem_inc(g_tr, RING)

            def dis_block(c, i, b):
                pe.wait_ge(g_hb, c + 1)
                pe.wait_ge(g_blk2, c + 1)
                nc.tensor.transpose(pst[:, b % 2, :], hb[:, b, :], ident[:]).then_inc(g_tr, 1)
            over_blocks(pe, dis_block)
            pe.wait_ge(g_blk2, NB + 1)
            agg_pe(pe, 1)

            def l0_block(c, i, b):
                pe.wait_ge(g_hb, NB + c + 1)
                nc.tensor.transpose(pst[:, b % 2, :], hb[:, b, :], ident[:]).then_inc(g_tr, 1)
                pe.wait_ge(g_blk, c + 1)
                nc.tensor.transpose(pst[:, 2 + b % 2, :], ob[:, b, :], ident[:]).then_inc(g_tr2, 1)
            over_blocks(pe, l0_block)
            pe.wait_ge(g_back, NB)

            for j in range(4):
                def y_block(c, i, b):
                    pe.wait_ge(g_hb, NB * (2 + j) + c + 1)
                    pe.wait_ge(g_blk, NB * (j + 1) + c)
                    nc.tensor.matmul(pst[:, b % 2, :], hb[:, b, :], Wc[:, min(j, 2), :], start=True,
                                     stop=True).then_inc(g_tr, 1)
                over_blocks(pe, y_block)
                agg_pe(pe, 2 + j)

            def fin_block(c, i, b):
                pe.wait_ge(g_hb, NB * 6 + c + 1)
                pe.wait_ge(g_blk, NB * 5 + c)
                nc.tensor.transpose(pst[:, b % 2, :], hb[:, b, :], ident[:]).then_inc(g_tr, 1)
            over_blocks(pe, fin_block)

        def batch_norm(vq, j):
            vq.step(nc.vector.reciprocal(sd[:, 1:2], sd[:, 0:1]))
            vq.step(nc.vector.tensor_tensor(gs[:, 0:1], sd[:, 1:2], cols[:, 3 * j + 1:3 * j + 2], ALU.mult))
            vq.step(nc.vector.tensor_tensor(sd[:, 1:2], mv[:, 0, 0:1], gs[:, 0:1], ALU.mult))
            return nc.vector.tensor_tensor(gs[:, 1:2], cols[:, 3 * j + 2:3 * j + 3], sd[:, 1:2], ALU.subtract)

        def power_scale(vq, rows, at, n, times=None):
            b = small[:, 12:12 + n]
            vq.step(nc.vector.reduce_max(b, rows, axis=AX.X))
            if times is not None:
                vq.step(nc.vector.tensor_scalar(b, b, times, None, ALU.mult))
            vq.step(nc.vector.tensor_scalar(b, b, 1e-30, None, ALU.max))
            vq.step(nc.vector.tensor_scalar(b.bitcast(I32), b.bitcast(I32), 0x7F800000, None, ALU.bitwise_and))
            vq.step(nc.vector.tensor_scalar(scl[:, 8 + at:8 + at + n], b, 2.0 ** -14, None, ALU.mult))
            vq.step(nc.vector.reciprocal(scl[:, at:at + n], scl[:, 8 + at:8 + at + n]))
        k_start = sem("k_start")
        k_ix = sem("k_ix")
        k_ld = [sem(f"k_ld{q}") for q in range(4)]
        k_oh = sem("k_oh")
        k_pt = sem("k_pt")
        k_ao = sem("k_ao")
        k_pa = sem("k_pa")
        k_pg = sem("k_pg")
        k_av = sem("k_av")
        k_acc = sem("k_acc")
        k_ldm = sem("k_ldm")
        k_rt = sem("k_rt")
        k_rh = sem("k_rh")
        k_rm = sem("k_rm")
        k_ro = sem("k_ro")
        k_z = sem("k_z")
        k_ex = sem("k_ex")
        k_var = sem("k_var")
        k_sq = sem("k_sq")
        k_ob = sem("k_ob")
        k_x1s = sem("k_x1s")
        k_tx = sem("k_tx")
        k_hbx = sem("k_hbx")
        k_y = sem("k_y")
        k_yh = sem("k_yh")
        k_yl = sem("k_yl")
        k_dt = sem("k_dt")
        k_dr = sem("k_dr")
        k_ds = sem("k_ds")
        k_db = sem("k_db")
        k_js = sem("k_js")
        k_jd = sem("k_jd")
        k_jh = sem("k_jh")
        k_jf = sem("k_jf")
        k_dcc = sem("k_dcc")
        k_ch = sem("k_ch")
        k_se = sem("k_se")
        k_bv = sem("k_bv")
        k_bs = sem("k_bs")
        k_bn = sem("k_bn")
        k_mx = sem("k_mx")
        k_x1l = sem("k_x1l")
        k_fa = sem("k_fa")
        k_ft = sem("k_ft")
        k_fv = sem("k_fv")
        k_fs = sem("k_fs")
        k_fm = sem("k_fm")
        k_fo = sem("k_fo")
        k_out = [sem(f"k_out{b}") for b in range(2)]

        rs1 = sb("rs1", [P, F], F32)
        islot_q = sb("islot_q", [P, TB], I32)
        HALF = MARGIN
        NGR = (NB + 3) // 4
        NJ = 1 + (NB - 1) // 4
        first_in = U[:, 512:512 + F]

        def group_in(k):
            return U[:, k * F:(k + 1) * F]
        dis_rows = U[0:NB, F:2 * F]
        nshift = sb("nshift", [P, 4, 4], F32)
        x1a = Yhl[:, 0:S1, :].rearrange("p c f -> p (c f)").bitcast(F32).rearrange("p (c f) -> p c f", f=F)
        x1b = Aflat[:, 0:(NB - S1) * 2 * F].bitcast(F32).rearrange("p (c f) -> p c f", f=F)
        wabs = sb("wabs", [P, F], F32)
        wf = Aflat[:, DW:DW + 8 * 512].bitcast(F32).rearrange("p (a w) -> p a w", a=4)
        of = Aflat[:, 3 * DW:3 * DW + 4 * 512].bitcast(F32).rearrange("p (a w) -> p a w", a=2)
        mvf = sb("mvf", [P, 4, 4, 2], F32)
        sdf = sb("sdf", [P, 4, 4], F32)

        def batches(last):
            return BATCH[:2] if last else BATCH

        def tiles_of(last, q):
            a, e = batches(last)[q]
            return a, min(e, KT - TB * (NB - 1)) if last else e

        def over_rounds(eng, body):
            body(0, True, False)
            with eng.Fori(1, NB - 1) as j:
                body(j, False, False)
            body(NB - 1, False, True)

        def bank_of(j):
            return j % 2

        def bank(b):
            return b if isinstance(b, int) else bass.ds(b, 1)

        def quick_pool(pool):
            pool.wait_ge(s_idx, 1)

            def gathers(j, first, last):
                for q in range(len(batches(last))):
                    pool.wait_ge(k_ix, 4 * j + q + 1)
                    if not first:
                        pool.wait_ge(k_pt, TB * (j - 1) + BATCH[q][1])
                    pool.sem_inc(s_pass, 1)
                    a, e = tiles_of(last, q)
                    for i in range(a, e):
                        pool.indirect_dma_start(out=ghl[:, i, 0:2 * F], out_offset=None, in_=table_rows[:, :],
                                                in_offset=bass.IndirectOffsetOnAxis(ap=islot_q[:, i:i + 1], axis=0)
                                                ).then_inc(k_ld[q], 16)
            over_rounds(pool, gathers)

        def quick_sp(sp):
            sp.sem_inc(k_x1s, 16)
            for b in range(TR):
                sp.wait_ge(s_tw[b], table_stored(b))

            def load(m):
                if not isinstance(m, int) or m:
                    sp.wait_ge(k_z, m)
                rows = LAST if isinstance(m, int) and m == NB - 1 else P
                sp.dma_start(xs1[0:rows], x[bass.ds(m * P, rows), :]).then_inc(k_ldm, 16)

            def store(m):
                sp.wait_ge(k_ob, m + 1)
                sp.dma_start(x1_dram[blk(m), :], ob1).then_inc(k_x1s, 16)
            load(0)
            with sp.Fori(0, NB - 2) as m:
                load(m + 1)
                store(m)
            load(NB - 1)
            store(NB - 2)
            store(NB - 1)
            sp.wait_ge(k_dr, 1)
            sp.dma_start(dis_dram, dis_rows).then_inc(k_ds, 16)
            sp.wait_ge(k_ds, 16)
            sp.dma_start(disB, bass.AP(tensor=dis_dram.tensor, offset=0, ap=[[0, P], [1, NPAD]])).then_inc(k_db, 16)
            sp.wait_ge(k_ch, NCH * 3 + 1)
            sp.wait_ge(k_x1s, 16 * NB + 16)
            sp.dma_start(x1a, x1_dram[0:S1 * P, :].rearrange("(c p) f -> p c f", p=P)).then_inc(k_x1l, 16)
            sp.dma_start(x1b, x1_dram[S1 * P:NPAD, :].rearrange("(c p) f -> p c f", p=P)).then_inc(k_x1l, 16)
            for g in range(NGR):
                sp.wait_ge(k_fo, g + 1)
                if g < NGR - 1:
                    sp.dma_start(out[g * 512:(g + 1) * 512, :].rearrange("(c p) f -> p c f", p=P),
                                 of[:, g % 2, :].rearrange("p (c f) -> p c f", f=F)).then_inc(k_out[g % 2], 16)
                else:
                    sp.dma_start(out[g * 512:N, :], of[0:LAST, g % 2, 0:F]).then_inc(k_out[g % 2], 16)
            for b in range(2):
                sp.wait_ge(k_out[b], 16 * ((NGR + 1 - b) // 2))

        def quick_act(act):
            act.wait_ge(s_idx, 1)
            for a, e in BATCH:
                nc.scalar.copy(islot_q[:, a:e], row_col[:, a:e]).then_inc(k_ix, 1)
            for b in range(TR):
                act.wait_ge(s_tw[b], table_stored(b))
            act.wait_ge(k_start, 1)

            def finish_exp(m):
                act.wait_ge(k_z, m + 1)
                nc.scalar.activation(w2t, w1t, ACT.Exp).then_inc(k_ex, 1)

            def finish_roots(m):
                act.wait_ge(k_var, m + 1)
                nc.scalar.activation(sd[:, 0:1], mv[:, 0, 1:2], ACT.Sqrt, bias=eps[:], scale=1.0)
                nc.scalar.activation(sd[:, 1:2], small[:, 20:21], ACT.Sqrt).then_inc(k_sq, 1)

            def finish_turn(m):
                act.wait_ge(k_tx, m + 1)
                nc.scalar.copy(hb1, acc[:, 4, 0:F]).then_inc(k_hbx, 1)

            def residual(m):
                act.wait_ge(k_rt, m + 1)
                nc.scalar.copy(hbr, pst[:, 0, :]).then_inc(k_rh, 1)

            def residual_out(m):
                act.wait_ge(k_rm, m + 1)
                nc.scalar.copy(rs1[:], pst[:, 1, :]).then_inc(k_ro, 1)

            def finish_y(m):
                act.wait_ge(k_y, m + 1)
                act.sem_inc(s_pass, 1)
                nc.scalar.activation(Yhl[:, bass.ds(m, 1), 0:F], acc[:, 5:6, 0:F], ACT.Copy,
                                     scale=dcc[:, bass.ds(m, 1)]).then_inc(k_yh, 1)

            def work(j, first, last):
                n = len(batches(last))
                for q in range(n):
                    if last and q == 1:
                        finish_exp(j - 1)
                    for gi in (2 * q, 2 * q + 1):
                        act.wait_ge(k_pg, GB * j + gi + 1)
                        act.sem_inc(s_pass, 1)
                        nc.scalar.activation(A[:, :, bass.ds(j * P + GW * gi, GW)],
                                             acc[:, 2 + gi % 2, 0:KW].rearrange("p (s r) -> p s r", r=GW),
                                             ACT.Copy).then_inc(k_av, 1)
                    if not last:
                        a, e = BATCH[q]
                        act.wait_ge(k_ld[q], 16 * (e - a) * (j + 1))
                        act.sem_inc(s_pass, 1)
                        nc.scalar.copy(islot_q[:, a:e], row_col[:, bass.ds(TB * j + TB + a, e - a)]).then_inc(k_ix, 1)
                    if not first and not last and q == 1:
                        finish_exp(j - 1)
                    if not first and q == min(2, n - 1):
                        finish_roots(j - 1)
                    if q == 2:
                        residual(j)
                    if q == 3:
                        residual_out(j)
                if not first:
                    finish_turn(j - 1)
                    if last:
                        residual(j)
                    finish_y(j - 1)
            over_rounds(act, work)
            residual_out(NB - 1)
            finish_exp(NB - 1)
            finish_roots(NB - 1)
            finish_turn(NB - 1)
            finish_y(NB - 1)

            act.wait_ge(k_dt, 1)
            nc.scalar.copy(dis_rows, pst[0:NB, 0, :]).then_inc(k_dr, 1)

            act.wait_ge(k_bv, 1)
            nc.scalar.activation(sd[:, 0:1], mv[:, 0, 1:2], ACT.Sqrt, bias=eps[:], scale=1.0).then_inc(k_bs, 1)
            for q in range(1, 4):
                def apply(g, cols_in, operand):
                    bias, scale = (gs[:, 1:2], gs[:, 0:1]) if q < 3 else (cols[:, 6:7], 1.0)
                    nc.scalar.activation(operand, S[:, cols_in], ACT.Relu, bias=bias, scale=scale).then_inc(k_js, 1)

                def high(g, blocks):
                    act.wait_ge(k_jd, NJ * (q - 1) + g + 1)
                    act.sem_inc(s_pass, 1)
                    for k, n in enumerate(blocks):
                        v = nc.scalar.activation(Yhl[:, bass.ds(n, 1), 0:F], pst[:, k:k + 1, :], ACT.Copy,
                                                 scale=dcc[:, bass.ds(n, 1)])
                    v.then_inc(k_jh, 1)

                def four(g):
                    return [4 * g - 3 + k for k in range(4)]
                if q < 3:
                    act.wait_ge(k_bn, q)
                else:
                    act.wait_ge(k_se, NCH * q)
                apply(0, slice(0, F), first_in)
                apply(1, slice(F, F + 512), U[:, 0:512])
                act.wait_ge(k_dcc, q)
                high(0, [0])
                with act.Fori(1, NJ - 1) as g:
                    high(g, four(g))
                    apply(g + 1, bass.ds((4 * g + 1) * F, 512), U[:, 0:512])
                high(NJ - 1, four(NJ - 1))
                if q < 2:
                    act.wait_ge(k_bv, q + 1)
                    nc.scalar.activation(sd[:, 0:1], mv[:, 0, 1:2], ACT.Sqrt, bias=eps[:], scale=1.0).then_inc(k_bs, 1)

            def roots(g):
                w = min(4, NB - 4 * g)
                act.wait_ge(k_fv, g + 1)
                nc.scalar.activation(sdf[:, g % 4, 0:w], mvf[:, g % 4, 0:w, 1], ACT.Sqrt, bias=eps[:],
                                     scale=1.0).then_inc(k_fs, 1)

            def outputs(g):
                w = min(4, NB - 4 * g)
                act.wait_ge(k_fm, g + 1)
                if g >= 2:
                    act.wait_ge(k_out[g % 2], 16 * (g // 2))
                for k in range(w):
                    v = nc.scalar.activation(of[:, g % 2, k * F:(k + 1) * F], wf[:, g % 4, k * F:(k + 1) * F],
                                             ACT.Identity, bias=nshift[:, g % 4, k:k + 1], scale=sdf[:, g % 4, k:k + 1])
                v.then_inc(k_fo, 1)
            def with_bias(g):
                w = min(512, NPAD - 512 * g)
                act.wait_ge(k_se, NCH * 3 + min(NCH, (512 * g + w + CH - 1) // CH))
                if g >= 2:
                    act.wait_ge(k_ft, g - 1)
                nc.scalar.activation(U[:, (g % 2) * 512:(g % 2) * 512 + w], S[:, 512 * g:512 * g + w], ACT.Identity,
                                     bias=cols[:, 6:7], scale=1.0).then_inc(k_fa, 1)
            act.wait_ge(k_jd, NJ * 3)
            act.wait_ge(k_x1s, 16 * NB + 16)
            with_bias(0)
            with_bias(1)
            for g in range(NGR):
                roots(g)
                if g + 2 < NGR:
                    with_bias(g + 2)
                if g:
                    outputs(g - 1)
            outputs(NGR - 1)

        def quick_dve(dve, vq):
            dve.sem_inc(k_yl, 1)
            nc.vector.tensor_copy(ident16[:], ident[:])
            nc.vector.memset(ghl[:, :, 2 * F:2 * F + 1], 1.0).then_inc(k_start, 1)
            dve.wait_ge(s_gc, 1)

            def finish_z(m, bk):
                dve.wait_ge(k_acc, m + 1)
                dve.wait_ge(k_ro, m + 1)
                stt(w4t, acc[:, bank(bk), 0:F], scl[:, 8:9], rs1[:], ALU.mult, ALU.add)
                vq.step(nc.vector.tensor_scalar(small[:, 20:21], acc[:, bank(bk), F:F + 1], 1.0, None, ALU.add))
                stt(w3t, w4t, 0.0, xs1, ALU.max, ALU.add)
                nc.vector.tensor_scalar(w1t, w4t, 0.0, None, ALU.min).then_inc(k_z, 1)

            def finish_stats(m):
                dve.wait_ge(k_ex, m + 1)
                vq.step(stt(w3t, w2t, -1.0, w3t, ALU.add, ALU.add))
                vq.step(nc.vector.bn_stats(bst[:, 0, :], w3t))
                dve.sem_inc(s_pass, 1)
                nc.vector.bn_aggr(mv[:, 0, :], bst[:, 0, :]).then_inc(k_var, 1)

            def finish_x1(m):
                dve.wait_ge(k_sq, m + 1)
                vq.step(nc.vector.reciprocal(sd[:, 2:4], sd[:, 0:2]))
                if isinstance(m, int) and m == NB - 1:
                    vq.step(nc.vector.tensor_tensor(sd[:, 3:4], sd[:, 3:4], valid[:], ALU.mult))
                nc.vector.tensor_scalar(disC[:, bass.ds(m, 1)], sd[:, 3:4], 1.0, None, ALU.mult)
                nc.vector.tensor_scalar(dcc[:, bass.ds(m, 1)], sd[:, 3:4], scl[:, 1:2], None, ALU.mult)
                dve.wait_ge(k_x1s, 16 * m + 16)
                nc.vector.tensor_scalar(ob1, w3t, mv[:, 0, 0:1], sd[:, 2:3], ALU.subtract, ALU.mult).then_inc(k_ob, 1)

            def finish_low(m):
                dve.wait_ge(k_yh, m + 1)
                stt(Yhl[:, bass.ds(m, 1), F:2 * F].rearrange("p a f -> p (a f)"), acc[:, 5, 0:F],
                    dcc[:, bass.ds(m, 1)], Yhl[:, bass.ds(m, 1), 0:F].rearrange("p a f -> p (a f)"), ALU.mult,
                    ALU.subtract).then_inc(k_yl, 1)

            def work(j, first, last):
                n = len(batches(last))
                for q in range(n):
                    if last and q == 1:
                        finish_z(j - 1, bank_of(j + 1))
                    for t in range(6 * q, 6 * q + 6):
                        if not (first and t < AHS):
                            dve.wait_ge(k_pa, GB * GT * j + t - AHS + 1)
                        g = GB * j + t // GT
                        nc.vector.tensor_scalar(aoh[:, t % AHS, 0:P], iota16[:, 0:P],
                                                lo_col[:, t % GT, bass.ds(g, 1)], None, ALU.is_equal)
                        nc.vector.tensor_scalar(aoh[:, t % AHS, P:P + KW], iota16[:],
                                                key_col[:, t % GT, bass.ds(g, 1)], None,
                                                ALU.is_equal).then_inc(k_ao, 1)
                    if q == 0 and (not isinstance(j, int) or j >= 2):
                        finish_low(j - 2)
                    if not first and not last and q == 1:
                        finish_z(j - 1, bank_of(j + 1))
                    if not first and q == (1 if last else 2):
                        finish_stats(j - 1)
                    if not first and q == (1 if last else 3):
                        finish_x1(j - 1)
                    a, e = tiles_of(last, q)
                    for i in range(a, e):
                        if i >= OHS:
                            dve.wait_ge(k_pt, TB * j + i - OHS + 1)
                        elif not first:
                            before = max(t for t in range(TB) if t % OHS == i)
                            dve.wait_ge(k_pt, TB * (j - 1) + before + 1)
                        w = P if HALF <= i < TB - HALF else 2 * P
                        nc.vector.tensor_scalar(oh[:, i % OHS, 0:w], iota16[:, 0:w],
                                                rel_col[:, bass.ds(TB * j + i, 1)], None,
                                                ALU.is_equal).then_inc(k_oh, 1)
            work(0, True, False)
            work(1, False, False)
            with vq.rounds(2, NB - 1, 4) as j:
                work(j, False, False)
            work(NB - 1, False, True)
            finish_low(NB - 2)
            finish_z(NB - 1, bank_of(NB - 1))
            finish_stats(NB - 1)
            finish_x1(NB - 1)
            finish_low(NB - 1)

            vq.step(nc.vector.memset(S[:, DW:], 0.0))

            def scale_sources(q):
                nc.vector.tensor_scalar(dcc[:], disC[:], scl[:, q + 1:q + 2], None, ALU.mult).then_inc(k_dcc, 1)
            for q in range(4):
                if q:
                    if q == 3:
                        vq.step(nc.vector.reduce_max(small[:, 16:17], mx[:, 0:NCH], axis=AX.X))
                        vq.step(nc.vector.tensor_scalar(small[:, 16:17], small[:, 16:17], cols[:, 6:7], 0.0, ALU.add,
                                                        ALU.max))
                        vq.step(magnitude(wabs[:], Wc[:, 2, :]))
                        nc.vector.tensor_scalar(wabs[:], wabs[:], small[:, 16:17], 1.01, ALU.mult,
                                                ALU.mult).then_inc(k_mx, 1)
                        dve.wait_ge(k_mx, 2)
                        power_scale(vq, pst[:, 3:4, :], 4, 1)
                        scale_sources(q)

                    def low(g, blocks):
                        dve.wait_ge(k_jh, NJ * (q - 1) + g + 1)
                        for k, n in enumerate(blocks):
                            v = stt(Yhl[:, bass.ds(n, 1), F:2 * F].rearrange("p a f -> p (a f)"), pst[:, k, :],
                                    dcc[:, bass.ds(n, 1)], Yhl[:, bass.ds(n, 1), 0:F].rearrange("p a f -> p (a f)"),
                                    ALU.mult, ALU.subtract)
                        v.then_inc(k_jf, 1)
                    low(0, [0])
                    with dve.Fori(1, NJ) as g:
                        low(g, [4 * g - 3 + k for k in range(4)])

                def stats(c):
                    w = min(N, (c + 1) * CH) - c * CH
                    dve.wait_ge(k_se, NCH * q + c + 1)
                    if q < 2:
                        return nc.vector.bn_stats(bst[:, c, :], S[:, c * CH:c * CH + w])
                    return nc.vector.reduce_max(mx[:, c:c + 1], S[:, c * CH:c * CH + w], axis=AX.X)

                def evacuate(c):
                    dve.wait_ge(k_ch, NCH * q + c + 1)
                    stt(S[:, chunk(c)], acc[:, c, 0:CH], scl[:, 9 + q:10 + q], disB[:, chunk(c)], ALU.mult,
                        ALU.mult).then_inc(k_se, 1)
                if q == 0:
                    dve.wait_ge(k_db, 16)
                if q < 3:
                    for c in range(NCH):
                        evacuate(c)
                        if c == 0 and q < 2:
                            scale_sources(q + 1)
                        v = stats(c)
                    vq.step(v)
                if q < 2:
                    nc.vector.bn_aggr(mv[:, 0, :], bst[:, 0:NCH, :].rearrange("p c s -> p (c s)")).then_inc(k_bv, 1)
                    dve.wait_ge(k_bs, q + 1)
                    b = cols[:, 3 * q:3 * q + 1]
                    nc.vector.tensor_tensor(mv[:, 0, 0:1], mv[:, 0, 0:1], b, ALU.add)
                    vq.step(nc.vector.reciprocal(sd[:, 1:2], sd[:, 0:1]))
                    nc.vector.tensor_tensor(mv[:, 0, 0:1], b, mv[:, 0, 0:1], ALU.subtract)
                    vq.step(nc.vector.tensor_tensor(gs[:, 0:1], sd[:, 1:2], cols[:, 3 * q + 1:3 * q + 2], ALU.mult))
                    stt(gs[:, 1:2], mv[:, 0, 0:1], gs[:, 0:1], cols[:, 3 * q + 2:3 * q + 3], ALU.mult,
                        ALU.add).then_inc(k_bn, 1)

            def scales(g):
                w = min(4, NB - 4 * g)
                dve.wait_ge(k_fs, g + 1)
                vq.step(nc.vector.reciprocal(sdf[:, g % 4, 0:w], sdf[:, g % 4, 0:w]))
                stt(nshift[:, g % 4, 0:w], mvf[:, g % 4, 0:w, 0], -1.0, sdf[:, g % 4, 0:w], ALU.mult,
                    ALU.mult).then_inc(k_fm, 1)

            def rows(g):
                w = min(4, NB - 4 * g)
                dve.wait_ge(k_ft, g + 1)
                if g >= 4:
                    dve.wait_ge(k_fo, g - 3)
                ps = pst if g % 2 else acc[:, 0, :].rearrange("p (c f) -> p c f", f=F)
                for c0, c1, x1v, off in ((4 * g, min(4 * g + w, S1), x1a, 0), (max(4 * g, S1), 4 * g + w, x1b, S1)):
                    if c0 < c1:
                        lo, hi = c0 - 4 * g, c1 - 4 * g
                        v = nc.vector.tensor_tensor(wf[:, g % 4, lo * F:hi * F].rearrange("p (c f) -> p c f", f=F),
                                                    ps[:, lo:hi, :], x1v[:, c0 - off:c1 - off, :], ALU.add)
                vq.step(v)
                for k in range(w):
                    v = nc.vector.bn_stats(bst[:, 4 * (g % 2) + k, :], wf[:, g % 4, k * F:(k + 1) * F])
                vq.step(v)
                for k in range(w):
                    v = nc.vector.bn_aggr(mvf[:, g % 4, k, :], bst[:, 4 * (g % 2) + k, :])
                v.then_inc(k_fv, 1)
                if g:
                    scales(g - 1)
            for c in range(NCH):
                evacuate(c)
                if c == 2:
                    dve.wait_ge(k_x1l, 32)
                if c >= 2:
                    rows(c - 2)
            for g in range(NCH - 2, NGR):
                rows(g)
            scales(NGR - 1)

        def quick_pe(pe):
            pe.wait_ge(k_start, 1)
            pe.wait_ge(s_w1, 16 * 12)

            def residual_turn(m):
                pe.wait_ge(k_ldm, 16 * m + 16)
                nc.tensor.transpose(pst[:, 0, :], xs1, ident[:]).then_inc(k_rt, 1)

            def residual_product(m):
                pe.wait_ge(k_rh, m + 1)
                nc.tensor.matmul(pst[:, 1, :], hbr, Wres[:], start=True, stop=False)
                nc.tensor.matmul(pst[:, 1, :], ones[0:1, :], bres[:], start=False, stop=True).then_inc(k_rm, 1)

            def finish_turn(m):
                pe.wait_ge(k_ob, m + 1)
                nc.tensor.transpose(acc[:, 4, 0:F], ob1, ident[:]).then_inc(k_tx, 1)

            def finish_y(m):
                pe.wait_ge(k_hbx, m + 1)
                pe.wait_ge(k_yl, m + 1)
                nc.tensor.matmul(acc[:, 5, 0:F], hb1, Wc[:, 0, :], start=True, stop=True).then_inc(k_y, 1)

            def work(j, first, last):
                for q in range(len(batches(last))):
                    for gi in (2 * q, 2 * q + 1):
                        if not (first and gi < 2):
                            pe.wait_ge(k_av, GB * j + gi - 1)
                        for e in range(GT):
                            t = GT * gi + e
                            pe.wait_ge(k_ao, GB * GT * j + t + 1)
                            nc.tensor.matmul(acc[:, 2 + gi % 2, 0:KW], aoh[:, t % AHS, 0:P],
                                             aoh[:, t % AHS, P:P + KW], start=(e == 0), stop=False).then_inc(k_pa, 1)
                        nc.tensor.matmul(acc[:, 2 + gi % 2, bass.ds(j * GW, GW)], ident16[:],
                                         ident16[:, GW * gi:GW * gi + GW], start=False, stop=True).then_inc(k_pg, 1)
                    if q == 3:
                        residual_product(j)
                    if q == (1 if last else 3) and not first:
                        finish_turn(j - 1)
                    if q == (1 if last else 2):
                        residual_turn(j)
                    a, e = tiles_of(last, q)
                    full = BATCH[q][1] - BATCH[q][0]
                    pe.wait_ge(k_ld[q], 16 * (full * j + e - a))
                    for i in range(a, e):
                        pe.wait_ge(k_oh, TB * j + i + 1)
                        if i < HALF:
                            halves = [(j - 1, bank_of(j + 1))] * (not first) + [(j, bank_of(j))]
                        elif i < TB - HALF:
                            halves = [(j, bank_of(j))]
                        else:
                            halves = [(j, bank_of(j)), (j + 1, bank_of(j + 1))]
                        for n, (b, bk) in enumerate(halves):
                            own = n if i >= TB - HALF else n + (len(halves) < 2 and i < HALF)
                            begins = (i == TB - HALF and n == 1) or (first and i == 0)
                            ends = (i == HALF - 1 and n == 0 and not first) or (last and i == e - 1 and e < BATCH[q][1])
                            if i == TB - HALF and n == 1 and not first:
                                pe.wait_ge(k_z, j)
                            lhs = oh[:, i % OHS, own * P:(own + 1) * P]
                            nc.tensor.matmul(acc[:, bank(bk), 0:F + 1], lhs, ghl[:, i, F:2 * F + 1], start=begins,
                                             stop=False)
                            v = nc.tensor.matmul(acc[:, bank(bk), 0:F], lhs, ghl[:, i, 0:F], start=False, stop=ends)
                            if ends:
                                v.then_inc(k_acc, 1)
                                if last and i == e - 1:
                                    pe.sem_inc(k_pt, 1)
                            if n == len(halves) - 1 and not ends:
                                v.then_inc(k_pt, 1)
                        if q == (1 if last else 3) and i == a + 1 and not first:
                            finish_y(j - 1)
            over_rounds(pe, work)
            residual_product(NB - 1)

            def begin_last_chunk(blocks):
                for s in blocks:
                    for half in range(2):
                        nc.tensor.matmul(acc[:, NCH - 1, 0:CH], Yhl[:, s, half * F:(half + 1) * F],
                                         A[:, s, (NCH - 1) * CH:DW], start=(s == 0 and half == 0), stop=False)
            pe.wait_ge(k_av, NG)
            pe.wait_ge(k_yl, NB - 1)
            begin_last_chunk(range(0, 12))
            finish_turn(NB - 1)
            nc.tensor.transpose(pst[0:NB, 0, :], disC[:], ident[:]).then_inc(k_dt, 1)
            begin_last_chunk(range(12, S2))
            finish_y(NB - 1)

            pe.wait_ge(k_yl, NB + 1)
            for q in range(4):
                if q == 3:
                    pe.wait_ge(k_mx, 1)
                    nc.tensor.matmul(pst[:, 3, :], ones[:], wabs[:], start=True, stop=True).then_inc(k_mx, 1)
                if q:
                    pe.wait_ge(k_se, NCH * q)
                    pe.wait_ge(k_dcc, q)

                def job(g, operands):
                    pe.wait_ge(k_js, NJ * (q - 1) + g + 1)
                    for k, operand in enumerate(operands):
                        v = nc.tensor.matmul(pst[:, k, :], operand, Wc[:, min(q, 2), :], start=True, stop=True)
                    v.then_inc(k_jd, 1)
                four = [group_in(k) for k in range(4)]

                def add(s):
                    for half in range(2):
                        for c in range(NCH - (q == 0)):
                            if isinstance(s, int):
                                lhs, rhs = Yhl[:, s, half * F:(half + 1) * F], A[:, s, c * CH:(c + 1) * CH]
                            else:
                                lhs = Yhl[:, bass.ds(s, 1), half * F:(half + 1) * F].rearrange("p a f -> p (a f)")
                                rhs = A[:, bass.ds(s, 1), c * CH:(c + 1) * CH].rearrange("p a f -> p (a f)")
                            nc.tensor.matmul(acc[:, c, 0:CH], lhs, rhs, start=(isinstance(s, int) and half == 0),
                                             stop=False)
                if q:
                    job(0, [first_in])
                    pe.wait_ge(k_jf, NJ * (q - 1) + 1)
                    job(1, four)
                add(0)
                with pe.Fori(0, ((S1 if q == 3 else S2) - 1) // 4) as i:
                    if q:
                        pe.wait_ge(k_jf, NJ * (q - 1) + i + 2)
                        job(i + 2, four)
                    for k in range(4):
                        add(i * 4 + 1 + k)

                def finish_chunk(c, blocks, last=True):
                    out_, cols_ = (acc[:, c:c + 1, 0:CH], slice(c * CH, (c + 1) * CH)) if isinstance(c, int) else \
                        (acc[:, bass.ds(c, 1), 0:CH], bass.ds(c * CH, CH))
                    for s in blocks:
                        for half in range(2):
                            v = nc.tensor.matmul(out_, Yhl[:, s, half * F:(half + 1) * F], A[:, s, cols_],
                                                 start=False, stop=(s == NB - 1 and half == 1))
                    if last:
                        v.then_inc(k_ch, 1)
                if q < 3:
                    if q:
                        pe.wait_ge(k_jf, NJ * q)
                    with pe.Fori(0, NCH) as c:
                        finish_chunk(c, range(S2, NB))

            def turn_rows(g):
                w = min(4, NB - 4 * g)
                pe.wait_ge(k_fa, g + 1)
                if g >= 2:
                    pe.wait_ge(k_fv, g - 1)
                ps = pst if g % 2 else acc[:, 0, :].rearrange("p (c f) -> p c f", f=F)
                for k in range(w):
                    v = nc.tensor.transpose(ps[:, k, :], U[:, (g % 2) * 512 + k * F:(g % 2) * 512 + (k + 1) * F],
                                            ident[:])
                v.then_inc(k_ft, 1)
            for g in range((S1 + 7) // 4, NJ + 1):
                pe.wait_ge(k_jf, NJ * 2 + g)
                if g < NJ:
                    job(g, four)
                finish_chunk(0, range(4 * g - 7, 4 * g - 3), last=(g == NJ))
            for c in range(1, NCH):
                finish_chunk(c, range(S1, NB))
                if c >= 2:
                    turn_rows(c - 2)
            for g in range(NCH - 2, NGR):
                turn_rows(g)
        def load_x(eng, c, b):
            rows = LAST if isinstance(c, int) and c == NB - 1 else P
            eng.dma_start(xs[0:rows, b, :], x[bass.ds(c * P, rows), :]).then_inc(s_xin[b], 16)

        @block.sync
        def _(sp):
            for b in range(TR):
                sp.sem_inc(s_tw[b], 16)
            half = NB // 2
            load_x(sp, 0, 0)
            sp.dma_start(x_all[:, 0:half, :], x[0:half * P, :].rearrange("(c p) f -> p c f", p=P)).then_inc(s_xa[0], 16)
            for b in range(1, TR):
                load_x(sp, b, b)
            sp.wait_ge(s_const, 1)
            full = (ER - 1) * EW
            for j, v in enumerate((dst, src, etype)):
                at = (1, 0, 2)[j]
                sp.dma_start(e_int[0:ER - 1, at, :], v[0:full].rearrange("(p e) -> p e", e=EW)).then_inc(s_e, 16)
                sp.dma_start(e_int[ER - 1:ER, at, 0:ETAIL], v[full:E].rearrange("(a e) -> a e", a=1)).then_inc(s_e, 16)
            sp.dma_start(n_next[0:ER - 2, :], dst[EW:full].rearrange("(p e) -> p e", e=EW)[:, 0:2]).then_inc(s_e, 16)
            sp.dma_start(n_next[ER - 2:ER - 1, :], dst[full:full + 2].rearrange("(p e) -> p e", e=2)).then_inc(s_e, 16)
            def store(c, i, b):
                sp.wait_ge(s_tlo, c + 1)
                sp.dma_start(table[blk(c), :], trow[:, b, :, :].rearrange("p t f -> p (t f)")).then_inc(s_tw[b], 16)

            def stores(first, last):
                with sp.Fori(first, last) as i:
                    for b in range(TR):
                        store(i * TR + b, i, b)
            stores(0, 2)
            sp.wait_ge(s_const, 4)
            sp.wait_ge(s_pack, 1)
            rows = KT * P // GR
            sp.dma_start(packed[0:rows, :].rearrange("(p r) e -> p (r e)", r=EW // GR), e_pack[0:ER, :]).then_inc(s_packed, 16)
            sp.dma_start(packed[rows:CROWS, :], g_t[0:CROWS - rows, 0:GR]).then_inc(s_packed, 16)

            stores(2, TROUNDS)
            store(NB - 1, TROUNDS, 0)

            bad = unsorted(sp)
            with sp.If(bad == 0):
                quick_sp(sp)
            with sp.Else():
                general_sp(sp)

        @block.gpsimd
        def _(pool):
            nc.gpsimd.memset(e_int[:, 0, :], 0)
            nc.gpsimd.memset(e_int[:, 1, :], NOWHERE)
            nc.gpsimd.memset(n_next[:], NOWHERE)
            nc.gpsimd.memset(e_int[:, 2, :], 0)
            nc.gpsimd.memset(x_all[:, NB - 1, :], 0.0).then_inc(s_const, 1)
            nc.gpsimd.memset(ident[:], 0.0).then_inc(s_const, 1)
            pool.wait_ge(s_const, 2)
            nc.gpsimd.affine_select(out=ident[:], in_=ident[:], compare_op=ALU.not_equal, fill=1.0, base=0,
                                    pattern=[[-1, P]], channel_multiplier=1).then_inc(s_const, 1)
            nc.gpsimd.memset(ones[:], 1.0)
            nc.gpsimd.memset(eps[:], EPS)
            nc.gpsimd.memset(vall[:], 0.0)
            nc.gpsimd.iota(g_m, pattern=[[1, GROWS]], base=0, channel_multiplier=0)
            nc.gpsimd.memset(g_t[:], PAD_EDGE)
            nc.gpsimd.iota(src_col[:, KT:KT + NB], pattern=[[P, NB]], base=0, channel_multiplier=1)
            nc.gpsimd.iota(dst_col[:, KT:KT + NB], pattern=[[P, NB]], base=0, channel_multiplier=1,
                           allow_small_or_imprecise_dtypes=True)
            nc.gpsimd.memset(src_col[:, KG - 1:KG], 0)
            nc.gpsimd.memset(dst_col[:, KG - 1:KG], float(NOWHERE))
            nc.gpsimd.memset(row_col[:, KT:], 0)
            nc.gpsimd.iota(iota16[:], pattern=[[1, KW]], base=0, channel_multiplier=0,
                           allow_small_or_imprecise_dtypes=True).then_inc(s_const, 1)
            pool.dma_start(Wres[:], W_res).then_inc(s_w1, 16)
            pool.dma_start(bres[:], b_res.rearrange("(a f) -> a f", a=1)).then_inc(s_w1, 16)
            for j, w in enumerate((W1, W2, W3)):
                pool.dma_start(Wc[:, j, :], w).then_inc(s_w1, 16)
            for j, v in enumerate((b1, g1, be1, b2, g2, be2, b3)):
                pool.dma_start(cols[:, j:j + 1], v.rearrange("(f a) -> f a", a=1)).then_inc(s_w1, 16)
            pool.wait_ge(s_gidx, 1)
            pool.wait_ge(s_packed, 32)
            for h in range(2):
                for m in range(GROWS):
                    at = h * GE + m * GR
                    pool.indirect_dma_start(out=g_e[0:GH, at:at + GR], out_offset=None, in_=packed[:, :],
                                            in_offset=bass.IndirectOffsetOnAxis(ap=g_idx[0:GH, h, m:m + 1], axis=0)
                                            ).then_inc(s_gf, 16)
            for b in range(TR):
                pool.wait_ge(s_tw[b], table_stored(b))
            bad = unsorted(pool)
            with pool.If(bad == 0):
                quick_pool(pool)
            with pool.Else():
                general_pool(pool)

        @block.scalar
        def _(act):
            act.dma_start(Ww.rearrange("k (t f) -> k t f", t=T), W_w.rearrange("t k f -> k t f")).then_inc(s_w, 16)
            half = NB // 2
            act.wait_ge(s_const, 1)
            act.dma_start(x_all[:, half:NB - 1, :],
                          x[half * P:(NB - 1) * P, :].rearrange("(c p) f -> p c f", p=P)).then_inc(s_xa[1], 16)
            act.dma_start(x_all[0:LAST, NB - 1, :], x[(NB - 1) * P:N, :]).then_inc(s_xa[1], 16)
            act.dma_start(cst, const).then_inc(s_cst, 16)
            act.dma_start(mask16, masks).then_inc(s_cst, 16)
            act.wait_ge(s_const, 4)
            nc.scalar.copy(sd[:, 7:8], eps[:])

            def turned(c, b):
                act.wait_ge(s_xt, c + 1)
                nc.scalar.copy(hb[:, b, :], pst[:, b, :]).then_inc(s_xTs, 1)

            def high(c, i, b):
                act.wait_ge(s_mm1, c + 1)
                act.wait_ge(s_tw[b], 16 * i + 16)
                nc.scalar.activation(trow[:, b, :, 0:F],
                                     acc[:, 2 * b:2 * b + 2, :].rearrange("p a (u f) -> p (a u) f", f=F), ACT.Copy,
                                     scale=scl[:, 0:1]).then_inc(s_thi, 1)

            def turn_and_load(c, b):
                turned(c, b)
                load_x(act, c + TR, b)

            turn_and_load(0, 0)
            turn_and_load(1, 1)
            act.wait_ge(s_scl, 1)
            high(0, 0, 0)
            turn_and_load(2, 2)
            high(1, 0, 1)
            turn_and_load(3, 0)
            high(2, 0, 2)
            with act.Fori(1, TROUNDS - 2) as i:
                for b in range(TR):
                    turn_and_load(i * TR + b + 1, (b + 1) % TR)
                    high(i * TR + b, i, b)
            for c in range(NB - 1 - 2 * TR, NB - 1):
                (turn_and_load if c + 1 + TR < NB else turned)(c + 1, (c + 1) % TR)
                high(c, c // TR, c % TR)
            high(NB - 1, TROUNDS, 0)

            act.wait_ge(s_et, 1)
            for j, col in enumerate((row_col, rel_col)):
                v = nc.scalar.copy(col[:, 0:KT].rearrange("q (p b) -> q b p", b=EB),
                                   acc[:, 2 + j, 0:KT].rearrange("q (b p) -> q b p", b=EB))
            v.then_inc(s_idx, 1)

            act.wait_ge(s_gt, 1)
            for h in range(2):
                for col, bank in ((key_col, 4 + h), (lo_col, h)):
                    v = nc.scalar.copy(col[:, :, h * GH:(h + 1) * GH],
                                       acc[:, bank, 0:GT * GH].rearrange("p (e g) -> p e g", e=GT))
            v.then_inc(s_gc, 1)
            bad = unsorted(act)
            with act.If(bad == 0):
                quick_act(act)
            with act.Else():
                general_act(act)

        def stt(*a, **k):
            return nc.vector.scalar_tensor_tensor(*a, **k)

        def magnitude(o, i):
            return nc.vector.tensor_scalar(o.bitcast(I32), i.bitcast(I32), 0x7FFFFFFF, None, ALU.bitwise_and)

        @block.vector
        def _(dve):
            vq = Chain(dve, s_vq)
            d, n = e_int[0:ER, 1, :], e_int[0:ER, 0, :]
            ef = e_f[0:ER]
            tmp = e_tmp[0:ER]
            base = cst[0:ER, 8 + NTHR:8 + NTHR + EB]
            top = cst[0:ER, 8 + NTHR + EB:8 + NTHR + 2 * EB]

            def per_tile(v):
                return v.unsqueeze(2).to_broadcast([ER, EB, P])

            def as_tiles(v):
                return v.rearrange("p (b e) -> p b e", b=EB)

            half = NB // 2
            dve.wait_ge(s_w, 16)
            nc.vector.tensor_reduce(bounds[:, 1:1 + F], Ww.rearrange("k (t f) -> k f t", t=T), AX.X, ALU.max,
                                    apply_absolute_value=True)
            dve.wait_ge(s_xa[0], 16)
            nc.vector.tensor_reduce(small[:, 3:4], x_all[:, 0:half, :].rearrange("p c f -> p (c f)"), AX.X, ALU.max,
                                    apply_absolute_value=True)
            dve.wait_ge(s_xa[1], 32)
            vq.step(nc.vector.tensor_reduce(small[:, 4:5], x_all[:, half:NB, :].rearrange("p c f -> p (c f)"), AX.X,
                                            ALU.max, apply_absolute_value=True))
            nc.vector.tensor_tensor(bounds[:, 0:1], small[:, 3:4], small[:, 4:5], ALU.max).then_inc(s_bnd, 1)
            dve.wait_ge(s_bnp, 1)
            vq.step(nc.vector.tensor_copy(small[:, 5:6], acc[:, 5, 0:1]))
            power_scale(vq, acc[:, 5:6, 1:1 + F], 0, 1, small[:, 5:6])
            dve.sem_inc(s_scl, 1)

            def threshold(m):
                return nc.vector.tensor_scalar(tmp, ef[:, 1, :], cst[0:ER, 8 + m:9 + m], None, ALU.is_lt, ALU.add,
                                               accum_out=cnt[0:ER, m:m + 1])

            def low(c, b):
                dve.wait_ge(s_thi, c + 1)
                stt(trow[:, b, :, F:2 * F], acc[:, 2 * b:2 * b + 2, :].rearrange("p a (u f) -> p (a u) f", f=F),
                    scl[:, 0:1], trow[:, b, :, 0:F], ALU.mult, ALU.subtract).then_inc(s_tlo, 1)

            dve.wait_ge(s_const, 4)
            dve.wait_ge(s_e, 16 * 8)
            nc.vector.tensor_copy(ef[:, 0, :], n)
            vq.step(nc.vector.tensor_copy(ef[:, 1, :], d))
            dve.wait_ge(s_cst, 16 * 2)
            low(0, 0)
            vq.step(threshold(0))
            vq.step(threshold(1))
            vq.step(threshold(2))
            low(1, 1)
            vq.step(threshold(3))
            vq.step(threshold(4))
            low(2, 2)
            vq.step(threshold(5))
            vq.step(threshold(6))
            low(3, 0)
            vq.step(threshold(7))
            vq.step(threshold(8))
            nc.vector.tensor_copy(cnt16[:, 0:NTHR], cnt[0:ER])
            nc.vector.tensor_copy(cnt16[:, NTHR:NTHR + 1], cst[0:ER, 0:1]).then_inc(s_cnt, 1)
            low(4, 1)
            nc.vector.tensor_scalar(t_src[0:ER], n, 7, None, ALU.logical_shift_right)
            vq.step(nc.vector.tensor_scalar(t_dst[0:ER], d, 4, None, ALU.logical_shift_right))
            low(5, 2)
            vq.step(stt(e_pack[0:ER], t_src[0:ER], float(GW * KCODE - P), n, ALU.mult, ALU.add))
            vq.step(stt(e_pack[0:ER], d, float(KCODE), e_pack[0:ER], ALU.mult, ALU.add))
            low(6, 0)
            stt(e_pack[0:ER], t_dst[0:ER], float(GCODE - GW * KCODE), e_pack[0:ER], ALU.mult,
                ALU.add).then_inc(s_pack, 1)
            low(7, 1)
            dve.wait_ge(s_off, 1)
            vq.step(nc.vector.tensor_copy(off_i[0:GH, 0:4], acc[0:GH, 5, 0:4]))
            vq.step(nc.vector.tensor_scalar(off_i[0:GH, 0:2], off_i[0:GH, 0:2], 5, None, ALU.logical_shift_right))
            for h in range(2):
                v = nc.vector.tensor_tensor(g_idx[0:GH, h, :], g_m[0:GH, :],
                                            off_i[0:GH, h:h + 1].to_broadcast([GH, GROWS]), ALU.add)
            v.then_inc(s_gidx, 1)
            low(8, 2)
            nc.vector.tensor_tensor(as_tiles(ef[:, 3, :]), as_tiles(ef[:, 1, :]), per_tile(base), ALU.subtract)
            stt(ef[:, 2, :], n, float(T), e_int[0:ER, 2, :], ALU.mult, ALU.add).then_inc(s_ef, 1)
            stt(small[0:GH, 0:2], off_i[0:GH, 0:2], -float(GR), off_i[0:GH, 2:4], ALU.mult, ALU.add)
            with dve.Fori(3, TROUNDS - 3) as i:
                for b in range(TR):
                    low(i * TR + b, b)

            c = (TROUNDS - 3) * TR
            low(c, 0)
            nc.vector.tensor_copy(valid[:], cst[:, 3:4])
            vq.step(nc.vector.tensor_copy(d_next[0:ER], n_next[0:ER, 0:1]))
            vq.step(nc.vector.tensor_scalar(vall[0:GH, 6:8], small[0:GH, 0:2], float(GE), None, ALU.is_gt))
            vq.step(stt(tmp[:, 0:EW - 1], ef[:, 1, 0:EW - 1], 0.0, ef[:, 1, 1:EW], ALU.add, ALU.is_gt,
                        accum_out=vall[0:ER, 0:1]))
            low(c + 1, 1)
            nc.vector.tensor_tensor(vall[0:ER, 1:2], ef[:, 1, EW - 1:EW], d_next[0:ER], ALU.is_gt)
            nc.vector.tensor_copy(vall[0:ER, 2:3], cnt[0:ER, 0:1])
            nc.vector.tensor_tensor(vall[0:ER, 3:4], cst[0:ER, 0:1], cnt[0:ER, NTHR - 1:NTHR], ALU.subtract)
            vq.step(stt(as_tiles(tmp), as_tiles(ef[:, 1, :]), 0.0, per_tile(base), ALU.add, ALU.is_lt,
                        accum_out=vall[0:ER, 4:5]))
            low(c + 2, 2)
            vq.step(stt(as_tiles(tmp), as_tiles(ef[:, 1, :]), 0.0, per_tile(top), ALU.add, ALU.is_gt,
                        accum_out=vall[0:ER, 5:6]))
            nc.vector.reduce_sum(small[:, 2:3], vall[:], axis=AX.X).then_inc(s_viol, 1)

            c += TR
            low(c, 0)
            dve.wait_ge(s_w1, 16 * 12)
            magnitude(wtmp[:], Wc[:, :, :].rearrange("p j f -> p (j f)"))
            for j in range(2):
                magnitude(small[:, 6 + j:7 + j], cols[:, 3 * j + 1:3 * j + 2])
                v = magnitude(small[:, 8 + j:9 + j], cols[:, 3 * j + 2:3 * j + 3])
            vq.step(v)
            vq.step(stt(small[:, 10:12], small[:, 6:8], 1.01 * N ** 0.5, small[:, 8:10], ALU.mult, ALU.add))
            nc.vector.tensor_scalar(wtmp[:, 0:F], wtmp[:, 0:F], 1.01 * F ** 0.5, None, ALU.mult)
            for j in range(2):
                w = wtmp[:, (1 + j) * F:(2 + j) * F]
                v = nc.vector.tensor_scalar(w, w, small[:, 10 + j:11 + j], None, ALU.mult)
            v.then_inc(s_bnd, 1)
            low(c + 1, 1)
            e, t, w = g_e[0:GH], g_t[0:GH], g_w[0:GH]
            dve.wait_ge(s_gf, 16 * 2 * GROWS)
            nc.vector.tensor_scalar(t, e, P - 1, None, ALU.bitwise_and)
            for h in range(2):
                half_ = slice(h * GE, (h + 1) * GE)
                v = nc.vector.tensor_scalar(w[:, half_], e[:, half_], cst[0:GH, 1 + h:2 + h], None, ALU.subtract)
            vq.step(v)
            low(c + 2, 2)
            vq.step(nc.vector.tensor_scalar(w, w, 7, None, ALU.arith_shift_right))
            nc.vector.tensor_copy(g_a[0:GH], w)
            nc.vector.tensor_copy(g_b[0:GH], t).then_inc(s_gk, 1)
            for c in range(NB - 1 - TR, NB):
                low(c, c % TR)
            dve.wait_ge(s_vsum, 1)
            nc.vector.tensor_scalar(flag[:], acc[:, 6, 4:5], 1.0, None, ALU.min).then_inc(s_flag, 1)
            dve.wait_ge(s_bnp, 2)
            power_scale(vq, pst[:, 0:3, :], 1, 3)
            bad = unsorted(dve)
            with dve.If(bad == 0):
                quick_dve(dve, vq)
            with dve.Else():
                general_dve(dve)

        @block.tensor
        def _(pe):
            pe.wait_ge(s_const, 3)
            def turn(c, count, b):
                pe.wait_ge(s_xin[b], 16 * count + 16)
                if not isinstance(c, int) or c:
                    pe.wait_ge(s_xTs, c)
                nc.tensor.transpose(pst[:, b, :], xs[:, b, :], ident[:]).then_inc(s_xt, 1)

            def products(c, b):
                pe.wait_ge(s_xTs, c + 1)
                if not isinstance(c, int) or c >= 3:
                    pe.wait_ge(s_tlo, c - 2)
                for h in range(2):
                    v = nc.tensor.matmul(acc[:, 2 * b + h, 0:512], hb[:, b, :], Ww[:, h * 512:(h + 1) * 512],
                                         start=True, stop=True)
                v.then_inc(s_mm1, 1)

            def turn_next(i, b):
                turn(i * TR + b + 1, i + (b + 1) // TR, (b + 1) % TR)

            turn(0, 0, 0)
            turn_next(0, 0)
            pe.wait_ge(s_w, 16)
            products(0, 0)
            pe.wait_ge(s_const, 4)
            pe.wait_ge(s_bnd, 1)
            nc.tensor.matmul(acc[:, 5, 0:1 + F], ones[:], bounds[:], start=True, stop=True).then_inc(s_bnp, 1)
            turn_next(0, 1)
            products(1, 1)
            pe.wait_ge(s_scl, 1)
            turn_next(0, 2)
            products(2, 2)
            for b in range(TR):
                turn_next(1, b)
                products(TR + b, b)
            for b in range(2):
                turn_next(2, b)
                products(2 * TR + b, b)
            pe.wait_ge(s_tlo, 2 * TR)
            pe.wait_ge(s_cnt, 1)
            for j in range(4):
                h, nxt = j % 2, j // 2
                for m in range(NTHR + 1):
                    a = m * (NG + 1) + h * GH + nxt
                    v = nc.tensor.matmul(acc[0:GH, 5, j:j + 1], mask16[:, a:a + GH], cnt16[:, m:m + 1], start=(m == 0),
                                         stop=(m == NTHR))
            v.then_inc(s_off, 1)
            turn_next(2, 2)
            pe.wait_ge(s_gidx, 1)
            products(3 * TR - 1, 2)
            with pe.Fori(3, TROUNDS) as i:
                for b in range(TR):
                    turn_next(i, b)
                    products(i * TR + b, b)
            products(NB - 1, 0)
            pe.wait_ge(s_ef, 1)
            pe.wait_ge(s_tlo, NB - 2)
            for j in range(2):
                for b in range(EB):
                    v = nc.tensor.transpose(acc[:, 2 + j, b * ER:(b + 1) * ER], e_f[0:ER, 2 + j, b * P:(b + 1) * P],
                                            ident[0:ER, 0:ER])
            v.then_inc(s_et, 1)
            pe.wait_ge(s_viol, 1)
            nc.tensor.matmul(acc[:, 6, 4:5], ones[:], small[:, 2:3], start=True, stop=True).then_inc(s_vsum, 1)
            pe.wait_ge(s_bnd, 2)
            nc.tensor.matmul(pst[:, 0:3, :].rearrange("p q f -> p (q f)"), ones[:], wtmp[:], start=True,
                             stop=True).then_inc(s_bnp, 1)
            pe.wait_ge(s_gk, 1)
            pe.wait_ge(s_tlo, NB)
            for src_, bank in ((g_a, 4), (g_b, 0)):
                for h in range(2):
                    for e in range(GT):
                        v = nc.tensor.transpose(acc[:, bank + h, e * GH:(e + 1) * GH],
                                                src_[0:GH, h * GE + e * P:h * GE + (e + 1) * P], ident[0:GH, 0:GH])
            v.then_inc(s_gt, 1)
            pe.wait_ge(s_gc, 1)
            bad = unsorted(pe)
            with pe.If(bad == 0):
                quick_pe(pe)
            with pe.Else():
                general_pe(pe)


_INS = ["x", "src", "dst", "edge_type_8", "L0_gnn_W_w", "L0_gnn_W_res", "L0_gnn_b_res",
        "L1_gnn_W1", "L1_gnn_b1", "L1_gnn_g1", "L1_gnn_be1", "L1_gnn_W2", "L1_gnn_b2", "L1_gnn_g2", "L1_gnn_be2",
        "L1_gnn_W3", "L1_gnn_b3"]


def kernel(**inputs):
    import numpy as _np
    import concourse.bacc as _bacc
    from concourse import mybir as _mybir
    from concourse.bass_utils import run_bass_kernel_spmd as _run

    nc = _bacc.Bacc("TRN2", target_bir_lowering=False, num_devices=1)
    arrays, args = {}, []
    for name in _INS:
        a = _np.ascontiguousarray(inputs[name])
        arrays[f"in_{name}_dram"] = a
        args.append(nc.dram_tensor(f"in_{name}_dram", a.shape, _mybir.dt.from_np(a.dtype), kind="ExternalInput").ap())
    c = constants()
    arrays["const_dram"] = c
    args.append(nc.dram_tensor("const_dram", c.shape, _mybir.dt.float32, kind="ExternalInput").ap())
    m = window_masks()
    arrays["masks_dram"] = m
    args.append(nc.dram_tensor("masks_dram", m.shape, _mybir.dt.float16, kind="ExternalInput").ap())
    args.append(nc.dram_tensor("out_0_dram", (N, F), _mybir.dt.float32, kind="ExternalOutput").ap())
    build(nc, *args)
    r = _run(nc, [arrays], core_ids=[0])
    return r.results[0]["out_0_dram"]
```
